# Optimizing a Trainium2 kernel written in Bass

```python
import numpy as np
import jax
import jax.numpy as jnp

def _softmax(x, axis=-1):
    return jax.nn.softmax(x, axis=axis)

def _gelu(x):
    return jax.nn.gelu(x, approximate=True)

def _silu(x):
    return jax.nn.silu(x)

def _sigmoid(x):
    return jax.nn.sigmoid(x)

def _layernorm(x, axis=-1, eps=1e-05):
    m = jnp.mean(x, axis=axis, keepdims=True)
    v = jnp.var(x, axis=axis, keepdims=True)
    return (x - m) / jnp.sqrt(v + eps)

def _scatter_add(tgt, idx, src, axis=0):
    return tgt.at[idx].add(src)

def _segment_sum(src, seg, n):
    return jax.ops.segment_sum(src, seg, n)
kernel_name = 'mk_flamingo_gated_d1_seqx_r8_d4f94b'

def setup_inputs(seed: int=0):
    np.random.seed(seed)
    _w = jnp.asarray

    def _rec_inputs():
        import jax
        import jax.numpy as jnp
        _rk = jax.random.key(seed)
        x = -0.0002928 + 1 * jax.random.normal(jax.random.fold_in(_rk, 1), (8, 256, 128), jnp.float32)
        _lenS = 256 - jax.random.randint(jax.random.fold_in(_rk, 7), (8,), 0, max(1, 256 // 4) + 1, jnp.int32)
        _lenS2 = 1601 - jax.random.randint(jax.random.fold_in(_rk, 8), (8,), 0, max(1, 1601 // 4) + 1, jnp.int32)
        _ctx_1024P = jax.random.normal(jax.random.fold_in(_rk, 11), (8, 16, 128), jnp.float32)
        _ctx_1024c = jax.random.dirichlet(jax.random.fold_in(_rk, 511), 0.3 * jnp.ones((16,), jnp.float32), (8, 1601))
        _ctx_1024t = jnp.einsum('bsk,bkd->bsd', _ctx_1024c, _ctx_1024P)
        _ctx_1024t = _ctx_1024t * jax.lax.rsqrt(jnp.mean(jnp.square(_ctx_1024t)) + 1e-12) * 0.953939
        ctx_1024 = -1.39393e-06 + 0.999914 * (_ctx_1024t + 0.3 * jax.random.normal(jax.random.fold_in(_rk, 611), (8, 1601, 128), jnp.float32))
        _validS = jnp.arange(256)[None, :] < _lenS[:, None]
        _validS2 = jnp.arange(1601)[None, :] < _lenS2[:, None]
        _causal = jnp.tril(jnp.ones((256, 256), dtype=bool))
        mask_1x1xSxS2_ik0 = jnp.where(jnp.broadcast_to(_validS2[0:1, None, None, :], (1, 1, 256, 1601)), 0, 1).astype(jnp.int32)
        _g = jax.random.normal(jax.random.fold_in(_rk, 9001), (2, 1), jnp.float32)
        _g = jnp.sign(_g) * jnp.maximum(jnp.abs(_g), 1.0) + (_g == 0) * 1.0
        g_xattn = _g[0]
        g_ffn = _g[1]
        return (x, ctx_1024, mask_1x1xSxS2_ik0, g_xattn, g_ffn)
    x, ctx_1024, mask_1x1xSxS2_ik0, g_xattn, g_ffn = _rec_inputs()

    def _L0_xattn_setup():
        import jax, jax.numpy as jnp
        import numpy as np
        NUM_HEAD = 16
        DIM_MODEL = 128
        D_K = DIM_MODEL // NUM_HEAD
        NEG = -1000000000.0
        key = jax.random.key(seed)
        ks = jax.random.split(key, 8)
        B, S, D = (2, 256, DIM_MODEL)
        q = jax.random.normal(ks[0], (B, S, D), dtype=jnp.float32)
        k = jax.random.normal(ks[1], (B, S, D), dtype=jnp.float32)
        v = jax.random.normal(ks[2], (B, S, D), dtype=jnp.float32)
        mask = jnp.tril(jnp.ones((S, S), dtype=jnp.int32))[None, None]
        scale = 1.0 / np.sqrt(D)
        w_q = jax.random.normal(ks[3], (D, D), dtype=jnp.float32) * scale
        w_k = jax.random.normal(ks[4], (D, D), dtype=jnp.float32) * scale
        w_v = jax.random.normal(ks[5], (D, D), dtype=jnp.float32) * scale
        w_o = jax.random.normal(ks[6], (D, D), dtype=jnp.float32) * scale
        return {'q': q, 'k': k, 'v': v, 'mask': mask, 'w_q': w_q, 'w_k': w_k, 'w_v': w_v, 'w_o': w_o}
    _L0_xattn_all = _L0_xattn_setup()
    _L0_xattn_in = {k: v for k, v in _L0_xattn_all.items() if k in ('w_q', 'w_k', 'w_v', 'w_o')}
    del _L0_xattn_all

    def _L0_ffn_setup():
        import jax, jax.numpy as jnp
        import numpy as np
        D = 128
        H = 512
        E = 8
        TOPK = 2
        CAP_F = 1.25
        key = jax.random.key(seed)
        ks = jax.random.split(key, 6)
        sc = 0.02
        return {'x': jax.random.normal(ks[0], (4, 256, D), jnp.float32), 'Wg': jax.random.normal(ks[1], (D, E), jnp.float32) * sc, 'bg': jnp.zeros((E,), jnp.float32), 'W1': jax.random.normal(ks[2], (E, D, H), jnp.float32) * sc, 'W2': jax.random.normal(ks[3], (E, D, H), jnp.float32) * sc, 'W3': jax.random.normal(ks[4], (E, H, D), jnp.float32) * sc}
    _L0_ffn_all = _L0_ffn_setup()
    _L0_ffn_in = {k: v for k, v in _L0_ffn_all.items() if k in ('Wg', 'bg', 'W1', 'W2', 'W3')}
    del _L0_ffn_all
    return {'x': x, 'ctx_1024': ctx_1024, 'mask_1x1xSxS2_ik0': mask_1x1xSxS2_ik0, 'g_xattn': g_xattn, 'g_ffn': g_ffn, 'L0_xattn_w_q': _L0_xattn_in['w_q'], 'L0_xattn_w_k': _L0_xattn_in['w_k'], 'L0_xattn_w_v': _L0_xattn_in['w_v'], 'L0_xattn_w_o': _L0_xattn_in['w_o'], 'L0_ffn_Wg': _L0_ffn_in['Wg'], 'L0_ffn_bg': _L0_ffn_in['bg'], 'L0_ffn_W1': _L0_ffn_in['W1'], 'L0_ffn_W2': _L0_ffn_in['W2'], 'L0_ffn_W3': _L0_ffn_in['W3']}

def reference(x, ctx_1024, mask_1x1xSxS2_ik0, g_xattn, g_ffn, L0_xattn_w_q, L0_xattn_w_k, L0_xattn_w_v, L0_xattn_w_o, L0_ffn_Wg, L0_ffn_bg, L0_ffn_W1, L0_ffn_W2, L0_ffn_W3):
    import jax
    import jax.numpy as jnp

    def _L0_xattn_ref(q, k, v, mask, w_q, w_k, w_v, w_o):
        import jax, jax.numpy as jnp
        import numpy as np
        NUM_HEAD = 16
        DIM_MODEL = 128
        D_K = DIM_MODEL // NUM_HEAD
        NEG = -1000000000.0
        B, S, D = q.shape
        H, dk = (NUM_HEAD, D_K)

        def proj(x, w):
            return (x @ w.T).reshape(B, -1, H, dk).transpose(0, 2, 1, 3)
        Q, K, V = (proj(q, w_q), proj(k, w_k), proj(v, w_v))
        scores = jnp.einsum('bhqd,bhkd->bhqk', Q, K) / jnp.sqrt(jnp.float32(dk))
        scores = jnp.where(mask == 0, NEG, scores)
        attn = jax.nn.softmax(scores, axis=-1)
        out = jnp.einsum('bhqk,bhkd->bhqd', attn, V)
        out = out.transpose(0, 2, 1, 3).reshape(B, S, D)
        return out @ w_o.T

    def _L0_ffn_ref(x, Wg, bg, W1, W2, W3):
        import jax, jax.numpy as jnp
        import numpy as np
        D = 128
        H = 512
        E = 8
        TOPK = 2
        CAP_F = 1.25
        b, s, d = x.shape
        xt = x.reshape(-1, d)
        T = xt.shape[0]
        capacity = int(T / E * CAP_F)
        gate_logits = xt @ Wg + bg
        top_v, top_i = jax.lax.top_k(gate_logits, TOPK)
        expert_label = jax.nn.one_hot(top_i, E, dtype=xt.dtype).sum(axis=1)
        seq = jnp.cumsum(expert_label, axis=0) * expert_label
        valid = (seq > 0) & (seq <= capacity)
        slot = (seq - 1.0).astype(jnp.int32)
        flat_idx = jnp.where(valid, jnp.arange(E, dtype=jnp.int32)[None, :] * capacity + slot, E * capacity)
        src = jnp.broadcast_to(xt[:, None, :], (T, E, d)).reshape(-1, d)
        buf = jnp.zeros((E * capacity + 1, d), xt.dtype).at[flat_idx.reshape(-1)].set(src)
        disp = buf[:-1].reshape(E, capacity, d)
        h = jax.nn.silu(jnp.einsum('ecd,edh->ech', disp, W1)) * jnp.einsum('ecd,edh->ech', disp, W2)
        out = jnp.einsum('ech,ehd->ecd', h, W3)
        out_flat = jnp.concatenate([out.reshape(E * capacity, d), jnp.zeros((1, d), xt.dtype)], axis=0)
        all_expert_output = out_flat[flat_idx]
        sel = jnp.take_along_axis(all_expert_output, top_i[:, :, None], axis=1)
        routing_w = jax.nn.softmax(top_v, axis=-1)
        y = (routing_w[:, :, None] * sel).sum(axis=1)
        return y.reshape(b, s, d)
    x = x + jnp.tanh(g_xattn[0]) * _L0_xattn_ref(_layernorm(x, axis=-1), ctx_1024, ctx_1024, mask_1x1xSxS2_ik0, L0_xattn_w_q, L0_xattn_w_k, L0_xattn_w_v, L0_xattn_w_o)
    x = x + jnp.tanh(g_ffn[0]) * _L0_ffn_ref(_layernorm(x, axis=-1), L0_ffn_Wg, L0_ffn_bg, L0_ffn_W1, L0_ffn_W2, L0_ffn_W3)
    return x

_drawn_inputs = setup_inputs


def setup_inputs(seed=0):
    import zlib

    import numpy as np

    out = dict(_drawn_inputs(seed))
    spreads = {'L0_ffn_bg': (0.0, 0.8)}
    factors = {'L0_ffn_Wg': 8.0, 'L0_ffn_W1': 8.0, 'L0_ffn_W2': 8.0, 'L0_ffn_W3': 8.0}
    for name, (base, spread) in spreads.items():
        noise = np.random.default_rng([zlib.crc32(name.encode()), seed]).standard_normal(out[name].shape)
        drawn = base * np.exp(spread * noise) if base else spread * noise
        out[name] = jnp.asarray(drawn.astype(out[name].dtype))
    for name, factor in factors.items():
        out[name] = (out[name] * factor).astype(out[name].dtype)
    return out
```

```python
from contextlib import ExitStack

import concourse.bass as bass
from concourse import mybir

F32 = mybir.dt.float32
BF16 = mybir.dt.bfloat16
I32 = mybir.dt.int32
U32 = mybir.dt.uint32
ALU = mybir.AluOpType
ACT = mybir.ActivationFunctionType
AX = mybir.AxisListType

P = 128
B, S, D = 8, 256, 128
H, DK = 16, 8
SK = 1601
QT = S // P
NWIN = 4
TILE = 100
WIN = 4 * TILE
WKEYS = WIN + 1
NT = NWIN * 4
E, HID, CAP = 8, 512, 320
HK = HID // P
T = B * S
NTT = T // P
ROW = D + 4
PAIRS = H // 2
PROWS = 6 * DK
HROWS = PROWS + 1
MAX_ROW = 2 * HROWS
SROWS = MAX_ROW + 6
NSET = 3
KPAD = WKEYS + 1
VCOL = 32
SCALE = float(DK) ** -0.5
EPS = 1e-5
FAR = 1.0e30
SKIP = 1.0e6
CT = [(0, 128), (128, 128), (256, 64)]


class Chain:

    def __init__(self, eng, sem, per, wait=None):
        self.eng, self.sem, self.per, self.wait = eng, sem, per, wait or (lambda eng, s, value: eng.wait_ge(s, value))

    def at(self, b):
        self.base, self.k = b * self.per, 0
        return self

    def next(self, instruction):
        self.k += 1
        instruction.then_inc(self.sem, 1)
        self.wait(self.eng, self.sem, self.base + self.k)

    def end(self):
        assert self.k == self.per, (self.k, self.per)


def flamingo_kernel(nc, x, ctx, mask, g_xattn, g_ffn, w_q, w_k, w_v, w_o, w_g, b_g, w1, w2, w3, out):
    slots = nc.dram_tensor("slots", [E * CAP, ROW], F32, kind="Internal").ap()
    kspread = nc.dram_tensor("kspread", [NSET, 3, P, WKEYS], BF16, kind="Internal").ap()
    qspread = nc.dram_tensor("qspread", [NSET, 3, P, S], BF16, kind="Internal").ap()
    out_rows = out.rearrange("b s d -> (b s) d")
    x_tiles = x.rearrange("b (q p) d -> p b q d", p=P)
    out_tiles = out.rearrange("b (q p) d -> p b q d", p=P)

    with ExitStack() as stack:
        def sb(name, shape, dt):
            return stack.enter_context(nc.sbuf_tensor(name, shape, dt))

        def sem(name):
            return stack.enter_context(nc.semaphore(name))

        ident = sb("ident", [P, P], F32)
        identb = sb("identb", [P, P], BF16)
        onesb = sb("onesb", [P, P], BF16)
        tri = sb("tri", [P, P], BF16)
        zrow = sb("zrow", [P, ROW], F32)
        iota8i = sb("iota8i", [P, E], I32)
        iota8 = sb("iota8", [P, E], F32)
        tok_i = sb("tok_i", [P, NTT], I32)
        tok = sb("tok", [P, NTT], F32)
        ones_row = sb("ones_row", [6, KPAD], BF16)
        zero_row = sb("zero_row", [1, KPAD], BF16)
        halfpow = sb("halfpow", [P, 2], F32)
        wraw = sb("wraw", [P, 4, D], F32)
        wT = sb("wT", [P, 4, D], F32)
        wg = sb("wg", [P, E], F32)
        bg = sb("bg", [P, QT, E], F32)
        gates = sb("gates", [P, 2], F32)
        tanhs = sb("tanhs", [P, 2], F32)
        attend = sb("attend", [P, QT, SK], BF16)
        colsum = sb("colsum", [1, 3, WKEYS], F32)
        stat = sb("stat", [1, 8], F32)
        keybias = sb("keybias", [1, WKEYS], BF16)
        flag = sb("flag", [1, 1], I32)
        X = sb("X", [P, NTT, D], F32)
        C = sb("C", [P, 2, 4, D], F32)
        ctxT = sb("ctxT", [P, WKEYS], F32)
        kparts = sb("kparts", [P, 3, WKEYS], BF16)
        krest = sb("krest", [P, WKEYS], F32)
        qparts = sb("qparts", [P, 3, S], BF16)
        qrest = sb("qrest", [P, S], F32)
        bn = sb("bn", [P, QT, 6], F32)
        mv = sb("mv", [P, QT, 2], F32)
        rstd = sb("rstd", [P, QT], F32)
        vareps = sb("vareps", [P, QT], F32)
        xn = sb("xn", [P, QT, D], F32)
        xnT = sb("xnT", [P, S], F32)
        valid = sb("valid", [P, 3, QT], F32)
        KSa = sb("KSa", [P, PAIRS * (SK + 3)], BF16)
        QS = sb("QS", [P, NSET, PAIRS, 2, S], BF16)
        VSf = sb("VSf", [P, NSET, 4, H * VCOL], F32)
        probs = sb("probs", [P, 8, 4 * S], F32)
        wmax = sb("wmax", [P, NWIN, QT, H], F32)
        rowmax = sb("rowmax", [P, QT, H], F32)
        mrest = sb("mrest", [P, 2, QT, H], F32)
        mparts = sb("mparts", [P, QT, 3, H], BF16)
        mT = sb("mT", [3 * H, S], BF16)
        OT = sb("OT", [P, S], F32)
        rsum = sb("rsum", [P, QT, 4], F32)
        O = sb("O", [P, QT, H, DK], F32)
        OCT = sb("OCT", [P, S], F32)
        bn2 = sb("bn2", [P, QT, 6], F32)
        mv2 = sb("mv2", [P, QT, 2], F32)
        rstd2 = sb("rstd2", [P, QT], F32)
        vareps2 = sb("vareps2", [P, QT], F32)
        rows = sb("rows", [P, 2, QT, ROW], F32)
        xn2T = sb("xn2T", [P, S], F32)
        logits = sb("logits", [P, QT, E], F32)
        top = sb("top", [P, QT, 8], F32)
        topi = sb("topi", [P, QT, 8], U32)
        topf = sb("topf", [P, QT, 2], F32)
        gap = sb("gap", [P, QT], F32)
        e2 = sb("e2", [P, QT], F32)
        den = sb("den", [P, QT], F32)
        rden = sb("rden", [P, QT], F32)
        hot = sb("hot", [P, QT, 2, E], F32)
        label = sb("label", [P, QT, E], BF16)
        before = sb("before", [P, 3, E], BF16)
        picked = sb("picked", [P, QT, 2, E], F32)
        place = sb("place", [P, QT, 2], F32)
        over = sb("over", [P, QT, 2], F32)
        first = sb("first", [P, QT, 2], F32)
        slot_i = sb("slot_i", [P, 2, QT, 2], I32)
        W1S = sb("W1S", [P, E, HID], F32)
        W2S = sb("W2S", [P, E, HID], F32)
        W3S = sb("W3S", [P, E, HK, D], F32)
        dispT = sb("dispT", [P, 2, CAP], F32)
        spare = sb("spare", [P, E, 3, 2], F32)
        slot_w = sb("slot_w", [P, E, 3], F32)
        slot_t = sb("slot_t", [P, E, 3], F32)
        slot_to = sb("slot_to", [P, E, 3], I32)

        KSp = [KSa[:, p * PAIRS * KPAD:(p + 1) * PAIRS * KPAD].rearrange("p (s k) -> p s k", s=PAIRS)
               for p in range(NSET)]
        KSg = KSa[:, :].rearrange("p (s k) -> p s k", s=PAIRS)
        VSg = [w[:, :, :].rearrange("p e n -> p (e n)").rearrange("p (t n) -> p t n", n=H * VCOL) for w in (W1S, W2S)]
        w3flat = W3S[:, :, :, :].rearrange("p e k n -> p (e k n)").bitcast(BF16)
        biasT = w3flat[:, 0:NT * S].rearrange("p (t q) -> p t q", t=NT)
        pflat = probs[:, :, :].rearrange("p s n -> p (s n)")
        maski = pflat[:, 0:QT * SK].bitcast(I32).rearrange("p (q k) -> p q k", q=QT)
        masked = W3S[:, :, :, :].rearrange("p e k n -> p (e k n)")[:, NT * S // 2:NT * S // 2 + WKEYS]
        disp = pflat[:, 0:E * 3 * ROW].rearrange("p (e c n) -> p e c n", e=E, c=3)
        o0 = E * 3 * ROW
        hT = pflat[:, o0:o0 + HK * CAP].rearrange("p (k n) -> p k n", k=HK)
        o1 = o0 + HK * CAP
        silu = pflat[:, o1:o1 + 2 * CAP].rearrange("p (b n) -> p b n", b=2)
        o2 = o1 + 2 * CAP
        orow = pflat[:, o2:o2 + 2 * 3 * D].rearrange("p (b c n) -> p b c n", b=2, c=3)
        o3 = o2 + 6 * D
        hT = [hT, pflat[:, o3:o3 + HK * CAP].rearrange("p (k n) -> p k n", k=HK)]
        assert o3 + HK * CAP <= 8 * 4 * S

        ps_s = [stack.enter_context(nc.psum_tensor(f"ps_s{i}", [P, 512], F32)) for i in range(2)]
        ps_t = [stack.enter_context(nc.psum_tensor(f"ps_t{i}", [P, 1024], F32)) for i in range(2)]
        ps_o = stack.enter_context(nc.psum_tensor("ps_o", [P, 512], F32))
        ps_m = stack.enter_context(nc.psum_tensor("ps_m", [P, 512], F32))

        s_w = sem("weights_loaded")
        s_mask = sem("mask_loaded")
        s_x = [sem(f"x_loaded{i}") for i in range(3)]
        s_ctx = [sem("ctx_loaded0"), sem("ctx_loaded1")]
        s_expw = sem("expert_weights_loaded")
        s_zero = sem("slots_zeroed")
        s_pre = sem("pool_setup")
        s_vpre = sem("vector_setup")
        s_attend = sem("attend_made")
        s_wT_ps = sem("weights_turned")
        s_wT = sem("weights_copied")
        s_col = sem("column_sums")
        s_stat = sem("mask_statistics")
        s_flag = sem("path_decided")
        s_kbias = sem("key_bias_made")
        s_kb = sem("key_bias_rows")
        s_tanh = sem("tanhs_made")
        s_fill = sem("stacks_filled")
        s_rowpat = sem("row_patterns_made")
        s_const = sem("stack_constants_written")
        s_vones = sem("v_buffers_cleared")
        s_gates = sem("small_tensors_loaded")
        s_rv = sem("rstd_of_valid_rows")
        s_ctxT_ps = sem("ctxT_in_psum")
        s_ctxT = sem("ctxT_copied")
        s_k_ps = sem("k_in_psum")
        s_k_hi = sem("k_high")
        s_k_r = sem("k_rest")
        s_k_mid = sem("k_middle")
        s_k_lo = sem("k_low")
        s_v_ps = sem("v_in_psum")
        s_v = sem("v_copied")
        s_ln = sem("ln_chain")
        s_rs = sem("rstd_chain")
        s_xn = sem("xn_made")
        s_xnT_ps = sem("xnT_in_psum")
        s_xnT = sem("xnT_copied")
        s_q_ps = sem("q_in_psum")
        s_q_hi = sem("q_high")
        s_q_r = sem("q_rest")
        s_q_mid = sem("q_middle")
        s_q_lo = sem("q_low")
        s_kd = sem("k_parts_in_dram")
        s_qd = sem("q_parts_in_dram")
        s_ks = [sem(f"k_stack_written{i}") for i in range(NWIN)]
        s_qs = [sem(f"q_stack_written{i}") for i in range(NSET)]
        s_sc = sem("scores_for_max")
        s_mx = sem("maxima_taken")
        s_mgen = sem("general_max_chain")
        s_mp = sem("max_parts_chain")
        s_mT_ps = sem("mT_in_psum")
        s_mT = sem("mT_copied")
        s_mr = sem("max_rows_written")
        s_st = sem("scores_for_exp")
        s_ex = sem("exp_done")
        s_pv = sem("pv_done")
        s_ot = sem("out_copied")
        s_oq = sem("out_turned")
        s_rsum = sem("sums_inverted")
        s_on = sem("out_normed")
        s_oc_ps = sem("outT_in_psum")
        s_oc = sem("outT_copied")
        s_y = sem("projected")
        s_x2 = sem("x2_made")
        s_x2out = sem("x2_stored")
        s_ln2 = sem("ln2_chain")
        s_rs2 = sem("rstd2_chain")
        s_xn2 = sem("xn2_made")
        s_xn2T_ps = sem("xn2T_in_psum")
        s_xn2T = sem("xn2T_copied")
        s_lg_ps = sem("logits_in_psum")
        s_lg = sem("logits_made")
        s_top = sem("top_values")
        s_topi = sem("top_indices")
        s_gap = sem("gap_made")
        s_e2 = sem("gap_exp")
        s_rden = sem("den_inverted")
        s_rt = sem("route_chain")
        s_seq = sem("seq_in_psum")
        s_pick = sem("place_picked")
        s_pickq = sem("first_tile_picked")
        s_place = sem("place_summed")
        s_scat = [sem("rows_scattered0"), sem("rows_scattered1")]
        s_disp = [sem(f"slots_loaded{e}") for e in range(E)]
        s_dT_ps = sem("dispT_in_psum")
        s_dT = sem("dispT_copied")
        s_h_ps = sem("h_in_psum")
        s_silu = sem("silu_done")
        s_h = sem("h_made")
        s_o_ps = sem("expert_out_in_psum")
        s_orow = sem("expert_rows")
        s_sw = sem("slot_chain")
        s_add = [sem("rows_added0"), sem("rows_added1")]
        s_gb = sem("general_bias_chain")
        s_gbq = sem("general_bias_first_tile")
        s_bT_ps = sem("biasT_in_psum")
        s_bT = sem("biasT_copied")
        s_vg = sem("general_v_cleared")
        s_settle = sem("nothing")

        class Path:

            def __init__(self, general):
                self.general = general
                self.windows = list(range(NWIN)) if general else [NWIN - 1]
                self.nw = len(self.windows)

            def set_of(self, b):
                return 0 if self.general else b % NSET

            def ks(self, b, i):
                return KSg[:, :, WIN * i:WIN * i + WKEYS] if self.general else KSp[b % NSET][:, :, 0:WKEYS]

            def vs(self, b, i, t):
                if not self.general:
                    return VSf[:, b % NSET, t, :]
                n = 4 * i + t
                return VSg[n // 8][:, n % 8, :]

            def depth(self, i, t):
                return TILE + (self.windows[i] == NWIN - 1 and t == 3)

        padded, general = Path(False), Path(True)
        block = stack.enter_context(nc.Block())

        def settle(eng):
            eng.sem_inc(s_settle, 1)

        def wait(eng, s, value):
            if not isinstance(value, int):
                eng.wait_ge(s, value)
                settle(eng)
            elif value > 0:
                eng.wait_ge(s, value)

        def x_pair(b):
            return X[:, 2 * b:2 * b + 2, :] if isinstance(b, int) else X[:, bass.ds(2 * b, 2), :]

        def end_of_batch(eng, b):
            wait(eng, s_scat[0], 64 * (b + 1))
            wait(eng, s_x2out, 16 * (b + 1))

        @block.sync
        def _(eng):
            eng.dma_start(maski, mask[0, 0].rearrange("(q p) k -> p q k", p=P)).then_inc(s_mask, 16)
            eng.dma_start(wraw[:, 1, :], w_k).then_inc(s_w, 16)
            eng.dma_start(wraw[:, 0, :], w_q).then_inc(s_w, 16)
            eng.dma_start(wraw[:, 2, :], w_v).then_inc(s_w, 16)
            eng.dma_start(wraw[:, 3, :], w_o).then_inc(s_w, 16)

            def load_ctx(path, b, i):
                n = b * path.nw + i
                cb = i % 2 if path.general else b % 2
                if path.general:
                    if i >= 2:
                        eng.wait_ge(s_ctxT_ps, n - 1)
                else:
                    wait(eng, s_ctxT_ps, n - 1)
                base = WIN * path.windows[i]
                eng.dma_start(C[0:TILE, cb, :, :], ctx[b, base:base + WIN, :].rearrange("(t k) d -> k t d", k=TILE))\
                   .then_inc(s_ctx[cb], 16)
                eng.dma_start(C[TILE:TILE + 1, cb, 3, :], ctx[b, base + WIN:base + WKEYS, :]).then_inc(s_ctx[cb], 16)

            def load_x():
                eng.dma_start(X[:, 2:4, :], x_tiles[:, 1]).then_inc(s_x[1], 16)
                eng.dma_start(X[:, 4:, :].rearrange("p (b q) d -> p b q d", q=QT), x_tiles[:, 2:]).then_inc(s_x[2], 16)

            def stack_k(path, b, i):
                n = b * path.nw + i
                st = path.set_of(b)
                eng.wait_ge(s_k_lo, n + 1)
                if path.general:
                    if i >= 1:
                        eng.wait_ge(s_ks[i - 1], 192 * (b + 1))
                else:
                    wait(eng, s_ks[st], 192 * (b // NSET))
                eng.dma_start(kspread[st].rearrange("c p k -> p c k"), kparts[:, :, :]).then_inc(s_kd, 16)
                eng.wait_ge(s_kd, 16 * (n + 1))
                if not path.general:
                    wait(eng, s_st, H * (b - NSET + 1))
                dst = path.ks(b, i)
                src = kspread[st].rearrange("c (s h d) k -> h c d s k", h=2, d=DK)
                for hp in range(2):
                    for row, parts in ((0, 3), (3, 2), (5, 1)):
                        for c in range(parts):
                            r0 = HROWS * hp + DK * (row + c)
                            eng.dma_start(dst[r0:r0 + DK, :, :], src[hp, c]).then_inc(s_ks[i if path.general else st], 16)

            def stack_q(path, b):
                st = path.set_of(b)
                eng.wait_ge(s_q_lo, b + 1)
                if not path.general:
                    wait(eng, s_qs[st], 192 * (b // NSET))
                eng.dma_start(qspread[st].rearrange("c p k -> p c k"), qparts[:, :, :]).then_inc(s_qd, 16)
                eng.wait_ge(s_qd, 16 * (b + 1))
                if not path.general:
                    wait(eng, s_st, H * (b - NSET + 1))
                src = qspread[st].rearrange("c (s h d) k -> h c d s k", h=2, d=DK)
                for hp in range(2):
                    for row, part in enumerate((0, 0, 0, 1, 1, 2)):
                        r0 = HROWS * hp + DK * row
                        eng.dma_start(QS[r0:r0 + DK, st, :, hp, :], src[hp, part]).then_inc(s_qs[st], 16)

            def max_rows(path, b):
                st = path.set_of(b)
                eng.wait_ge(s_mT, b + 1)
                for hp in range(2):
                    for c in range(3):
                        r0 = MAX_ROW + 3 * hp + c
                        eng.dma_start(QS[r0:r0 + 1, st, :, hp, :], mT[H * c + hp:H * (c + 1):2, :]).then_inc(s_mr, 16)

            def store_x2(b):
                eng.wait_ge(s_x2, b + 1)
                eng.dma_start(out_tiles[:, b], x_pair(b)).then_inc(s_x2out, 16)

            def expert_weights(e):
                eng.dma_start(W1S[:, e, :], w1[e]).then_inc(s_expw, 16)
                eng.dma_start(W2S[:, e, :], w2[e]).then_inc(s_expw, 16)
                eng.dma_start(W3S[:, e, :, :], w3[e].rearrange("(k p) d -> p k d", p=P)).then_inc(s_expw, 16)

            def q_ones(r0, hp):
                for st in range(NSET):
                    eng.dma_start(QS[r0:r0 + 1, st, :, hp, :],
                                  ones_row[0:1, 0:S].unsqueeze(1).broadcast_to([1, PAIRS, S])).then_inc(s_const, 16)

            eng.dma_start(X[:, 0:2, :], x_tiles[:, 0]).then_inc(s_x[0], 16)
            eng.wait_ge(s_flag, 1)
            fast = eng.value_load(flag[0:1, 0:1], min_val=0, max_val=1)
            with eng.If(fast == 1):
                load_ctx(padded, 0, 0)
                load_ctx(padded, 1, 0)
                load_x()
                eng.wait_ge(s_rowpat, 2)
                eng.wait_ge(s_fill, NSET)
                every = KSa[:, 0:NSET * PAIRS * KPAD].rearrange("p (s k) -> p s k", k=KPAD)
                eng.dma_start(every[MAX_ROW:SROWS], ones_row[:, :].unsqueeze(1).broadcast_to([6, NSET * PAIRS, KPAD]))\
                   .then_inc(s_const, 16)
                for hp in range(2):
                    r0 = HROWS * hp + PROWS
                    q_ones(r0, hp)
                    eng.wait_ge(s_kbias, 1)
                    eng.dma_start(every[r0:r0 + 1, :, 0:WKEYS],
                                  keybias[:, :].unsqueeze(1).broadcast_to([1, NSET * PAIRS, WKEYS])).then_inc(s_const, 16)
                for b in range(2):
                    stack_k(padded, b, 0)
                    stack_q(padded, b)
                max_rows(padded, 0)
                for b in range(B):
                    if b + 2 < B:
                        load_ctx(padded, b + 2, 0)
                    expert_weights(b)
                    if b + 2 < B:
                        stack_k(padded, b + 2, 0)
                        stack_q(padded, b + 2)
                    if b + 1 < B:
                        max_rows(padded, b + 1)
                    store_x2(b)
            with eng.Else():
                load_x()
                eng.wait_ge(s_rowpat, 2)
                eng.wait_ge(s_fill, NSET)
                quarters = KSa[:, :].rearrange("p (s k) -> p s k", k=(SK + 3) // 4)
                quarter = (SK + 3) // 4
                eng.dma_start(quarters[MAX_ROW:SROWS], ones_row[:, 0:quarter].unsqueeze(1)
                              .broadcast_to([6, 4 * PAIRS, quarter])).then_inc(s_const, 16)
                for hp in range(2):
                    r0 = HROWS * hp + PROWS
                    q_ones(r0, hp)
                    eng.dma_start(quarters[r0:r0 + 1], zero_row[:, 0:quarter].unsqueeze(1)
                                  .broadcast_to([1, 4 * PAIRS, quarter])).then_inc(s_const, 16)
                with eng.Fori(0, B) as b:
                    load_ctx(general, b, 0)
                    load_ctx(general, b, 1)
                    for i in range(NWIN):
                        stack_k(general, b, i)
                        if i + 2 < NWIN:
                            load_ctx(general, b, i + 2)
                    stack_q(general, b)
                    max_rows(general, b)
                    store_x2(b)
                    end_of_batch(eng, b)
                for e in range(E):
                    expert_weights(e)
            with eng.If(fast == 1):
                eng.wait_ge(s_scat[0], 32 * B)
                eng.wait_ge(s_scat[1], 32 * B)
            with eng.Else():
                eng.wait_ge(s_scat[0], 64 * B)
            for e in range(E):
                eng.dma_start(disp[:, e, 0:2, :], slots[CAP * e:CAP * e + 256, :].rearrange("(c p) n -> p c n", p=P))\
                   .then_inc(s_disp[e], 16)
                eng.dma_start(disp[0:64, e, 2, :], slots[CAP * e + 256:CAP * (e + 1), :]).then_inc(s_disp[e], 16)
            eng.wait_ge(s_add[0], 24 * E)
            eng.wait_ge(s_add[1], 24 * E)
            eng.wait_ge(s_zero, 16)
            eng.wait_ge(s_x2out, 16 * B)

        @block.gpsimd
        def _(eng):
            setup = Chain(eng, s_pre, 11).at(0)
            setup.next(eng.memset(ident[:, :], 0.0))
            setup.next(eng.affine_select(out=ident[:, :], in_=ident[:, :], compare_op=ALU.not_equal, fill=1.0,
                                         base=0, pattern=[[-1, P]], channel_multiplier=1))
            setup.next(eng.memset(onesb[:, :], 1.0))
            setup.next(eng.tensor_copy(identb[:, :], ident[:, :]))
            setup.next(eng.affine_select(out=tri[:, :], in_=onesb[:, :], compare_op=ALU.is_ge, fill=0.0,
                                         base=0, pattern=[[1, P]], channel_multiplier=-1))
            setup.next(eng.iota(iota8i[:, :], pattern=[[1, E]], base=0, channel_multiplier=0))
            setup.next(eng.tensor_copy(iota8[:, :], iota8i[:, :]))
            setup.next(eng.iota(tok_i[:, :], pattern=[[P, NTT]], base=1, channel_multiplier=1))
            setup.next(eng.tensor_copy(tok[:, :], tok_i[:, :]))
            setup.next(eng.memset(halfpow[:, :], -0.5))
            setup.next(eng.memset(before[:, :, :], 0.0))
            setup.end()
            for st in range(NSET):
                eng.memset(VSf[:, st, :, :], 0.0).then_inc(s_vones, 1)
            eng.wait_ge(s_vones, NSET)
            for st in range(NSET):
                eng.memset(VSf[:, st, :, :].rearrange("p t (h c) -> p (t h) c", c=VCOL)[:, :, DK:DK + 1], 1.0)\
                   .then_inc(s_vones, 1)

            rs_chain = Chain(eng, s_rs, 2, wait)
            mp_chain = Chain(eng, s_mp, 6, wait)
            rs2_chain = Chain(eng, s_rs2, 2, wait)
            rt_chain = Chain(eng, s_rt, 19, wait)

            def rstd_of(b):
                wait(eng, s_ln, 4 * (b + 1))
                if isinstance(b, int):
                    wait(eng, s_xn, 2 * b)
                c = rs_chain.at(b)
                c.next(eng.tensor_scalar(vareps[:, :], mv[:, :, 1], EPS, None, ALU.add))
                c.next(eng.tensor_tensor(rstd[:, :], vareps[:, :], halfpow[:, :], ALU.pow))

            def split_k(path, b, i):
                n = b * path.nw + i
                wait(eng, s_k_r, n + 1)
                if i >= 1 or not path.general:
                    wait(eng, s_kd, 16 * n)
                eng.tensor_copy(kparts[:, 1, :], krest[:, :]).then_inc(s_k_mid, 1)
                wait(eng, s_k_mid, n + 1)
                eng.tensor_tensor(kparts[:, 2, :], krest[:, :], kparts[:, 1, :], ALU.subtract).then_inc(s_k_lo, 1)

            def split_q(path, b):
                wait(eng, s_q_r, b + 1)
                if not path.general:
                    wait(eng, s_qd, 16 * b)
                eng.tensor_copy(qparts[:, 1, :], qrest[:, :]).then_inc(s_q_mid, 1)
                wait(eng, s_q_mid, b + 1)
                eng.tensor_tensor(qparts[:, 2, :], qrest[:, :], qparts[:, 1, :], ALU.subtract).then_inc(s_q_lo, 1)

            def max_parts(path, b):
                if path.general:
                    wait(eng, s_mgen, (2 * 2 * H * NWIN + 1) * (b + 1))
                else:
                    eng.wait_ge(s_mx, 2 * H * (b + 1))
                    wait(eng, s_mT_ps, b)
                c = mp_chain.at(b)
                src = rowmax[:, :, :] if path.general else wmax[:, b % 2, :, :]
                c.next(eng.tensor_scalar(mrest[:, 0], src, -1.0, None, ALU.mult))
                c.next(eng.tensor_copy(mparts[:, :, 0, :], mrest[:, 0]))
                c.next(eng.tensor_tensor(mrest[:, 1], mrest[:, 0], mparts[:, :, 0, :], ALU.subtract))
                c.next(eng.tensor_copy(mparts[:, :, 1, :], mrest[:, 1]))
                c.next(eng.tensor_tensor(mrest[:, 0], mrest[:, 1], mparts[:, :, 1, :], ALU.subtract))
                c.next(eng.tensor_copy(mparts[:, :, 2, :], mrest[:, 0]))
                c.end()

            def rstd2_of(b):
                wait(eng, s_ln2, 4 * (b + 1))
                c = rs2_chain.at(b)
                c.next(eng.tensor_scalar(vareps2[:, :], mv2[:, :, 1], EPS, None, ALU.add))
                c.next(eng.tensor_tensor(rstd2[:, :], vareps2[:, :], halfpow[:, :], ALU.pow))

            def route_labels(b, p):
                row = rows[:, p, :, :]
                wait(eng, s_topi, 2 * (b + 1))
                if isinstance(b, int):
                    wait(eng, s_e2, b)
                eng.tensor_tensor(gap[:, :], top[:, :, 1], top[:, :, 0], ALU.subtract).then_inc(s_gap, 1)
                c = rt_chain.at(b)
                c.next(eng.tensor_copy(topf[:, :, :], topi[:, :, 0:2]))
                for q in range(QT):
                    for k in range(2):
                        c.next(eng.tensor_scalar(hot[:, q, k, :], iota8[:, :], topf[:, q, k:k + 1], None, ALU.is_equal))
                c.next(eng.tensor_tensor(label[:, :, :], hot[:, :, 0, :], hot[:, :, 1, :], ALU.add))
                c.next(eng.tensor_tensor(before[:, 1, :], before[:, 0, :], label[:, 0, :], ALU.add))
                c.next(eng.tensor_tensor(before[:, 2, :], before[:, 1, :], label[:, 1, :], ALU.add))
                wait(eng, s_e2, b + 1)
                c.next(eng.tensor_scalar(den[:, :], e2[:, :], 1.0, None, ALU.add))
                wait(eng, s_rden, b + 1)
                if isinstance(b, int):
                    wait(eng, s_scat[p], 64 * (b // 2))
                c.next(eng.tensor_scalar(row[:, :, D + 1], rden[:, :], tanhs[:, 1:2], None, ALU.mult))
                c.next(eng.tensor_tensor(row[:, :, D + 2], row[:, :, D + 1], e2[:, :], ALU.mult))
                c.next(eng.tensor_copy(row[:, :, D + 3], topf[:, :, 0]))
                c.next(eng.tensor_copy(row[:, :, D], tok[:, 2 * b:2 * b + 2] if isinstance(b, int)
                                       else tok[:, bass.ds(2 * b, 2)]))
                return c

            def scatter(b, p, c):
                row = rows[:, p, :, :]
                wait(eng, s_place, b + 1)
                c.next(eng.tensor_copy(before[:, 0, :], before[:, 2, :]))
                c.next(eng.tensor_scalar(over[:, :, :], place[:, :, :], float(CAP), SKIP, ALU.is_gt, ALU.mult))
                c.next(eng.tensor_scalar(first[:, :, :], topf[:, :, :], float(CAP), -1.0, ALU.mult, ALU.add))
                c.next(eng.tensor_tensor(first[:, :, :], over[:, :, :], first[:, :, :], ALU.add))
                c.next(eng.tensor_tensor(first[:, :, :], first[:, :, :], place[:, :, :], ALU.add))
                c.next(eng.tensor_copy(slot_i[:, p, :, :], first[:, :, :]))
                c.end()
                for q in range(QT):
                    for k in range(2):
                        eng.indirect_dma_start(slots[:, :], bass.IndirectOffsetOnAxis(ap=slot_i[:, p, q, k:k + 1], axis=0),
                                               row[:, q, :], None, bounds_check=E * CAP - 1, oob_is_err=False)\
                           .then_inc(s_scat[p], 16)

            eng.wait_ge(s_tanh, 1)
            eng.wait_ge(s_zero, 16)
            eng.wait_ge(s_flag, 1)
            fast = eng.value_load(flag[0:1, 0:1], min_val=0, max_val=1)
            with eng.If(fast == 1):
                for b in range(2):
                    rstd_of(b)
                    split_k(padded, b, 0)
                    split_q(padded, b)
                max_parts(padded, 0)
                for b in range(B):
                    if b + 2 < B:
                        rstd_of(b + 2)
                        split_k(padded, b + 2, 0)
                    if b >= 1:
                        rstd2_of(b - 1)
                    if b + 2 < B:
                        split_q(padded, b + 2)
                    if b >= 1:
                        c = route_labels(b - 1, (b - 1) % 2)
                    if b + 1 < B:
                        max_parts(padded, b + 1)
                    if b >= 1:
                        scatter(b - 1, (b - 1) % 2, c)
                rstd2_of(B - 1)
                scatter(B - 1, (B - 1) % 2, route_labels(B - 1, (B - 1) % 2))
            with eng.Else():
                eng.memset(VSg[0], 0.0).then_inc(s_vg, 1)
                eng.memset(VSg[1], 0.0).then_inc(s_vg, 1)
                eng.wait_ge(s_vg, 2)
                for g in range(2):
                    eng.memset(VSg[g].rearrange("p t (h c) -> p (t h) c", c=VCOL)[:, :, DK:DK + 1], 1.0).then_inc(s_vg, 1)
                with eng.Fori(0, B) as b:
                    rstd_of(b)
                    for i in range(NWIN):
                        split_k(general, b, i)
                    split_q(general, b)
                    max_parts(general, b)
                    rstd2_of(b)
                    scatter(b, 0, route_labels(b, 0))
                    end_of_batch(eng, b)

            sw_chain = Chain(eng, s_sw, 14)
            for e in range(E):
                eng.wait_ge(s_disp[e], 32)
                c = sw_chain.at(e)
                for n, cs in ((P, slice(0, 2)), (64, slice(2, 3))):
                    number, first_w, second_w, first_e = (disp[0:n, e, cs, D + k] for k in range(4))
                    to, wt, is_first = slot_t[0:n, e, cs], slot_w[0:n, e, cs], spare[0:n, e, cs, 0]
                    c.next(eng.tensor_scalar(to, number, 0.0, SKIP, ALU.is_equal, ALU.mult))
                    c.next(eng.tensor_tensor(to, to, number, ALU.add))
                    c.next(eng.tensor_scalar(slot_to[0:n, e, cs], to, -1.0, None, ALU.add))
                    c.next(eng.tensor_scalar(is_first, first_e, float(e), None, ALU.is_equal))
                    c.next(eng.tensor_tensor(wt, first_w, second_w, ALU.subtract))
                    c.next(eng.tensor_tensor(wt, wt, is_first, ALU.mult))
                    c.next(eng.tensor_tensor(wt, wt, second_w, ALU.add))
                c.end()
            eng.wait_ge(s_x2out, 16 * B)
            for e in range(E):
                eng.wait_ge(s_orow, 3 * (e + 1))
                if e >= 1:
                    eng.wait_ge(s_add[(e - 1) % 2], 48 * ((e + 1) // 2))
                for k, (_, n) in enumerate(CT):
                    eng.indirect_dma_start(out_rows, bass.IndirectOffsetOnAxis(ap=slot_to[0:n, e, k:k + 1], axis=0),
                                           orow[0:n, e % 2, k, :], None, bounds_check=T - 1, oob_is_err=False,
                                           compute_op=ALU.add).then_inc(s_add[e % 2], 16)

        @block.scalar
        def _(eng):
            eng.dma_start(gates[:, 0:1], g_xattn.rearrange("(a n) -> a n", a=1).broadcast_to([P, 1])).then_inc(s_gates, 16)
            eng.dma_start(gates[:, 1:2], g_ffn.rearrange("(a n) -> a n", a=1).broadcast_to([P, 1])).then_inc(s_gates, 16)
            eng.dma_start(wg[:, :], w_g).then_inc(s_gates, 16)
            for q in range(QT):
                eng.dma_start(bg[:, q, :], b_g.rearrange("(a n) -> a n", a=1).broadcast_to([P, E])).then_inc(s_gates, 16)
            eng.wait_ge(s_vpre, 1)
            eng.dma_start(slots.rearrange("(p r) n -> p r n", p=P),
                          zrow[:, :].unsqueeze(1).broadcast_to([P, E * CAP // P, ROW])).then_inc(s_zero, 16)
            eng.wait_ge(s_gates, 80)
            eng.activation(tanhs[:, :], gates[:, :], ACT.Tanh).then_inc(s_tanh, 1)

            def copy_ctxT(path, b, i):
                n = b * path.nw + i
                eng.wait_ge(s_ctxT_ps, n + 1)
                if i >= 1 or not path.general:
                    wait(eng, s_v_ps, n)
                eng.activation(ctxT[:, :], ps_m[:, 0:WKEYS], ACT.Copy).then_inc(s_ctxT, 1)

            def high_k(path, b, i):
                n = b * path.nw + i
                eng.wait_ge(s_k_ps, n + 1)
                if i >= 1 or not path.general:
                    wait(eng, s_kd, 16 * n)
                eng.activation(kparts[:, 0, :], ps_m[:, 0:WKEYS], ACT.Copy).then_inc(s_k_hi, 1)

            def copy_xnT(b):
                eng.wait_ge(s_xnT_ps, b + 1)
                eng.activation(xnT[:, :], ps_m[:, 0:S], ACT.Copy).then_inc(s_xnT, 1)

            def copy_v(path, b, i):
                n = b * path.nw + i
                eng.wait_ge(s_v_ps, n + 1)
                if path.general:
                    eng.wait_ge(s_vg, 4)
                    g = 4 * i
                    dst = VSg[g // 8][:, g % 8:g % 8 + 4, :]
                else:
                    if b < NSET:
                        eng.wait_ge(s_vones, 2 * NSET)
                    wait(eng, s_pv, 4 * (b - NSET + 1))
                    dst = VSf[:, b % NSET, :, :]
                dst = dst.rearrange("p t (h c) -> p (t h) c", c=VCOL)[0:TILE + 1, :, 0:DK]
                src = ps_m[0:TILE + 1, :].rearrange("p (n c) -> p n c", c=DK)
                eng.activation(dst, src, ACT.Copy).then_inc(s_v, 1)

            def high_q(path, b):
                eng.wait_ge(s_q_ps, b + 1)
                if not path.general:
                    wait(eng, s_qd, 16 * b)
                eng.activation(qparts[:, 0, :], ps_m[:, 0:S], ACT.Copy).then_inc(s_q_hi, 1)

            def copy_mT(path, b):
                eng.wait_ge(s_mT_ps, b + 1)
                if not path.general:
                    wait(eng, s_mr, 96 * b)
                eng.activation(mT[:, :], ps_m[0:3 * H, 0:S // 2].bitcast(BF16), ACT.Copy).then_inc(s_mT, 1)

            def exp(path, b, r, j):
                n = 16 * path.nw * b + 4 * r + j
                eng.wait_ge(s_st, n + 1)
                if r >= 2 or not path.general:
                    wait(eng, s_pv, 4 * path.nw * b + r - 1)
                eng.activation(probs[0:TILE + 1, (4 * r + j) % 8, :], ps_t[(4 * r + j) % 2][0:TILE + 1, :], ACT.Exp,
                               scale=SCALE).then_inc(s_ex, 1)

            def copy_o(path, b, u):
                eng.wait_ge(s_pv, path.nw * (4 * b + u + 1))
                if u >= 1 or not path.general:
                    wait(eng, s_oq, 4 * b + u)
                eng.activation(OT[:, :], ps_o[:, 0:S], ACT.Copy).then_inc(s_ot, 1)

            def copy_oc(b):
                eng.wait_ge(s_oc_ps, b + 1)
                eng.activation(OCT[:, :], ps_m[:, 0:S], ACT.Copy).then_inc(s_oc, 1)

            def copy_xn2T(b):
                eng.wait_ge(s_xn2T_ps, b + 1)
                eng.activation(xn2T[:, :], ps_m[:, 0:S], ACT.Copy).then_inc(s_xn2T, 1)

            def exp_gap(b):
                eng.wait_ge(s_gap, b + 1)
                if isinstance(b, int):
                    wait(eng, s_rt, 19 * b)
                eng.activation(e2[:, :], gap[:, :], ACT.Exp).then_inc(s_e2, 1)

            eng.wait_ge(s_flag, 1)
            fast = eng.value_load(flag[0:1, 0:1], min_val=0, max_val=1)
            with eng.If(fast == 1):
                for b in range(2):
                    copy_ctxT(padded, b, 0)
                    high_k(padded, b, 0)
                    copy_xnT(b)
                    copy_v(padded, b, 0)
                    high_q(padded, b)
                copy_mT(padded, 0)
                for b in range(B):
                    for h in range(H):
                        exp(padded, b, h // 4, h % 4)
                        if b + 2 < B:
                            if h == 0:
                                copy_ctxT(padded, b + 2, 0)
                            if h == 1:
                                high_k(padded, b + 2, 0)
                            if h == 2:
                                copy_xnT(b + 2)
                            if h == 3:
                                copy_v(padded, b + 2, 0)
                            if h == 4:
                                high_q(padded, b + 2)
                        if b >= 1:
                            if h == 5:
                                copy_xn2T(b - 1)
                            if h == 10:
                                exp_gap(b - 1)
                        if h % 4 == 2 and h >= 6:
                            copy_o(padded, b, h // 4 - 1)
                        if h == 14 and b + 1 < B:
                            copy_mT(padded, b + 1)
                    copy_o(padded, b, 3)
                    copy_oc(b)
                copy_xn2T(B - 1)
                exp_gap(B - 1)
            with eng.Else():
                for t in range(0, NT, 4):
                    eng.wait_ge(s_bT_ps, t // 4 + 1)
                    eng.activation(biasT[0:TILE + 1, t:t + 4, :].rearrange("p t q -> p (t q)"),
                                   ps_m[0:TILE + 1, :].bitcast(BF16), ACT.Copy).then_inc(s_bT, 1)
                with eng.Fori(0, B) as b:
                    for i in range(NWIN):
                        copy_ctxT(general, b, i)
                        high_k(general, b, i)
                        copy_v(general, b, i)
                    copy_xnT(b)
                    high_q(general, b)
                    copy_mT(general, b)
                    for u in range(4):
                        for i in range(NWIN):
                            for j in range(4):
                                exp(general, b, NWIN * u + i, j)
                        copy_o(general, b, u)
                    copy_oc(b)
                    copy_xn2T(b)
                    exp_gap(b)
                    end_of_batch(eng, b)

            def silu_of(e, k):
                n = HK * e + k
                eng.wait_ge(s_h_ps, n + 1)
                wait(eng, s_h, n - 1)
                eng.activation(silu[:, n % 2, :], ps_t[n % 2][:, 0:CAP], ACT.Silu).then_inc(s_silu, 1)

            def weighted_rows(e):
                eng.wait_ge(s_o_ps, e + 1)
                eng.wait_ge(s_sw, 14 * (e + 1))
                wait(eng, s_add[e % 2], 48 * (e // 2))
                for k, (_, n) in enumerate(CT):
                    eng.activation(orow[0:n, e % 2, k, :], ps_s[e % 2][0:n, D * k:D * (k + 1)], ACT.Copy,
                                   scale=slot_w[0:n, e, k:k + 1]).then_inc(s_orow, 1)

            for e in range(E):
                for k in range(HK):
                    silu_of(e, k)
                    if k == 1 and e >= 1:
                        weighted_rows(e - 1)
            weighted_rows(E - 1)

        @block.tensor
        def _(eng):
            eng.wait_ge(s_pre, 5)
            eng.wait_ge(s_w, 64)
            for n in range(4):
                ins = eng.transpose(ps_m[:, D * n:D * (n + 1)], wraw[:, n, :], ident[:, :])
            ins.then_inc(s_wT_ps, 1)
            eng.wait_ge(s_attend, 1)
            for q in range(QT):
                eng.matmul(ps_s[0][0:1, 0:WKEYS], onesb[:, 0:1], attend[:, q, SK - WKEYS:SK],
                           start=(q == 0), stop=(q == QT - 1)).then_inc(s_col, 1)
            for n in range(QT * (NWIN - 1)):
                q, w = n % QT, n // QT
                eng.matmul(ps_s[1][0:1, 0:WIN], onesb[:, 0:1], attend[:, q, WIN * w:WIN * (w + 1)],
                           start=(n == 0), stop=(n == QT * (NWIN - 1) - 1)).then_inc(s_col, 1)

            def turn_ctx(path, b, i, free):
                wait(eng, *free)
                if path.general:
                    eng.wait_ge(s_ctx[i % 2], 32 * (2 * b + i // 2 + 1))
                    cb = i % 2
                else:
                    eng.wait_ge(s_ctx[b % 2], 32 * (b // 2 + 1))
                    cb = b % 2
                for t in range(4):
                    n = TILE + (t == 3)
                    ins = eng.transpose(ps_m[:, TILE * t:TILE * t + n], C[0:n, cb, t, :], ident[0:n, 0:n])
                ins.then_inc(s_ctxT_ps, 1)

            def project_k(path, b, i):
                eng.wait_ge(s_ctxT, b * path.nw + i + 1)
                eng.matmul(ps_m[:, 0:WKEYS], wT[:, 1, :], ctxT[:, :], start=True, stop=True).then_inc(s_k_ps, 1)

            def turn_xn(b, free):
                wait(eng, *free)
                eng.wait_ge(s_xn, 2 * (b + 1))
                for q in range(QT):
                    ins = eng.transpose(ps_m[:, P * q:P * (q + 1)], xn[:, q, :], ident[:, :])
                ins.then_inc(s_xnT_ps, 1)

            def project_v(path, b, i, free):
                wait(eng, *free)
                eng.wait_ge(s_ctxT, b * path.nw + i + 1)
                for t in range(4):
                    ins = eng.matmul(ps_m[0:TILE + 1, D * t:D * (t + 1)], ctxT[:, TILE * t:TILE * t + TILE + 1],
                                     wT[:, 2, :], start=True, stop=True)
                ins.then_inc(s_v_ps, 1)

            def project_q(b, free):
                wait(eng, *free)
                eng.wait_ge(s_xnT, b + 1)
                eng.matmul(ps_m[:, 0:S], wT[:, 0, :], xnT[:, :], start=True, stop=True).then_inc(s_q_ps, 1)

            def score_for_max(path, b, k):
                i, h, q = k // (2 * H), k // 2 % H, k % 2
                n = 2 * H * path.nw * b + k
                if k % (2 * H) == 0:
                    if path.general:
                        eng.wait_ge(s_ks[i], 192 * (b + 1))
                    else:
                        eng.wait_ge(s_ks[b % NSET], 192 * (b // NSET + 1))
                if k == 0:
                    if path.general:
                        eng.wait_ge(s_qs[0], 192 * (b + 1))
                    else:
                        eng.wait_ge(s_qs[b % NSET], 192 * (b // NSET + 1))
                    eng.wait_ge(s_const, 16 * 9)
                if not path.general:
                    wait(eng, s_mx, n - 1)
                elif k >= 2:
                    eng.wait_ge(s_mgen, 257 * b + 2 * (k - 2) + 1)
                eng.matmul(ps_s[k % 2][:, 0:WKEYS], QS[0:MAX_ROW, path.set_of(b), h // 2, h % 2, P * q:P * (q + 1)],
                           path.ks(b, i)[0:MAX_ROW, h // 2, :], start=True, stop=True).then_inc(s_sc, 1)

            def turn_max(b, free):
                wait(eng, *free)
                wait(eng, s_mp, 6 * (b + 1))
                dst = ps_m[0:3 * H, 0:S // 2].bitcast(BF16)
                for q in range(QT):
                    ins = eng.transpose(dst[:, P * q:P * (q + 1)], mparts[:, q, :, :].rearrange("p c h -> p (c h)"), identb[:, :])
                ins.then_inc(s_mT_ps, 1)

            def score_for_exp(path, b, r, j):
                u, i = r // path.nw, r % path.nw
                h, k = 4 * u + j, 4 * r + j
                n = 16 * path.nw * b + k
                if k == 0:
                    eng.wait_ge(s_mr, 96 * (b + 1))
                if k >= 2 or not path.general:
                    wait(eng, s_ex, n - 1)
                dst, st = ps_t[k % 2], path.set_of(b)
                for t in range(4):
                    ins = eng.matmul(dst[0:TILE + 1, S * t:S * (t + 1)],
                                     path.ks(b, i)[0:SROWS, h // 2, TILE * t:TILE * t + TILE + 1],
                                     QS[0:SROWS, st, h // 2, h % 2, :], start=True, stop=not path.general)
                    if path.general:
                        ins = eng.matmul(dst[0:TILE + 1, S * t:S * (t + 1)], identb[0:TILE + 1, 0:TILE + 1],
                                         biasT[0:TILE + 1, 4 * i + t, :], start=False, stop=True)
                ins.then_inc(s_st, 1)

            def weigh_v(path, b, r):
                u, i = r // path.nw, r % path.nw
                eng.wait_ge(s_ex, path.nw * 16 * b + 4 * r + 4)
                if u == 0 and i == 0:
                    eng.wait_ge(s_v, path.nw * (b + 1))
                if i == 0 and (u >= 1 or not path.general):
                    wait(eng, s_ot, 4 * b + u)
                for t in range(4):
                    d = path.depth(i, t)
                    for j in range(4):
                        h = 4 * u + j
                        ins = eng.matmul(ps_o[VCOL * j:VCOL * (j + 1), 0:S],
                                         path.vs(b, i, t)[0:d, VCOL * h:VCOL * (h + 1)],
                                         probs[0:d, (4 * r + j) % 8, S * t:S * (t + 1)],
                                         start=(i == 0 and t == 0), stop=(i == path.nw - 1 and t == 3))
                ins.then_inc(s_pv, 1)

            def turn_out(b, u, free):
                wait(eng, *free)
                eng.wait_ge(s_ot, 4 * b + u + 1)
                for q in range(QT):
                    ins = eng.transpose(ps_m[:, P * q:P * (q + 1)], OT[:, P * q:P * (q + 1)], ident[:, :])
                ins.then_inc(s_oq, 1)

            def turn_normed(b):
                eng.wait_ge(s_on, 4 * (b + 1))
                for q in range(QT):
                    ins = eng.transpose(ps_m[:, P * q:P * (q + 1)], O[:, q, :, :].rearrange("p h d -> p (h d)"), ident[:, :])
                ins.then_inc(s_oc_ps, 1)

            def project_out(b):
                eng.wait_ge(s_oc, b + 1)
                for q in range(QT):
                    ins = eng.matmul(ps_m[:, D * q:D * (q + 1)], OCT[:, P * q:P * (q + 1)], wT[:, 3, :], start=True, stop=True)
                ins.then_inc(s_y, 1)

            def turn_xn2(b, p, free):
                wait(eng, *free)
                eng.wait_ge(s_xn2, 2 * (b + 1))
                for q in range(QT):
                    ins = eng.transpose(ps_m[:, P * q:P * (q + 1)], rows[:, p, q, 0:D], ident[:, :])
                ins.then_inc(s_xn2T_ps, 1)

            def make_logits(b, free):
                wait(eng, *free)
                eng.wait_ge(s_xn2T, b + 1)
                for q in range(QT):
                    ins = eng.matmul(ps_m[:, E * q:E * (q + 1)], xn2T[:, P * q:P * (q + 1)], wg[:, :], start=True, stop=True)
                ins.then_inc(s_lg_ps, 1)

            def number_tokens(b, free):
                wait(eng, *free)
                eng.wait_ge(s_rt, 19 * b + 8)
                both = QT * E
                eng.matmul(ps_m[:, 0:both], tri[:, :], label[:, :, :].rearrange("p q e -> p (q e)"), start=True, stop=False)
                eng.matmul(ps_m[:, 0:both], onesb[:, :], before[:, 0:QT, :].rearrange("p q e -> p (q e)"),
                           start=False, stop=True).then_inc(s_seq, 1)

            eng.wait_ge(s_wT, 2)
            eng.wait_ge(s_gates, 80)
            eng.wait_ge(s_flag, 1)
            fast = eng.value_load(flag[0:1, 0:1], min_val=0, max_val=1)
            with eng.If(fast == 1):
                for b in range(2):
                    turn_ctx(padded, b, 0, (s_q_r, b))
                    project_k(padded, b, 0)
                    turn_xn(b, (s_k_r, b + 1))
                    project_v(padded, b, 0, (s_xnT, b + 1))
                    project_q(b, (s_v, b + 1))
                for k in range(2 * H):
                    score_for_max(padded, 0, k)
                turn_max(0, (s_q_r, 2))
                for b in range(B):
                    left = list(range(2 * H)) if b + 1 < B else []
                    for h in range(H):
                        score_for_exp(padded, b, h // 4, h % 4)
                        if b + 2 < B:
                            if h == 0:
                                turn_ctx(padded, b + 2, 0, (s_x2, b) if b else (s_mT, 1))
                            if h == 1:
                                project_k(padded, b + 2, 0)
                            if h == 2:
                                turn_xn(b + 2, (s_k_r, b + 3))
                            if h == 3:
                                project_v(padded, b + 2, 0, (s_xnT, b + 3))
                            if h == 4:
                                project_q(b + 2, (s_v, b + 3))
                        if h == 5 and b >= 1:
                            turn_xn2(b - 1, (b - 1) % 2, (s_q_r, b + 3) if b + 2 < B else (s_x2, b))
                        if h == 7:
                            turn_out(b, 0, (s_xn2T, b) if b else (s_q_r, 3))
                        if h == 8 and b >= 1:
                            make_logits(b - 1, (s_on, 4 * b + 1))
                        if h == 12 and b >= 1:
                            number_tokens(b - 1, (s_lg, b))
                        if h == 13:
                            turn_out(b, 1, (s_pick, b) if b else (s_on, 1))
                        if h == 14 and b + 1 < B:
                            turn_max(b + 1, (s_on, 4 * b + 2))
                        if h == 15:
                            turn_out(b, 2, (s_mT, b + 2) if b + 1 < B else (s_on, 4 * b + 2))
                        if h % 4 == 1 and h >= 5:
                            weigh_v(padded, b, h // 4 - 1)
                        for k in left[3 * h:3 * h + 3]:
                            score_for_max(padded, b + 1, k)
                    weigh_v(padded, b, 3)
                    turn_out(b, 3, (s_on, 4 * b + 3))
                    turn_normed(b)
                    project_out(b)
                turn_xn2(B - 1, (B - 1) % 2, (s_x2, B))
                make_logits(B - 1, (s_xn2T, B))
                number_tokens(B - 1, (s_lg, B))
            with eng.Else():
                eng.wait_ge(s_gb, 4)
                for t in range(NT):
                    if t % 4 == 0 and t:
                        eng.wait_ge(s_bT, t // 4)
                    for q in range(QT):
                        ins = eng.transpose(ps_m[0:TILE + 1, :].bitcast(BF16)[:, S * (t % 4) + P * q:S * (t % 4) + P * (q + 1)],
                                            attend[:, q, TILE * t:TILE * t + TILE + 1], identb[:, :])
                    if t % 4 == 3:
                        ins.then_inc(s_bT_ps, 1)
                eng.wait_ge(s_bT, 4)
                with eng.Fori(0, B) as b:
                    for i in range(NWIN):
                        turn_ctx(general, b, i, (s_v, NWIN * b + i) if i else (s_bT, 4))
                        project_k(general, b, i)
                        project_v(general, b, i, (s_k_r, NWIN * b + i + 1))
                    turn_xn(b, (s_v, NWIN * (b + 1)))
                    project_q(b, (s_xnT, b + 1))
                    for k in range(2 * H * NWIN):
                        score_for_max(general, b, k)
                    turn_max(b, (s_q_r, b + 1))
                    for u in range(4):
                        for i in range(NWIN):
                            for j in range(4):
                                score_for_exp(general, b, NWIN * u + i, j)
                            weigh_v(general, b, NWIN * u + i)
                        turn_out(b, u, (s_on, 4 * b + u) if u else (s_mT, b + 1))
                    turn_normed(b)
                    project_out(b)
                    turn_xn2(b, 0, (s_x2, b + 1))
                    make_logits(b, (s_xn2T, b + 1))
                    number_tokens(b, (s_lg, b + 1))
                    end_of_batch(eng, b)

            def turn_slots(e):
                if e == 0:
                    eng.wait_ge(s_pick, B)
                else:
                    eng.wait_ge(s_dT, e)
                eng.wait_ge(s_disp[e], 32)
                for k, (c0, n) in enumerate(CT):
                    ins = eng.transpose(ps_m[:, c0:c0 + n], disp[0:n, e, k, 0:D], ident[0:n, 0:n])
                ins.then_inc(s_dT_ps, 1)

            def hidden(e, k):
                n = HK * e + k
                if k == 0:
                    eng.wait_ge(s_dT, e + 1)
                    wait(eng, s_expw, 48 * E if e == 0 else 0)
                wait(eng, s_h, n - 1)
                for g, w in enumerate((W1S, W2S)):
                    ins = eng.matmul(ps_t[n % 2][:, 512 * g:512 * g + CAP], w[:, e, P * k:P * (k + 1)],
                                     dispT[:, e % 2, :], start=True, stop=True)
                ins.then_inc(s_h_ps, 1)

            def expert_out(e):
                eng.wait_ge(s_h, HK * (e + 1))
                wait(eng, s_orow, 3 * (e - 1))
                for c, (c0, n) in enumerate(CT):
                    for k in range(HK):
                        ins = eng.matmul(ps_s[e % 2][0:n, D * c:D * (c + 1)], hT[e % 2][:, k, c0:c0 + n], W3S[:, e, k, :],
                                         start=(k == 0), stop=(k == HK - 1))
                ins.then_inc(s_o_ps, 1)

            turn_slots(0)
            for e in range(E):
                for k in range(HK):
                    hidden(e, k)
                    if k == 1 and e >= 1:
                        expert_out(e - 1)
                    if k == 2 and e + 1 < E:
                        turn_slots(e + 1)
            expert_out(E - 1)

        @block.vector
        def _(eng):
            eng.memset(zrow[:, :], 0.0).then_inc(s_vpre, 1)
            eng.memset(ones_row[:, :], 1.0).then_inc(s_rowpat, 1)
            eng.memset(zero_row[:, :], 0.0).then_inc(s_rowpat, 1)
            for st in range(NSET):
                eng.memset(QS[:, st].rearrange("p s h q -> p (s h q)").bitcast(U32), 0).then_inc(s_fill, 1)
            eng.wait_ge(s_wT_ps, 1)
            eng.tensor_copy(wT[:, 0:3, :], ps_m[:, 0:3 * D].rearrange("p (n d) -> p n d", n=3)).then_inc(s_wT, 1)
            eng.wait_ge(s_tanh, 1)
            eng.tensor_scalar(wT[:, 3, :], ps_m[:, 3 * D:4 * D], tanhs[:, 0:1], None, ALU.mult).then_inc(s_wT, 1)
            eng.wait_ge(s_mask, 16)
            eng.tensor_scalar(attend[:, :, :], maski, 0.0, None, ALU.not_equal).then_inc(s_attend, 1)
            stats = Chain(eng, s_stat, 11).at(0)
            eng.wait_ge(s_col, 2)
            stats.next(eng.tensor_copy(colsum[:, 0, :], ps_s[0][0:1, 0:WKEYS]))
            stats.next(eng.tensor_scalar(colsum[:, 1, :], colsum[:, 0, :], -1.0, float(S), ALU.mult, ALU.add))
            stats.next(eng.tensor_tensor(colsum[:, 2, :], colsum[:, 0, :], colsum[:, 1, :], ALU.min))
            stats.next(eng.tensor_reduce(stat[:, 0:1], colsum[:, 2, :], AX.X, ALU.max))
            stats.next(eng.tensor_reduce(stat[:, 1:2], colsum[:, 0, :], AX.X, ALU.max))
            eng.wait_ge(s_col, QT * NWIN)
            stats.next(eng.tensor_reduce(stat[:, 2:3], ps_s[1][0:1, 0:WIN], AX.X, ALU.max))
            stats.next(eng.tensor_tensor(stat[:, 3:4], stat[:, 0:1], stat[:, 2:3], ALU.add))
            stats.next(eng.tensor_scalar(stat[:, 4:5], stat[:, 3:4], 0.0, None, ALU.is_equal))
            stats.next(eng.tensor_scalar(stat[:, 5:6], stat[:, 1:2], float(S), None, ALU.is_equal))
            stats.next(eng.tensor_tensor(stat[:, 6:7], stat[:, 4:5], stat[:, 5:6], ALU.mult))
            stats.next(eng.tensor_copy(flag[:, :], stat[:, 6:7]))
            stats.end()
            eng.tensor_scalar(keybias[:, :], colsum[:, 1, :], -FAR / S, None, ALU.mult).then_inc(s_kbias, 1)
            eng.tensor_copy(stat[:, 7:8], stat[:, 6:7]).then_inc(s_flag, 1)

            ln = Chain(eng, s_ln, 4, wait)
            ln2 = Chain(eng, s_ln2, 4, wait)
            gmax = Chain(eng, s_mgen, 4 * H * NWIN + 1, wait)

            def moments(b):
                wait(eng, s_rs, 2 * b) if isinstance(b, int) else None
                if isinstance(b, int):
                    eng.wait_ge(s_x[min(b, 2)], 16)
                c, xb = ln.at(b), x_pair(b)
                for q in range(QT):
                    c.next(eng.bn_stats(bn[:, q, :], xb[:, q, :]))
                for q in range(QT):
                    c.next(eng.bn_aggr(mv[:, q, :], bn[:, q, :]))

            def normalise(path, b):
                wait(eng, s_rs, 2 * (b + 1))
                if path.general:
                    eng.tensor_tensor(rstd[:, :], rstd[:, :], valid[:, 1, :], ALU.mult).then_inc(s_rv, 1)
                    wait(eng, s_rv, b + 1)
                else:
                    wait(eng, s_xnT_ps, b)
                xb = x_pair(b)
                for q in range(QT):
                    eng.tensor_scalar(xn[:, q, :], xb[:, q, :], mv[:, q, 0:1], rstd[:, q:q + 1], ALU.subtract, ALU.mult)\
                       .then_inc(s_xn, 1)

            def rest_k(path, b, i):
                n = b * path.nw + i
                wait(eng, s_k_hi, n + 1)
                if i >= 1 or not path.general:
                    wait(eng, s_k_lo, n)
                eng.tensor_tensor(krest[:, :], ps_m[:, 0:WKEYS], kparts[:, 0, :], ALU.subtract).then_inc(s_k_r, 1)

            def rest_q(path, b):
                wait(eng, s_q_hi, b + 1)
                if not path.general:
                    wait(eng, s_q_lo, b)
                eng.tensor_tensor(qrest[:, :], ps_m[:, 0:S], qparts[:, 0, :], ALU.subtract).then_inc(s_q_r, 1)

            def maximum(b, k):
                if k == 0:
                    wait(eng, s_mp, 6 * (b - 1))
                wait(eng, s_sc, 2 * H * b + k + 1)
                eng.tensor_reduce(wmax[:, b % 2, k % 2, k // 2:k // 2 + 1], ps_s[k % 2][:, 0:WKEYS], AX.X, ALU.max)\
                   .then_inc(s_mx, 1)

            def general_maxima(b):
                c = gmax.at(b)
                for k in range(2 * H * NWIN):
                    i, h, q = k // (2 * H), k // 2 % H, k % 2
                    wait(eng, s_sc, 2 * H * NWIN * b + k + 1)
                    c.next(eng.tensor_tensor(masked, ps_s[k % 2][:, 0:WKEYS], attend[:, q, WIN * i:WIN * i + WKEYS], ALU.add))
                    c.next(eng.tensor_reduce(wmax[:, i, q, h:h + 1], masked, AX.X, ALU.max))
                c.next(eng.tensor_reduce(rowmax[:, :, :].rearrange("p q h -> p (q h)"),
                                         wmax[:, :, :, :].rearrange("p i q h -> p (q h) i"), AX.X, ALU.max))
                c.end()

            def norm_out(path, b, u):
                wait(eng, s_oq, 4 * b + u + 1)
                if u >= 1 or not path.general:
                    wait(eng, s_on, 4 * b + u)
                if u == 0 and not path.general:
                    wait(eng, s_oc_ps, b)
                turned = ps_m[:, 0:S].rearrange("p (q j c) -> p q j c", q=QT, c=VCOL)
                eng.reciprocal(rsum[:, :, :], turned[:, :, :, DK]).then_inc(s_rsum, 1)
                wait(eng, s_rsum, 4 * b + u + 1)
                for q in range(QT):
                    ins = eng.tensor_tensor(O[:, q, 4 * u:4 * u + 4, :], turned[:, q, :, 0:DK],
                                            rsum[:, q, :].unsqueeze(2).broadcast_to([P, 4, DK]), ALU.mult)
                    if q == QT - 1:
                        ins.then_inc(s_on, 1)

            def add_out(b):
                wait(eng, s_y, b + 1)
                xb = x_pair(b)
                eng.tensor_tensor(xb, ps_m[:, 0:S].rearrange("p (q d) -> p q d", q=QT), xb, ALU.add).then_inc(s_x2, 1)

            def moments2(b):
                wait(eng, s_x2, b + 1)
                if isinstance(b, int):
                    wait(eng, s_rs2, 2 * b)
                c, xb = ln2.at(b), x_pair(b)
                for q in range(QT):
                    c.next(eng.bn_stats(bn2[:, q, :], xb[:, q, :]))
                for q in range(QT):
                    c.next(eng.bn_aggr(mv2[:, q, :], bn2[:, q, :]))

            def normalise2(b, p):
                wait(eng, s_rs2, 2 * (b + 1))
                if isinstance(b, int):
                    wait(eng, s_scat[p], 64 * (b // 2))
                xb = x_pair(b)
                for q in range(QT):
                    eng.tensor_scalar(rows[:, p, q, 0:D], xb[:, q, :], mv2[:, q, 0:1], rstd2[:, q:q + 1],
                                      ALU.subtract, ALU.mult).then_inc(s_xn2, 1)

            def top_two(b):
                if isinstance(b, int):
                    wait(eng, s_rt, 19 * b)
                wait(eng, s_lg_ps, b + 1)
                eng.tensor_tensor(logits[:, :, :], ps_m[:, 0:QT * E].rearrange("p (q e) -> p q e", q=QT), bg[:, :, :], ALU.add)\
                   .then_inc(s_lg, 1)
                wait(eng, s_lg, b + 1)
                for q in range(QT):
                    eng.max(top[:, q, :], logits[:, q, :]).then_inc(s_top, 1)
                for q in range(QT):
                    wait(eng, s_top, 2 * b + q + 1)
                    eng.max_index(topi[:, q, :], top[:, q, :], logits[:, q, :]).then_inc(s_topi, 1)

            def invert_den(b):
                wait(eng, s_rt, 19 * b + 9)
                eng.reciprocal(rden[:, :], den[:, :]).then_inc(s_rden, 1)

            def pick_places(b):
                wait(eng, s_seq, b + 1)
                for q in range(QT):
                    ins = eng.tensor_tensor(picked[:, q, :, :], ps_m[:, E * q:E * (q + 1)].unsqueeze(1).broadcast_to([P, 2, E]),
                                            hot[:, q, :, :], ALU.mult)
                    ins.then_inc(s_pickq, 1) if q == 0 else ins.then_inc(s_pick, 1)
                wait(eng, s_pickq, b + 1)
                wait(eng, s_pick, b + 1)
                eng.tensor_reduce(place[:, :, :].rearrange("p q c -> p (q c)"),
                                  picked[:, :, :, :].rearrange("p q c e -> p (q c) e"), AX.X, ALU.add).then_inc(s_place, 1)

            fast = eng.value_load(flag[0:1, 0:1], min_val=0, max_val=1)
            with eng.If(fast == 1):
                for b in range(2):
                    moments(b)
                    rest_k(padded, b, 0)
                    normalise(padded, b)
                    rest_q(padded, b)
                for k in range(2 * H):
                    maximum(0, k)
                for b in range(B):
                    left = list(range(2 * H)) if b + 1 < B else []
                    for h in range(H):
                        if b + 2 < B:
                            if h == 0:
                                moments(b + 2)
                            if h == 1:
                                rest_k(padded, b + 2, 0)
                                normalise(padded, b + 2)
                            if h == 4:
                                rest_q(padded, b + 2)
                        if b >= 1:
                            if h == 2:
                                moments2(b - 1)
                            if h == 4:
                                normalise2(b - 1, (b - 1) % 2)
                            if h == 9:
                                top_two(b - 1)
                            if h == 11:
                                invert_den(b - 1)
                            if h == 12:
                                pick_places(b - 1)
                        if h in (8, 14):
                            norm_out(padded, b, h // 14)
                        for k in left[3 * h:3 * h + 3]:
                            maximum(b + 1, k)
                    norm_out(padded, b, 2)
                    norm_out(padded, b, 3)
                    add_out(b)
                moments2(B - 1)
                normalise2(B - 1, (B - 1) % 2)
                top_two(B - 1)
                invert_den(B - 1)
                pick_places(B - 1)
            with eng.Else():
                gb = Chain(eng, s_gb, 4).at(0)
                gb.next(eng.tensor_reduce(valid[:, 0, :], attend[:, :, :], AX.X, ALU.max))
                gb.next(eng.tensor_scalar(valid[:, 1, :], valid[:, 0, :], 0.0, None, ALU.is_gt))
                gb.next(eng.tensor_scalar(valid[:, 2, :], valid[:, 1, :], FAR, None, ALU.mult))
                for q in range(QT):
                    ins = eng.tensor_scalar(attend[:, q, :], attend[:, q, :], -1.0, valid[:, 2, q:q + 1], ALU.add, ALU.mult)
                    if q == 0:
                        ins.then_inc(s_gbq, 1)
                gb.next(ins)
                eng.wait_ge(s_gbq, 1)
                for n in range(3):
                    eng.wait_ge(s_x[n], 16)
                with eng.Fori(0, B) as b:
                    moments(b)
                    for i in range(NWIN):
                        rest_k(general, b, i)
                    normalise(general, b)
                    rest_q(general, b)
                    general_maxima(b)
                    for u in range(4):
                        norm_out(general, b, u)
                    add_out(b)
                    moments2(b)
                    normalise2(b, 0)
                    top_two(b)
                    invert_den(b)
                    pick_places(b)
                    end_of_batch(eng, b)

            def copy_slots(e):
                eng.wait_ge(s_dT_ps, e + 1)
                wait(eng, s_h_ps, HK * (e - 1))
                eng.tensor_copy(dispT[:, e % 2, :], ps_m[:, 0:CAP]).then_inc(s_dT, 1)

            copy_slots(0)
            for e in range(E):
                for k in range(HK):
                    n = HK * e + k
                    eng.wait_ge(s_silu, n + 1)
                    wait(eng, s_o_ps, e - 1)
                    eng.tensor_tensor(hT[e % 2][:, k, :], ps_t[n % 2][:, 512:512 + CAP], silu[:, n % 2, :], ALU.mult)\
                       .then_inc(s_h, 1)
                    if k == 2 and e + 1 < E:
                        copy_slots(e + 1)


_INS = ["x", "ctx_1024", "mask_1x1xSxS2_ik0", "g_xattn", "g_ffn", "L0_xattn_w_q", "L0_xattn_w_k", "L0_xattn_w_v",
        "L0_xattn_w_o", "L0_ffn_Wg", "L0_ffn_bg", "L0_ffn_W1", "L0_ffn_W2", "L0_ffn_W3"]
_OUT = ((B, S, D), "float32")


def kernel(**inputs):
    import numpy as _np
    import concourse.bacc as _bacc
    from concourse import mybir as _mybir
    from concourse.bass_utils import run_bass_kernel_spmd as _run

    nc = _bacc.Bacc("TRN2", target_bir_lowering=False, num_devices=1)
    arrays, args = {}, []
    for name in _INS:
        a = _np.ascontiguousarray(inputs[name])
        arrays[f"in_{name}_dram"] = a
        args.append(nc.dram_tensor(f"in_{name}_dram", a.shape, _mybir.dt.from_np(a.dtype), kind="ExternalInput").ap())
    shape, dtype = _OUT
    args.append(nc.dram_tensor("out_0_dram", shape, _mybir.dt.from_np(_np.dtype(dtype)), kind="ExternalOutput").ap())
    flamingo_kernel(nc, *args)
    r = _run(nc, [arrays], core_ids=[0])
    return r.results[0]["out_0_dram"]
```

```python
from contextlib import ExitStack

import concourse.bass as bass
from concourse import mybir

F32 = mybir.dt.float32
BF16 = mybir.dt.bfloat16
I32 = mybir.dt.int32
U32 = mybir.dt.uint32
ALU = mybir.AluOpType
ACT = mybir.ActivationFunctionType
AX = mybir.AxisListType

P = 128
B, S, D = 8, 256, 128
H, DK = 16, 8
SK = 1601
QT = S // P
NWIN = 4
TILE = 100
WIN = 4 * TILE
WKEYS = WIN + 1
NT = NWIN * 4
E, HID, CAP = 8, 512, 320
HK = HID // P
T = B * S
NTT = T // P
ROW = D + 4
PAIRS = H // 2
PROWS = 6 * DK
MASK_ROW = 2 * PROWS
MAX_ROW = MASK_ROW + 1
SROWS = MAX_ROW + 3
NSET = 3
KPAD = WKEYS + 1
VCOL = 32
SCALE = float(DK) ** -0.5
EPS = 1e-5
FAR = 1.0e30
SKIP = 1.0e6
CT = [(0, 128), (128, 128), (256, 64)]


class Chain:

    def __init__(self, eng, sem, per, wait=None):
        self.eng, self.sem, self.per, self.wait = eng, sem, per, wait or (lambda eng, s, value: eng.wait_ge(s, value))

    def at(self, b):
        self.base, self.k = b * self.per, 0
        return self

    def next(self, instruction):
        self.k += 1
        instruction.then_inc(self.sem, 1)
        self.wait(self.eng, self.sem, self.base + self.k)

    def also(self, instruction):
        self.k += 1
        instruction.then_inc(self.sem, 1)

    def end(self):
        assert self.k == self.per, (self.k, self.per)


def flamingo_kernel(nc, x, ctx, mask, g_xattn, g_ffn, w_q, w_k, w_v, w_o, w_g, b_g, w1, w2, w3, out):
    slots = nc.dram_tensor("slots", [E * CAP, ROW], F32, kind="Internal").ap()
    kspread = nc.dram_tensor("kspread", [NSET, P, 6, WKEYS], BF16, kind="Internal").ap()
    qspread = nc.dram_tensor("qspread", [NSET, P, 6, S], BF16, kind="Internal").ap()
    out_rows = out.rearrange("b s d -> (b s) d")
    x_tiles = x.rearrange("b (q p) d -> p b q d", p=P)
    out_tiles = out.rearrange("b (q p) d -> p b q d", p=P)

    with ExitStack() as stack:
        def sb(name, shape, dt):
            return stack.enter_context(nc.sbuf_tensor(name, shape, dt))

        def sem(name):
            return stack.enter_context(nc.semaphore(name))

        ident = sb("ident", [P, P], F32)
        identb = sb("identb", [P, P], BF16)
        onesb = sb("onesb", [P, P], BF16)
        tri = sb("tri", [P, P], BF16)
        zrow = sb("zrow", [P, ROW], F32)
        iota8i = sb("iota8i", [P, E], I32)
        iota8 = sb("iota8", [P, E], F32)
        tok_i = sb("tok_i", [P, NTT], I32)
        tok = sb("tok", [P, NTT], F32)
        ones_row = sb("ones_row", [3, KPAD], BF16)
        zero_row = sb("zero_row", [1, KPAD], BF16)
        halfpow = sb("halfpow", [P, 2], F32)
        wraw = sb("wraw", [P, 4, D], F32)
        wT = sb("wT", [P, 4, D], F32)
        wg = sb("wg", [P, E], F32)
        bg = sb("bg", [P, QT, E], F32)
        gates = sb("gates", [P, 2], F32)
        tanhs = sb("tanhs", [P, 2], F32)
        attend = sb("attend", [P, QT, SK], BF16)
        colsum = sb("colsum", [1, 3, WKEYS], F32)
        stat = sb("stat", [1, 8], F32)
        keybias = sb("keybias", [1, WKEYS], BF16)
        flag = sb("flag", [1, 1], I32)
        X = sb("X", [P, NTT, D], F32)
        C = sb("C", [P, 2, 4, D], F32)
        ctxT = sb("ctxT", [P, WKEYS], F32)
        kparts = sb("kparts", [P, 3, WKEYS], BF16)
        krest = sb("krest", [P, WKEYS], F32)
        qparts = sb("qparts", [P, 3, S], BF16)
        qrest = sb("qrest", [P, S], F32)
        bn = sb("bn", [P, QT, 6], F32)
        mv = sb("mv", [P, QT, 2], F32)
        rstd = sb("rstd", [P, QT], F32)
        vareps = sb("vareps", [P, QT], F32)
        xn = sb("xn", [P, QT, D], F32)
        xnT = sb("xnT", [P, S], F32)
        valid = sb("valid", [P, 3, QT], F32)
        KSa = sb("KSa", [P, PAIRS * (SK + 3)], BF16)
        QS = sb("QS", [P, NSET, PAIRS, 2, S], BF16)
        VSf = sb("VSf", [P, NSET, 4, H * VCOL], F32)
        probs = sb("probs", [P, 8, 4 * S], F32)
        wmax = sb("wmax", [P, NWIN, QT, H], F32)
        rowmax = sb("rowmax", [P, QT, H], F32)
        mrest = sb("mrest", [P, 2, QT, H], F32)
        mparts = sb("mparts", [P, QT, 3, H], BF16)
        mT = sb("mT", [3 * H, S], BF16)
        OT = sb("OT", [P, S], F32)
        rsum = sb("rsum", [P, QT, 4], F32)
        O = sb("O", [P, QT, H, DK], F32)
        OCT = sb("OCT", [P, S], F32)
        bn2 = sb("bn2", [P, QT, 6], F32)
        mv2 = sb("mv2", [P, QT, 2], F32)
        rstd2 = sb("rstd2", [P, QT], F32)
        vareps2 = sb("vareps2", [P, QT], F32)
        rows = sb("rows", [P, 2, QT, ROW], F32)
        xn2T = sb("xn2T", [P, S], F32)
        logits = sb("logits", [P, QT, E], F32)
        top = sb("top", [P, QT, 8], F32)
        topi = sb("topi", [P, QT, 8], U32)
        topf = sb("topf", [P, QT, 2], F32)
        gap = sb("gap", [P, QT], F32)
        e2 = sb("e2", [P, QT], F32)
        den = sb("den", [P, QT], F32)
        rden = sb("rden", [P, QT], F32)
        hot = sb("hot", [P, QT, 2, E], F32)
        label = sb("label", [P, QT, E], BF16)
        before = sb("before", [P, 3, E], BF16)
        picked = sb("picked", [P, QT, 2, E], F32)
        place = sb("place", [P, QT, 2], F32)
        over = sb("over", [P, QT, 2], F32)
        first = sb("first", [P, QT, 2], F32)
        slot_i = sb("slot_i", [P, 2, QT, 2], I32)
        W1S = sb("W1S", [P, E, HID], F32)
        W2S = sb("W2S", [P, E, HID], F32)
        W3S = sb("W3S", [P, E, HK, D], F32)
        dispT = sb("dispT", [P, 2, CAP], F32)
        spare = sb("spare", [P, E, 3, 2], F32)
        slot_w = sb("slot_w", [P, E, 3], F32)
        slot_t = sb("slot_t", [P, E, 3], F32)
        slot_to = sb("slot_to", [P, E, 3], I32)

        KSp = [KSa[:, p * PAIRS * KPAD:(p + 1) * PAIRS * KPAD].rearrange("p (s k) -> p s k", s=PAIRS)
               for p in range(NSET)]
        KSg = KSa[:, :].rearrange("p (s k) -> p s k", s=PAIRS)
        VSg = [w[:, :, :].rearrange("p e n -> p (e n)").rearrange("p (t n) -> p t n", n=H * VCOL) for w in (W1S, W2S)]
        w3flat = W3S[:, :, :, :].rearrange("p e k n -> p (e k n)").bitcast(BF16)
        biasT = w3flat[:, 0:NT * S].rearrange("p (t q) -> p t q", t=NT)
        pflat = probs[:, :, :].rearrange("p s n -> p (s n)")
        maski = pflat[:, 0:QT * SK].bitcast(I32).rearrange("p (q k) -> p q k", q=QT)
        masked = W3S[:, :, :, :].rearrange("p e k n -> p (e k n)")[:, NT * S // 2:NT * S // 2 + WKEYS]
        disp = pflat[:, 0:E * 3 * ROW].rearrange("p (e c n) -> p e c n", e=E, c=3)
        o0 = E * 3 * ROW
        hT = pflat[:, o0:o0 + HK * CAP].rearrange("p (k n) -> p k n", k=HK)
        o1 = o0 + HK * CAP
        silu = pflat[:, o1:o1 + 2 * CAP].rearrange("p (b n) -> p b n", b=2)
        o2 = o1 + 2 * CAP
        orow = pflat[:, o2:o2 + 2 * 3 * D].rearrange("p (b c n) -> p b c n", b=2, c=3)
        o3 = o2 + 6 * D
        hT = [hT, pflat[:, o3:o3 + HK * CAP].rearrange("p (k n) -> p k n", k=HK)]
        assert o3 + HK * CAP <= 8 * 4 * S

        ps_s = [stack.enter_context(nc.psum_tensor(f"ps_s{i}", [P, 512], F32)) for i in range(2)]
        ps_t = [stack.enter_context(nc.psum_tensor(f"ps_t{i}", [P, 1024], F32)) for i in range(2)]
        ps_o = stack.enter_context(nc.psum_tensor("ps_o", [P, 512], F32))
        ps_m = stack.enter_context(nc.psum_tensor("ps_m", [P, 512], F32))

        s_w = sem("weights_loaded")
        s_mask = sem("mask_loaded")
        s_x = [sem(f"x_loaded{i}") for i in range(3)]
        s_ctx = [sem("ctx_loaded0"), sem("ctx_loaded1")]
        s_expw = sem("expert_weights_loaded")
        s_zero = sem("slots_zeroed")
        s_pre = sem("pool_setup")
        s_vpre = sem("vector_setup")
        s_attend = sem("attend_made")
        s_wT_ps = sem("weights_turned")
        s_wT = sem("weights_copied")
        s_col = sem("column_sums")
        s_stat = sem("mask_statistics")
        s_flag = sem("path_decided")
        s_kbias = sem("key_bias_made")
        s_kb = sem("key_bias_rows")
        s_tanh = sem("tanhs_made")
        s_fill = sem("stacks_filled")
        s_rowpat = sem("row_patterns_made")
        s_const = sem("stack_constants_written")
        s_vones = sem("v_buffers_cleared")
        s_gates = sem("small_tensors_loaded")
        s_rv = sem("rstd_of_valid_rows")
        s_ctxT_ps = sem("ctxT_in_psum")
        s_ctxT = sem("ctxT_copied")
        s_k_ps = sem("k_in_psum")
        s_k_hi = sem("k_high")
        s_k_r = sem("k_rest")
        s_k_mid = sem("k_middle")
        s_k_lo = sem("k_low")
        s_v_ps = sem("v_in_psum")
        s_v = sem("v_copied")
        s_ln = sem("ln_chain")
        s_rs = sem("rstd_chain")
        s_xn = sem("xn_made")
        s_xnT_ps = sem("xnT_in_psum")
        s_xnT = sem("xnT_copied")
        s_q_ps = sem("q_in_psum")
        s_q_hi = sem("q_high")
        s_q_r = sem("q_rest")
        s_q_mid = sem("q_middle")
        s_q_lo = sem("q_low")
        s_kd = sem("k_parts_in_dram")
        s_qd = sem("q_parts_in_dram")
        s_ks = [sem(f"k_stack_written{i}") for i in range(NWIN)]
        s_qs = [sem(f"q_stack_written{i}") for i in range(NSET)]
        s_sc = sem("scores_for_max")
        s_mx = sem("maxima_taken")
        s_mgen = sem("general_max_chain")
        s_mp = sem("max_parts_chain")
        s_mT_ps = sem("mT_in_psum")
        s_mT = sem("mT_copied")
        s_mr = sem("max_rows_written")
        s_st = sem("scores_for_exp")
        s_ex = sem("exp_done")
        s_pv = sem("pv_done")
        s_ot = sem("out_copied")
        s_oq = sem("out_turned")
        s_rsum = sem("sums_inverted")
        s_on = sem("out_normed")
        s_oc_ps = sem("outT_in_psum")
        s_oc = sem("outT_copied")
        s_y = sem("projected")
        s_x2 = sem("x2_made")
        s_x2out = sem("x2_stored")
        s_ln2 = sem("ln2_chain")
        s_rs2 = sem("rstd2_chain")
        s_xn2 = sem("xn2_made")
        s_xn2T_ps = sem("xn2T_in_psum")
        s_xn2T = sem("xn2T_copied")
        s_lg_ps = sem("logits_in_psum")
        s_lg = sem("logits_made")
        s_top = sem("top_values")
        s_topi = sem("top_indices")
        s_gap = sem("gap_made")
        s_e2 = sem("gap_exp")
        s_rden = sem("den_inverted")
        s_rt = sem("route_chain")
        s_seq = sem("seq_in_psum")
        s_pick = sem("place_picked")
        s_pickq = sem("first_tile_picked")
        s_place = sem("place_summed")
        s_scat = [sem("rows_scattered0"), sem("rows_scattered1")]
        s_disp = [sem(f"slots_loaded{e}") for e in range(E)]
        s_dT_ps = sem("dispT_in_psum")
        s_dT = sem("dispT_copied")
        s_h_ps = sem("h_in_psum")
        s_silu = sem("silu_done")
        s_h = sem("h_made")
        s_o_ps = sem("expert_out_in_psum")
        s_orow = sem("expert_rows")
        s_sw = sem("slot_chain")
        s_add = [sem("rows_added0"), sem("rows_added1")]
        s_gb = sem("general_bias_chain")
        s_gbq = sem("general_bias_first_tile")
        s_bT_ps = sem("biasT_in_psum")
        s_bT = sem("biasT_copied")
        s_vg = sem("general_v_cleared")
        s_settle = sem("nothing")

        class Path:

            def __init__(self, general):
                self.general = general
                self.windows = list(range(NWIN)) if general else [NWIN - 1]
                self.nw = len(self.windows)

            def set_of(self, b):
                return 0 if self.general else b % NSET

            def ks(self, b, i):
                return KSg[:, :, WIN * i:WIN * i + WKEYS] if self.general else KSp[b % NSET][:, :, 0:WKEYS]

            def vs(self, b, i, t):
                if not self.general:
                    return VSf[:, b % NSET, t, :]
                n = 4 * i + t
                return VSg[n // 8][:, n % 8, :]

            def depth(self, i, t):
                return TILE + (self.windows[i] == NWIN - 1 and t == 3)

        padded, general = Path(False), Path(True)
        block = stack.enter_context(nc.Block())

        def settle(eng):
            eng.sem_inc(s_settle, 1)

        def wait(eng, s, value):
            if not isinstance(value, int):
                eng.wait_ge(s, value)
                settle(eng)
            elif value > 0:
                eng.wait_ge(s, value)

        def x_pair(b):
            return X[:, 2 * b:2 * b + 2, :] if isinstance(b, int) else X[:, bass.ds(2 * b, 2), :]

        def end_of_batch(eng, b):
            wait(eng, s_scat[0], 64 * (b + 1))
            wait(eng, s_x2out, 16 * (b + 1))

        @block.sync
        def _(eng):
            eng.dma_start(maski, mask[0, 0].rearrange("(q p) k -> p q k", p=P)).then_inc(s_mask, 16)
            eng.dma_start(wraw[:, 1, :], w_k).then_inc(s_w, 16)
            eng.dma_start(wraw[:, 0, :], w_q).then_inc(s_w, 16)
            eng.dma_start(wraw[:, 2, :], w_v).then_inc(s_w, 16)
            eng.dma_start(wraw[:, 3, :], w_o).then_inc(s_w, 16)

            def load_ctx(path, b, i):
                n = b * path.nw + i
                cb = i % 2 if path.general else b % 2
                if path.general:
                    if i >= 2:
                        eng.wait_ge(s_ctxT_ps, n - 1)
                else:
                    wait(eng, s_ctxT_ps, n - 1)
                base = WIN * path.windows[i]
                eng.dma_start(C[0:TILE, cb, :, :], ctx[b, base:base + WIN, :].rearrange("(t k) d -> k t d", k=TILE))\
                   .then_inc(s_ctx[cb], 16)
                eng.dma_start(C[TILE:TILE + 1, cb, 3, :], ctx[b, base + WIN:base + WKEYS, :]).then_inc(s_ctx[cb], 16)

            def load_x():
                eng.dma_start(X[:, 2:4, :], x_tiles[:, 1]).then_inc(s_x[1], 16)
                eng.dma_start(X[:, 4:, :].rearrange("p (b q) d -> p b q d", q=QT), x_tiles[:, 2:]).then_inc(s_x[2], 16)

            def stack_k(path, b, i):
                n = b * path.nw + i
                st = path.set_of(b)
                eng.wait_ge(s_k_lo, n + 1)
                if path.general:
                    if i >= 1:
                        eng.wait_ge(s_ks[i - 1], 32 * (b + 1))
                else:
                    wait(eng, s_ks[st], 32 * (b // NSET))
                for r0, parts in ((0, 3), (3, 2), (5, 1)):
                    eng.dma_start(kspread[st, :, r0:r0 + parts, :], kparts[:, 0:parts, :]).then_inc(s_kd, 16)
                eng.wait_ge(s_kd, 48 * (n + 1))
                if not path.general:
                    wait(eng, s_st, H * (b - NSET + 1))
                dst = path.ks(b, i)
                src = kspread[st].rearrange("(s h d) n k -> h (d n) s k", h=2, d=DK)
                for hp in range(2):
                    eng.dma_start(dst[PROWS * hp:PROWS * (hp + 1), :, :], src[hp])\
                       .then_inc(s_ks[i if path.general else st], 16)

            def stack_q(path, b):
                st = path.set_of(b)
                eng.wait_ge(s_q_lo, b + 1)
                if not path.general:
                    wait(eng, s_qs[st], 32 * (b // NSET))
                for r0, parts, part in ((0, 3, 0), (3, 2, 1), (5, 1, 2)):
                    eng.dma_start(qspread[st, :, r0:r0 + parts, :],
                                  qparts[:, part:part + 1, :].broadcast_to([P, parts, S])).then_inc(s_qd, 16)
                eng.wait_ge(s_qd, 48 * (b + 1))
                if not path.general:
                    wait(eng, s_st, H * (b - NSET + 1))
                src = qspread[st].rearrange("(s h d) n k -> h (d n) s k", h=2, d=DK)
                for hp in range(2):
                    eng.dma_start(QS[PROWS * hp:PROWS * (hp + 1), st, :, hp, :], src[hp]).then_inc(s_qs[st], 16)

            def max_rows(path, b):
                st = path.set_of(b)
                eng.wait_ge(s_mT, b + 1)
                for c in range(3):
                    eng.dma_start(QS[MAX_ROW + c:MAX_ROW + c + 1, st, :, :, :].rearrange("c s h q -> c (s h) q"),
                                  mT[H * c:H * (c + 1), :]).then_inc(s_mr, 16)

            def store_x2(b):
                eng.wait_ge(s_x2, b + 1)
                eng.dma_start(out_tiles[:, b], x_pair(b)).then_inc(s_x2out, 16)

            def expert_weights(e):
                eng.dma_start(W1S[:, e, :], w1[e]).then_inc(s_expw, 16)
                eng.dma_start(W2S[:, e, :], w2[e]).then_inc(s_expw, 16)
                eng.dma_start(W3S[:, e, :, :], w3[e].rearrange("(k p) d -> p k d", p=P)).then_inc(s_expw, 16)

            def q_ones():
                eng.dma_start(QS[MASK_ROW:MAX_ROW].rearrange("c t s h q -> c (t s h) q"),
                              ones_row[0:1, 0:S].unsqueeze(1).broadcast_to([1, NSET * H, S])).then_inc(s_const, 16)

            eng.dma_start(X[:, 0:2, :], x_tiles[:, 0]).then_inc(s_x[0], 16)
            eng.wait_ge(s_flag, 1)
            fast = eng.value_load(flag[0:1, 0:1], min_val=0, max_val=1)
            with eng.If(fast == 1):
                load_ctx(padded, 0, 0)
                load_ctx(padded, 1, 0)
                load_x()
                eng.wait_ge(s_rowpat, 2)
                eng.wait_ge(s_fill, NSET)
                every = KSa[:, 0:NSET * PAIRS * KPAD].rearrange("p (s k) -> p s k", k=KPAD)
                eng.dma_start(every[MAX_ROW:SROWS], ones_row[0:3, :].unsqueeze(1).broadcast_to([3, NSET * PAIRS, KPAD]))\
                   .then_inc(s_const, 16)
                q_ones()
                eng.wait_ge(s_kbias, 1)
                eng.dma_start(every[MASK_ROW:MAX_ROW, :, 0:WKEYS],
                              keybias[:, :].unsqueeze(1).broadcast_to([1, NSET * PAIRS, WKEYS])).then_inc(s_const, 16)
                for b in range(2):
                    stack_k(padded, b, 0)
                    stack_q(padded, b)
                max_rows(padded, 0)
                load_ctx(padded, 2, 0)
                for b in range(B):
                    expert_weights(b)
                    if b + 3 < B:
                        load_ctx(padded, b + 3, 0)
                    if b + 2 < B:
                        stack_k(padded, b + 2, 0)
                        stack_q(padded, b + 2)
                    if b >= 1:
                        store_x2(b - 1)
                    if b + 1 < B:
                        max_rows(padded, b + 1)
                store_x2(B - 1)
            with eng.Else():
                load_x()
                eng.wait_ge(s_rowpat, 2)
                eng.wait_ge(s_fill, NSET)
                quarters = KSa[:, :].rearrange("p (s k) -> p s k", k=(SK + 3) // 4)
                quarter = (SK + 3) // 4
                eng.dma_start(quarters[MAX_ROW:SROWS], ones_row[0:3, 0:quarter].unsqueeze(1)
                              .broadcast_to([3, 4 * PAIRS, quarter])).then_inc(s_const, 16)
                q_ones()
                eng.dma_start(quarters[MASK_ROW:MAX_ROW], zero_row[:, 0:quarter].unsqueeze(1)
                              .broadcast_to([1, 4 * PAIRS, quarter])).then_inc(s_const, 16)
                with eng.Fori(0, B) as b:
                    load_ctx(general, b, 0)
                    load_ctx(general, b, 1)
                    for i in range(NWIN):
                        stack_k(general, b, i)
                        if i + 2 < NWIN:
                            load_ctx(general, b, i + 2)
                    stack_q(general, b)
                    max_rows(general, b)
                    store_x2(b)
                    end_of_batch(eng, b)
                for e in range(E):
                    expert_weights(e)
            with eng.If(fast == 1):
                eng.wait_ge(s_scat[0], 32 * B)
                eng.wait_ge(s_scat[1], 32 * B)
            with eng.Else():
                eng.wait_ge(s_scat[0], 64 * B)
            for e in range(E):
                eng.dma_start(disp[:, e, 0:2, :], slots[CAP * e:CAP * e + 256, :].rearrange("(c p) n -> p c n", p=P))\
                   .then_inc(s_disp[e], 16)
                eng.dma_start(disp[0:64, e, 2, :], slots[CAP * e + 256:CAP * (e + 1), :]).then_inc(s_disp[e], 16)
            eng.wait_ge(s_add[0], 24 * E)
            eng.wait_ge(s_add[1], 24 * E)
            eng.wait_ge(s_zero, 16)
            eng.wait_ge(s_x2out, 16 * B)

        @block.gpsimd
        def _(eng):
            setup = Chain(eng, s_pre, 11).at(0)
            setup.next(eng.memset(ident[:, :], 0.0))
            setup.next(eng.affine_select(out=ident[:, :], in_=ident[:, :], compare_op=ALU.not_equal, fill=1.0,
                                         base=0, pattern=[[-1, P]], channel_multiplier=1))
            setup.next(eng.memset(onesb[:, :], 1.0))
            setup.next(eng.tensor_copy(identb[:, :], ident[:, :]))
            setup.next(eng.affine_select(out=tri[:, :], in_=onesb[:, :], compare_op=ALU.is_ge, fill=0.0,
                                         base=0, pattern=[[1, P]], channel_multiplier=-1))
            setup.next(eng.iota(iota8i[:, :], pattern=[[1, E]], base=0, channel_multiplier=0))
            setup.next(eng.tensor_copy(iota8[:, :], iota8i[:, :]))
            setup.next(eng.iota(tok_i[:, :], pattern=[[P, NTT]], base=1, channel_multiplier=1))
            setup.next(eng.tensor_copy(tok[:, :], tok_i[:, :]))
            setup.next(eng.memset(halfpow[:, :], -0.5))
            setup.next(eng.memset(before[:, :, :], 0.0))
            setup.end()
            for st in range(NSET):
                eng.memset(VSf[:, st, :, :], 0.0).then_inc(s_vones, 1)
            eng.wait_ge(s_vones, NSET)
            for st in range(NSET):
                eng.memset(VSf[:, st, :, :].rearrange("p t (h c) -> p (t h) c", c=VCOL)[:, :, DK:DK + 1], 1.0)\
                   .then_inc(s_vones, 1)

            rs_chain = Chain(eng, s_rs, 2, wait)
            mp_chain = Chain(eng, s_mp, 6, wait)
            rs2_chain = Chain(eng, s_rs2, 2, wait)
            rt_chain = Chain(eng, s_rt, 19, wait)

            def rstd_of(b):
                wait(eng, s_ln, 4 * (b + 1))
                if isinstance(b, int):
                    wait(eng, s_xn, 2 * b)
                c = rs_chain.at(b)
                c.next(eng.tensor_scalar(vareps[:, :], mv[:, :, 1], EPS, None, ALU.add))
                c.next(eng.tensor_tensor(rstd[:, :], vareps[:, :], halfpow[:, :], ALU.pow))

            def split_k(path, b, i):
                n = b * path.nw + i
                wait(eng, s_k_r, n + 1)
                if i >= 1 or not path.general:
                    wait(eng, s_kd, 48 * n)
                eng.tensor_copy(kparts[:, 1, :], krest[:, :]).then_inc(s_k_mid, 1)
                wait(eng, s_k_mid, n + 1)
                eng.tensor_tensor(kparts[:, 2, :], krest[:, :], kparts[:, 1, :], ALU.subtract).then_inc(s_k_lo, 1)

            def split_q(path, b):
                wait(eng, s_q_r, b + 1)
                if not path.general:
                    wait(eng, s_qd, 48 * b)
                eng.tensor_copy(qparts[:, 1, :], qrest[:, :]).then_inc(s_q_mid, 1)
                wait(eng, s_q_mid, b + 1)
                eng.tensor_tensor(qparts[:, 2, :], qrest[:, :], qparts[:, 1, :], ALU.subtract).then_inc(s_q_lo, 1)

            def max_parts(path, b):
                if path.general:
                    wait(eng, s_mgen, (2 * 2 * H * NWIN + 1) * (b + 1))
                else:
                    eng.wait_ge(s_mx, 2 * H * (b + 1))
                    wait(eng, s_mT_ps, b)
                c = mp_chain.at(b)
                src = rowmax[:, :, :] if path.general else wmax[:, b % 2, :, :]
                c.next(eng.tensor_scalar(mrest[:, 0], src, -1.0, None, ALU.mult))
                c.next(eng.tensor_copy(mparts[:, :, 0, :], mrest[:, 0]))
                c.next(eng.tensor_tensor(mrest[:, 1], mrest[:, 0], mparts[:, :, 0, :], ALU.subtract))
                c.next(eng.tensor_copy(mparts[:, :, 1, :], mrest[:, 1]))
                c.next(eng.tensor_tensor(mrest[:, 0], mrest[:, 1], mparts[:, :, 1, :], ALU.subtract))
                c.next(eng.tensor_copy(mparts[:, :, 2, :], mrest[:, 0]))
                c.end()

            def rstd2_of(b):
                wait(eng, s_ln2, 4 * (b + 1))
                c = rs2_chain.at(b)
                c.next(eng.tensor_scalar(vareps2[:, :], mv2[:, :, 1], EPS, None, ALU.add))
                c.next(eng.tensor_tensor(rstd2[:, :], vareps2[:, :], halfpow[:, :], ALU.pow))

            def route_labels(b, p):
                row = rows[:, p, :, :]
                wait(eng, s_topi, 2 * (b + 1))
                if isinstance(b, int):
                    wait(eng, s_e2, b)
                eng.tensor_tensor(gap[:, :], top[:, :, 1], top[:, :, 0], ALU.subtract).then_inc(s_gap, 1)
                c = rt_chain.at(b)
                c.next(eng.tensor_copy(topf[:, :, :], topi[:, :, 0:2]))
                for q in range(QT):
                    for k in range(2):
                        c.next(eng.tensor_scalar(hot[:, q, k, :], iota8[:, :], topf[:, q, k:k + 1], None, ALU.is_equal))
                c.next(eng.tensor_tensor(label[:, :, :], hot[:, :, 0, :], hot[:, :, 1, :], ALU.add))
                c.next(eng.tensor_tensor(before[:, 1, :], before[:, 0, :], label[:, 0, :], ALU.add))
                c.next(eng.tensor_tensor(before[:, 2, :], before[:, 1, :], label[:, 1, :], ALU.add))
                wait(eng, s_e2, b + 1)
                c.next(eng.tensor_scalar(den[:, :], e2[:, :], 1.0, None, ALU.add))
                wait(eng, s_rden, b + 1)
                if isinstance(b, int):
                    wait(eng, s_scat[p], 64 * (b // 2))
                c.next(eng.tensor_scalar(row[:, :, D + 1], rden[:, :], tanhs[:, 1:2], None, ALU.mult))
                c.next(eng.tensor_tensor(row[:, :, D + 2], row[:, :, D + 1], e2[:, :], ALU.mult))
                c.next(eng.tensor_copy(row[:, :, D + 3], topf[:, :, 0]))
                c.next(eng.tensor_copy(row[:, :, D], tok[:, 2 * b:2 * b + 2] if isinstance(b, int)
                                       else tok[:, bass.ds(2 * b, 2)]))
                return c

            def scatter(b, p, c):
                row = rows[:, p, :, :]
                wait(eng, s_place, b + 1)
                c.next(eng.tensor_copy(before[:, 0, :], before[:, 2, :]))
                c.next(eng.tensor_scalar(over[:, :, :], place[:, :, :], float(CAP), SKIP, ALU.is_gt, ALU.mult))
                c.next(eng.tensor_scalar(first[:, :, :], topf[:, :, :], float(CAP), -1.0, ALU.mult, ALU.add))
                c.next(eng.tensor_tensor(first[:, :, :], over[:, :, :], first[:, :, :], ALU.add))
                c.next(eng.tensor_tensor(first[:, :, :], first[:, :, :], place[:, :, :], ALU.add))
                c.next(eng.tensor_copy(slot_i[:, p, :, :], first[:, :, :]))
                c.end()
                for q in range(QT):
                    for k in range(2):
                        eng.indirect_dma_start(slots[:, :], bass.IndirectOffsetOnAxis(ap=slot_i[:, p, q, k:k + 1], axis=0),
                                               row[:, q, :], None, bounds_check=E * CAP - 1, oob_is_err=False)\
                           .then_inc(s_scat[p], 16)

            eng.wait_ge(s_tanh, 1)
            eng.wait_ge(s_zero, 16)
            eng.wait_ge(s_flag, 1)
            fast = eng.value_load(flag[0:1, 0:1], min_val=0, max_val=1)
            with eng.If(fast == 1):
                for b in range(2):
                    rstd_of(b)
                    split_k(padded, b, 0)
                    split_q(padded, b)
                max_parts(padded, 0)
                c = None
                for b in range(B):
                    if b + 2 < B:
                        rstd_of(b + 2)
                        split_k(padded, b + 2, 0)
                    if b >= 2:
                        scatter(b - 2, b % 2, c)
                    if b >= 1:
                        rstd2_of(b - 1)
                    if b + 2 < B:
                        split_q(padded, b + 2)
                    if b + 1 < B:
                        max_parts(padded, b + 1)
                    if b >= 1:
                        c = route_labels(b - 1, (b - 1) % 2)
                scatter(B - 2, B % 2, c)
                rstd2_of(B - 1)
                scatter(B - 1, (B - 1) % 2, route_labels(B - 1, (B - 1) % 2))
            with eng.Else():
                eng.memset(VSg[0], 0.0).then_inc(s_vg, 1)
                eng.memset(VSg[1], 0.0).then_inc(s_vg, 1)
                eng.wait_ge(s_vg, 2)
                for g in range(2):
                    eng.memset(VSg[g].rearrange("p t (h c) -> p (t h) c", c=VCOL)[:, :, DK:DK + 1], 1.0).then_inc(s_vg, 1)
                with eng.Fori(0, B) as b:
                    rstd_of(b)
                    for i in range(NWIN):
                        split_k(general, b, i)
                    split_q(general, b)
                    max_parts(general, b)
                    rstd2_of(b)
                    scatter(b, 0, route_labels(b, 0))
                    end_of_batch(eng, b)

            sw_chain = Chain(eng, s_sw, 14)
            for e in range(E):
                eng.wait_ge(s_disp[e], 32)
                c = sw_chain.at(e)
                for n, cs in ((P, slice(0, 2)), (64, slice(2, 3))):
                    number, first_w, second_w, first_e = (disp[0:n, e, cs, D + k] for k in range(4))
                    to, wt, is_first = slot_t[0:n, e, cs], slot_w[0:n, e, cs], spare[0:n, e, cs, 0]
                    c.next(eng.tensor_scalar(to, number, 0.0, SKIP, ALU.is_equal, ALU.mult))
                    c.next(eng.tensor_tensor(to, to, number, ALU.add))
                    c.next(eng.tensor_scalar(slot_to[0:n, e, cs], to, -1.0, None, ALU.add))
                    c.next(eng.tensor_scalar(is_first, first_e, float(e), None, ALU.is_equal))
                    c.next(eng.tensor_tensor(wt, first_w, second_w, ALU.subtract))
                    c.next(eng.tensor_tensor(wt, wt, is_first, ALU.mult))
                    c.next(eng.tensor_tensor(wt, wt, second_w, ALU.add))
                c.end()
            eng.wait_ge(s_x2out, 16 * B)
            for e in range(E):
                eng.wait_ge(s_orow, 3 * (e + 1))
                if e >= 1:
                    eng.wait_ge(s_add[(e - 1) % 2], 48 * ((e + 1) // 2))
                for k, (_, n) in enumerate(CT):
                    eng.indirect_dma_start(out_rows, bass.IndirectOffsetOnAxis(ap=slot_to[0:n, e, k:k + 1], axis=0),
                                           orow[0:n, e % 2, k, :], None, bounds_check=T - 1, oob_is_err=False,
                                           compute_op=ALU.add).then_inc(s_add[e % 2], 16)

        @block.scalar
        def _(eng):
            eng.dma_start(gates[:, 0:1], g_xattn.rearrange("(a n) -> a n", a=1).broadcast_to([P, 1])).then_inc(s_gates, 16)
            eng.dma_start(gates[:, 1:2], g_ffn.rearrange("(a n) -> a n", a=1).broadcast_to([P, 1])).then_inc(s_gates, 16)
            eng.dma_start(wg[:, :], w_g).then_inc(s_gates, 16)
            for q in range(QT):
                eng.dma_start(bg[:, q, :], b_g.rearrange("(a n) -> a n", a=1).broadcast_to([P, E])).then_inc(s_gates, 16)
            eng.wait_ge(s_vpre, 1)
            eng.dma_start(slots.rearrange("(p r) n -> p r n", p=P),
                          zrow[:, :].unsqueeze(1).broadcast_to([P, E * CAP // P, ROW])).then_inc(s_zero, 16)
            eng.wait_ge(s_gates, 80)
            eng.activation(tanhs[:, :], gates[:, :], ACT.Tanh).then_inc(s_tanh, 1)

            def copy_ctxT(path, b, i):
                n = b * path.nw + i
                eng.wait_ge(s_ctxT_ps, n + 1)
                if i >= 1 or not path.general:
                    wait(eng, s_v_ps, n)
                eng.activation(ctxT[:, :], ps_m[:, 0:WKEYS], ACT.Copy).then_inc(s_ctxT, 1)

            def high_k(path, b, i):
                n = b * path.nw + i
                eng.wait_ge(s_k_ps, n + 1)
                if i >= 1 or not path.general:
                    wait(eng, s_kd, 48 * n)
                eng.activation(kparts[:, 0, :], ps_m[:, 0:WKEYS], ACT.Copy).then_inc(s_k_hi, 1)

            def copy_xnT(b):
                eng.wait_ge(s_xnT_ps, b + 1)
                eng.activation(xnT[:, :], ps_m[:, 0:S], ACT.Copy).then_inc(s_xnT, 1)

            def copy_v(path, b, i):
                n = b * path.nw + i
                eng.wait_ge(s_v_ps, n + 1)
                if path.general:
                    eng.wait_ge(s_vg, 4)
                    g = 4 * i
                    dst = VSg[g // 8][:, g % 8:g % 8 + 4, :]
                else:
                    if b < NSET:
                        eng.wait_ge(s_vones, 2 * NSET)
                    wait(eng, s_pv, 4 * (b - NSET + 1))
                    dst = VSf[:, b % NSET, :, :]
                dst = dst.rearrange("p t (h c) -> p (t h) c", c=VCOL)[0:TILE + 1, :, 0:DK]
                src = ps_m[0:TILE + 1, :].rearrange("p (n c) -> p n c", c=DK)
                eng.activation(dst, src, ACT.Copy).then_inc(s_v, 1)

            def high_q(path, b):
                eng.wait_ge(s_q_ps, b + 1)
                if not path.general:
                    wait(eng, s_qd, 48 * b)
                eng.activation(qparts[:, 0, :], ps_m[:, 0:S], ACT.Copy).then_inc(s_q_hi, 1)

            def copy_mT(path, b):
                eng.wait_ge(s_mT_ps, b + 1)
                if not path.general:
                    wait(eng, s_mr, 48 * b)
                eng.activation(mT[:, :], ps_m[0:3 * H, 0:S // 2].bitcast(BF16), ACT.Copy).then_inc(s_mT, 1)

            def exp(path, b, r, j):
                n = 16 * path.nw * b + 4 * r + j
                eng.wait_ge(s_st, n + 1)
                if r >= 2 or not path.general:
                    wait(eng, s_pv, 4 * path.nw * b + r - 1)
                eng.activation(probs[0:TILE + 1, (4 * r + j) % 8, :], ps_t[(4 * r + j) % 2][0:TILE + 1, :], ACT.Exp,
                               scale=SCALE).then_inc(s_ex, 1)

            def copy_o(path, b, u):
                eng.wait_ge(s_pv, path.nw * (4 * b + u + 1))
                if u >= 1 or not path.general:
                    wait(eng, s_oq, 4 * b + u)
                eng.activation(OT[:, :], ps_o[:, 0:S], ACT.Copy).then_inc(s_ot, 1)

            def copy_oc(b):
                eng.wait_ge(s_oc_ps, b + 1)
                eng.activation(OCT[:, :], ps_m[:, 0:S], ACT.Copy).then_inc(s_oc, 1)

            def copy_xn2T(b):
                eng.wait_ge(s_xn2T_ps, b + 1)
                eng.activation(xn2T[:, :], ps_m[:, 0:S], ACT.Copy).then_inc(s_xn2T, 1)

            def exp_gap(b):
                eng.wait_ge(s_gap, b + 1)
                if isinstance(b, int):
                    wait(eng, s_rt, 19 * b)
                eng.activation(e2[:, :], gap[:, :], ACT.Exp).then_inc(s_e2, 1)

            eng.wait_ge(s_flag, 1)
            fast = eng.value_load(flag[0:1, 0:1], min_val=0, max_val=1)
            with eng.If(fast == 1):
                for b in range(2):
                    copy_ctxT(padded, b, 0)
                    high_k(padded, b, 0)
                    copy_xnT(b)
                    copy_v(padded, b, 0)
                    high_q(padded, b)
                copy_mT(padded, 0)
                for b in range(B):
                    ahead = b + 2 < B
                    for h in range(H):
                        if h == 1 and ahead:
                            copy_ctxT(padded, b + 2, 0)
                        if h == 2 and ahead:
                            high_k(padded, b + 2, 0)
                        if h == 2 and b >= 1:
                            copy_o(padded, b - 1, 3)
                        if h == 5 and ahead:
                            copy_v(padded, b + 2, 0)
                        if h == 6 and b >= 1:
                            copy_oc(b - 1)
                        if h == 7 and ahead:
                            copy_xnT(b + 2)
                        if h == 9 and ahead:
                            high_q(padded, b + 2)
                        if h == 11 and b >= 1:
                            copy_xn2T(b - 1)
                        if h == 14 and b + 1 < B:
                            copy_mT(padded, b + 1)
                        if h in (6, 10, 14):
                            copy_o(padded, b, h // 4 - 1)
                        exp(padded, b, h // 4, h % 4)
                    if b >= 1:
                        exp_gap(b - 1)
                copy_o(padded, B - 1, 3)
                copy_oc(B - 1)
                copy_xn2T(B - 1)
                exp_gap(B - 1)
            with eng.Else():
                for t in range(0, NT, 4):
                    eng.wait_ge(s_bT_ps, t // 4 + 1)
                    eng.activation(biasT[0:TILE + 1, t:t + 4, :].rearrange("p t q -> p (t q)"),
                                   ps_m[0:TILE + 1, :].bitcast(BF16), ACT.Copy).then_inc(s_bT, 1)
                with eng.Fori(0, B) as b:
                    for i in range(NWIN):
                        copy_ctxT(general, b, i)
                        high_k(general, b, i)
                        copy_v(general, b, i)
                    copy_xnT(b)
                    high_q(general, b)
                    copy_mT(general, b)
                    for u in range(4):
                        for i in range(NWIN):
                            for j in range(4):
                                exp(general, b, NWIN * u + i, j)
                        copy_o(general, b, u)
                    copy_oc(b)
                    copy_xn2T(b)
                    exp_gap(b)
                    end_of_batch(eng, b)

            def silu_of(e, k):
                n = HK * e + k
                eng.wait_ge(s_h_ps, n + 1)
                wait(eng, s_h, n - 1)
                eng.activation(silu[:, n % 2, :], ps_t[n % 2][:, 0:CAP], ACT.Silu).then_inc(s_silu, 1)

            def weighted_rows(e):
                eng.wait_ge(s_o_ps, e + 1)
                eng.wait_ge(s_sw, 14 * (e + 1))
                wait(eng, s_add[e % 2], 48 * (e // 2))
                for k, (_, n) in enumerate(CT):
                    eng.activation(orow[0:n, e % 2, k, :], ps_s[e % 2][0:n, D * k:D * (k + 1)], ACT.Copy,
                                   scale=slot_w[0:n, e, k:k + 1]).then_inc(s_orow, 1)

            for e in range(E):
                for k in range(HK):
                    silu_of(e, k)
                    if k == 1 and e >= 1:
                        weighted_rows(e - 1)
            weighted_rows(E - 1)

        @block.tensor
        def _(eng):
            eng.wait_ge(s_pre, 5)
            eng.wait_ge(s_w, 64)
            for n in range(4):
                ins = eng.transpose(ps_m[:, D * n:D * (n + 1)], wraw[:, n, :], ident[:, :])
            ins.then_inc(s_wT_ps, 1)
            eng.wait_ge(s_attend, 1)
            for q in range(QT):
                eng.matmul(ps_s[0][0:1, 0:WKEYS], onesb[:, 0:1], attend[:, q, SK - WKEYS:SK],
                           start=(q == 0), stop=(q == QT - 1)).then_inc(s_col, 1)
            for n in range(QT * (NWIN - 1)):
                q, w = n % QT, n // QT
                eng.matmul(ps_s[1][0:1, 0:WIN], onesb[:, 0:1], attend[:, q, WIN * w:WIN * (w + 1)],
                           start=(n == 0), stop=(n == QT * (NWIN - 1) - 1)).then_inc(s_col, 1)

            def turn_ctx(path, b, i, free):
                wait(eng, *free)
                if path.general:
                    eng.wait_ge(s_ctx[i % 2], 32 * (2 * b + i // 2 + 1))
                    cb = i % 2
                else:
                    eng.wait_ge(s_ctx[b % 2], 32 * (b // 2 + 1))
                    cb = b % 2
                for t in range(4):
                    n = TILE + (t == 3)
                    ins = eng.transpose(ps_m[:, TILE * t:TILE * t + n], C[0:n, cb, t, :], ident[0:n, 0:n])
                ins.then_inc(s_ctxT_ps, 1)

            def project_k(path, b, i):
                eng.wait_ge(s_ctxT, b * path.nw + i + 1)
                eng.matmul(ps_m[:, 0:WKEYS], wT[:, 1, :], ctxT[:, :], start=True, stop=True).then_inc(s_k_ps, 1)

            def turn_xn(b, free):
                wait(eng, *free)
                eng.wait_ge(s_xn, 2 * (b + 1))
                for q in range(QT):
                    ins = eng.transpose(ps_m[:, P * q:P * (q + 1)], xn[:, q, :], ident[:, :])
                ins.then_inc(s_xnT_ps, 1)

            def project_v(path, b, i, free):
                wait(eng, *free)
                eng.wait_ge(s_ctxT, b * path.nw + i + 1)
                for t in range(4):
                    ins = eng.matmul(ps_m[0:TILE + 1, D * t:D * (t + 1)], ctxT[:, TILE * t:TILE * t + TILE + 1],
                                     wT[:, 2, :], start=True, stop=True)
                ins.then_inc(s_v_ps, 1)

            def project_q(b, free):
                wait(eng, *free)
                eng.wait_ge(s_xnT, b + 1)
                eng.matmul(ps_m[:, 0:S], wT[:, 0, :], xnT[:, :], start=True, stop=True).then_inc(s_q_ps, 1)

            def score_for_max(path, b, k):
                i, h, q = k // (2 * H), k // 2 % H, k % 2
                n = 2 * H * path.nw * b + k
                if k % (2 * H) == 0:
                    if path.general:
                        eng.wait_ge(s_ks[i], 32 * (b + 1))
                    else:
                        eng.wait_ge(s_ks[b % NSET], 32 * (b // NSET + 1))
                if k == 0:
                    if path.general:
                        eng.wait_ge(s_qs[0], 32 * (b + 1))
                    else:
                        eng.wait_ge(s_qs[b % NSET], 32 * (b // NSET + 1))
                    eng.wait_ge(s_const, 48)
                if not path.general:
                    wait(eng, s_mx, n - 1)
                elif k >= 2:
                    eng.wait_ge(s_mgen, 257 * b + 2 * (k - 2) + 1)
                eng.matmul(ps_s[k % 2][:, 0:WKEYS], QS[0:MAX_ROW, path.set_of(b), h // 2, h % 2, P * q:P * (q + 1)],
                           path.ks(b, i)[0:MAX_ROW, h // 2, :], start=True, stop=True).then_inc(s_sc, 1)

            def turn_max(b, free):
                wait(eng, *free)
                wait(eng, s_mp, 6 * (b + 1))
                dst = ps_m[0:3 * H, 0:S // 2].bitcast(BF16)
                for q in range(QT):
                    ins = eng.transpose(dst[:, P * q:P * (q + 1)], mparts[:, q, :, :].rearrange("p c h -> p (c h)"), identb[:, :])
                ins.then_inc(s_mT_ps, 1)

            def score_for_exp(path, b, r, j):
                u, i = r // path.nw, r % path.nw
                h, k = 4 * u + j, 4 * r + j
                n = 16 * path.nw * b + k
                if k == 0:
                    eng.wait_ge(s_mr, 48 * (b + 1))
                if k >= 2 or not path.general:
                    wait(eng, s_ex, n - 1)
                dst, st = ps_t[k % 2], path.set_of(b)
                for t in range(4):
                    ins = eng.matmul(dst[0:TILE + 1, S * t:S * (t + 1)],
                                     path.ks(b, i)[0:SROWS, h // 2, TILE * t:TILE * t + TILE + 1],
                                     QS[0:SROWS, st, h // 2, h % 2, :], start=True, stop=not path.general)
                    if path.general:
                        ins = eng.matmul(dst[0:TILE + 1, S * t:S * (t + 1)], identb[0:TILE + 1, 0:TILE + 1],
                                         biasT[0:TILE + 1, 4 * i + t, :], start=False, stop=True)
                ins.then_inc(s_st, 1)

            def weigh_v(path, b, r):
                u, i = r // path.nw, r % path.nw
                eng.wait_ge(s_ex, path.nw * 16 * b + 4 * r + 4)
                if u == 0 and i == 0:
                    eng.wait_ge(s_v, path.nw * (b + 1))
                if i == 0 and (u >= 1 or not path.general):
                    wait(eng, s_ot, 4 * b + u)
                for t in range(4):
                    d = path.depth(i, t)
                    for j in range(4):
                        h = 4 * u + j
                        ins = eng.matmul(ps_o[VCOL * j:VCOL * (j + 1), 0:S],
                                         path.vs(b, i, t)[0:d, VCOL * h:VCOL * (h + 1)],
                                         probs[0:d, (4 * r + j) % 8, S * t:S * (t + 1)],
                                         start=(i == 0 and t == 0), stop=(i == path.nw - 1 and t == 3))
                ins.then_inc(s_pv, 1)

            def turn_out(b, u, free):
                wait(eng, *free)
                eng.wait_ge(s_ot, 4 * b + u + 1)
                for q in range(QT):
                    ins = eng.transpose(ps_m[:, P * q:P * (q + 1)], OT[:, P * q:P * (q + 1)], ident[:, :])
                ins.then_inc(s_oq, 1)

            def turn_normed(b, free):
                wait(eng, *free)
                eng.wait_ge(s_on, 4 * (b + 1))
                for q in range(QT):
                    ins = eng.transpose(ps_m[:, P * q:P * (q + 1)], O[:, q, :, :].rearrange("p h d -> p (h d)"), ident[:, :])
                ins.then_inc(s_oc_ps, 1)

            def project_out(b, free):
                wait(eng, *free)
                eng.wait_ge(s_oc, b + 1)
                for q in range(QT):
                    ins = eng.matmul(ps_m[:, D * q:D * (q + 1)], OCT[:, P * q:P * (q + 1)], wT[:, 3, :], start=True, stop=True)
                ins.then_inc(s_y, 1)

            def turn_xn2(b, p, free):
                wait(eng, *free)
                eng.wait_ge(s_xn2, 2 * (b + 1))
                for q in range(QT):
                    ins = eng.transpose(ps_m[:, P * q:P * (q + 1)], rows[:, p, q, 0:D], ident[:, :])
                ins.then_inc(s_xn2T_ps, 1)

            def make_logits(b, free):
                wait(eng, *free)
                eng.wait_ge(s_xn2T, b + 1)
                for q in range(QT):
                    ins = eng.matmul(ps_m[:, E * q:E * (q + 1)], xn2T[:, P * q:P * (q + 1)], wg[:, :], start=True, stop=True)
                ins.then_inc(s_lg_ps, 1)

            def number_tokens(b, free):
                wait(eng, *free)
                eng.wait_ge(s_rt, 19 * b + 8)
                both = QT * E
                eng.matmul(ps_m[:, 0:both], tri[:, :], label[:, :, :].rearrange("p q e -> p (q e)"), start=True, stop=False)
                eng.matmul(ps_m[:, 0:both], onesb[:, :], before[:, 0:QT, :].rearrange("p q e -> p (q e)"),
                           start=False, stop=True).then_inc(s_seq, 1)

            eng.wait_ge(s_wT, 2)
            eng.wait_ge(s_gates, 80)
            eng.wait_ge(s_flag, 1)
            fast = eng.value_load(flag[0:1, 0:1], min_val=0, max_val=1)
            with eng.If(fast == 1):
                for b in range(2):
                    turn_ctx(padded, b, 0, (s_q_r, b))
                    project_k(padded, b, 0)
                    turn_xn(b, (s_k_r, b + 1))
                    project_v(padded, b, 0, (s_xnT, b + 1))
                    project_q(b, (s_v, b + 1))
                for k in range(2 * H):
                    score_for_max(padded, 0, k)
                turn_max(0, (s_q_r, 2))
                for b in range(B):
                    left = list(range(2 * H)) if b + 1 < B else []
                    ahead = b + 2 < B
                    for h in range(H):
                        score_for_exp(padded, b, h // 4, h % 4)
                        for k in left[3 * h:3 * h + 1]:
                            score_for_max(padded, b + 1, k)
                        if h == 0 and ahead:
                            turn_ctx(padded, b + 2, 0, (s_on, 4 * b - 1) if b else (s_mT, 1))
                        if h == 1 and ahead:
                            project_k(padded, b + 2, 0)
                        if h == 2 and b >= 2:
                            number_tokens(b - 2, (s_k_r, b + 3) if ahead else (s_on, 4 * b - 1))
                        if h == 3 and b >= 1:
                            turn_out(b - 1, 3, (s_pick, b - 1) if b >= 2 else (s_k_r, b + 3))
                        if h == 4 and ahead:
                            project_v(padded, b + 2, 0, (s_on, 4 * b) if b else (s_k_r, 3))
                        if h == 5 and b >= 1:
                            turn_normed(b - 1, (s_v, b + 3) if ahead else (s_on, 4 * b))
                        if h == 6 and ahead:
                            turn_xn(b + 2, (s_oc, b) if b else (s_v, 3))
                        if h == 7 and b >= 1:
                            project_out(b - 1, (s_xnT, b + 3) if ahead else (s_oc, b))
                        if h == 8 and ahead:
                            project_q(b + 2, (s_x2, b))
                        if h == 9:
                            turn_out(b, 0, (s_q_r, b + 3) if ahead else (s_x2, b))
                        if h == 10 and b >= 1:
                            turn_xn2(b - 1, (b - 1) % 2, (s_on, 4 * b + 1))
                        if h == 11:
                            turn_out(b, 1, (s_xn2T, b) if b else (s_on, 1))
                        if h == 12 and b >= 1:
                            make_logits(b - 1, (s_on, 4 * b + 2))
                        if h == 13 and b + 1 < B:
                            turn_max(b + 1, (s_lg, b) if b else (s_on, 2))
                        if h == 15:
                            turn_out(b, 2, (s_mT, b + 2) if b + 1 < B else (s_lg, b))
                        if h % 4 == 1 and h >= 5:
                            weigh_v(padded, b, h // 4 - 1)
                        if h == 1 and b >= 1:
                            weigh_v(padded, b - 1, 3)
                        for k in left[3 * h + 1:3 * h + 3]:
                            score_for_max(padded, b + 1, k)
                weigh_v(padded, B - 1, 3)
                number_tokens(B - 2, (s_on, 4 * B - 1))
                turn_out(B - 1, 3, (s_pick, B - 1))
                turn_normed(B - 1, (s_on, 4 * B))
                project_out(B - 1, (s_oc, B))
                turn_xn2(B - 1, (B - 1) % 2, (s_x2, B))
                make_logits(B - 1, (s_xn2T, B))
                number_tokens(B - 1, (s_lg, B))
            with eng.Else():
                eng.wait_ge(s_gb, 4)
                for t in range(NT):
                    if t % 4 == 0 and t:
                        eng.wait_ge(s_bT, t // 4)
                    for q in range(QT):
                        ins = eng.transpose(ps_m[0:TILE + 1, :].bitcast(BF16)[:, S * (t % 4) + P * q:S * (t % 4) + P * (q + 1)],
                                            attend[:, q, TILE * t:TILE * t + TILE + 1], identb[:, :])
                    if t % 4 == 3:
                        ins.then_inc(s_bT_ps, 1)
                eng.wait_ge(s_bT, 4)
                with eng.Fori(0, B) as b:
                    for i in range(NWIN):
                        turn_ctx(general, b, i, (s_v, NWIN * b + i) if i else (s_bT, 4))
                        project_k(general, b, i)
                        project_v(general, b, i, (s_k_r, NWIN * b + i + 1))
                    turn_xn(b, (s_v, NWIN * (b + 1)))
                    project_q(b, (s_xnT, b + 1))
                    for k in range(2 * H * NWIN):
                        score_for_max(general, b, k)
                    turn_max(b, (s_q_r, b + 1))
                    for u in range(4):
                        for i in range(NWIN):
                            for j in range(4):
                                score_for_exp(general, b, NWIN * u + i, j)
                            weigh_v(general, b, NWIN * u + i)
                        turn_out(b, u, (s_on, 4 * b + u) if u else (s_mT, b + 1))
                    turn_normed(b, (s_on, 4 * b + 4))
                    project_out(b, (s_oc, b + 1))
                    turn_xn2(b, 0, (s_x2, b + 1))
                    make_logits(b, (s_xn2T, b + 1))
                    number_tokens(b, (s_lg, b + 1))
                    end_of_batch(eng, b)

            def turn_slots(e):
                if e == 0:
                    eng.wait_ge(s_pick, B)
                else:
                    eng.wait_ge(s_dT, e)
                eng.wait_ge(s_disp[e], 32)
                for k, (c0, n) in enumerate(CT):
                    ins = eng.transpose(ps_m[:, c0:c0 + n], disp[0:n, e, k, 0:D], ident[0:n, 0:n])
                ins.then_inc(s_dT_ps, 1)

            def hidden(e, k):
                n = HK * e + k
                if k == 0:
                    eng.wait_ge(s_dT, e + 1)
                    wait(eng, s_expw, 48 * E if e == 0 else 0)
                wait(eng, s_h, n - 1)
                for g, w in enumerate((W1S, W2S)):
                    ins = eng.matmul(ps_t[n % 2][:, 512 * g:512 * g + CAP], w[:, e, P * k:P * (k + 1)],
                                     dispT[:, e % 2, :], start=True, stop=True)
                ins.then_inc(s_h_ps, 1)

            def expert_out(e):
                eng.wait_ge(s_h, HK * (e + 1))
                wait(eng, s_orow, 3 * (e - 1))
                for c, (c0, n) in enumerate(CT):
                    for k in range(HK):
                        ins = eng.matmul(ps_s[e % 2][0:n, D * c:D * (c + 1)], hT[e % 2][:, k, c0:c0 + n], W3S[:, e, k, :],
                                         start=(k == 0), stop=(k == HK - 1))
                ins.then_inc(s_o_ps, 1)

            turn_slots(0)
            for e in range(E):
                for k in range(HK):
                    hidden(e, k)
                    if k == 1 and e >= 1:
                        expert_out(e - 1)
                    if k == 2 and e + 1 < E:
                        turn_slots(e + 1)
            expert_out(E - 1)

        @block.vector
        def _(eng):
            eng.memset(zrow[:, :], 0.0).then_inc(s_vpre, 1)
            eng.memset(ones_row[:, :], 1.0).then_inc(s_rowpat, 1)
            eng.memset(zero_row[:, :], 0.0).then_inc(s_rowpat, 1)
            for st in range(NSET):
                eng.memset(QS[:, st].rearrange("p s h q -> p (s h q)").bitcast(U32), 0).then_inc(s_fill, 1)
            eng.wait_ge(s_wT_ps, 1)
            eng.tensor_copy(wT[:, 0:3, :], ps_m[:, 0:3 * D].rearrange("p (n d) -> p n d", n=3)).then_inc(s_wT, 1)
            eng.wait_ge(s_tanh, 1)
            eng.tensor_scalar(wT[:, 3, :], ps_m[:, 3 * D:4 * D], tanhs[:, 0:1], None, ALU.mult).then_inc(s_wT, 1)
            eng.wait_ge(s_mask, 16)
            eng.tensor_scalar(attend[:, :, :], maski, 0.0, None, ALU.not_equal).then_inc(s_attend, 1)
            stats = Chain(eng, s_stat, 11).at(0)
            eng.wait_ge(s_col, 2)
            stats.next(eng.tensor_copy(colsum[:, 0, :], ps_s[0][0:1, 0:WKEYS]))
            stats.next(eng.tensor_scalar(colsum[:, 1, :], colsum[:, 0, :], -1.0, float(S), ALU.mult, ALU.add))
            stats.next(eng.tensor_tensor(colsum[:, 2, :], colsum[:, 0, :], colsum[:, 1, :], ALU.min))
            stats.next(eng.tensor_reduce(stat[:, 0:1], colsum[:, 2, :], AX.X, ALU.max))
            stats.next(eng.tensor_reduce(stat[:, 1:2], colsum[:, 0, :], AX.X, ALU.max))
            eng.wait_ge(s_col, QT * NWIN)
            stats.next(eng.tensor_reduce(stat[:, 2:3], ps_s[1][0:1, 0:WIN], AX.X, ALU.max))
            stats.next(eng.tensor_tensor(stat[:, 3:4], stat[:, 0:1], stat[:, 2:3], ALU.add))
            stats.next(eng.tensor_scalar(stat[:, 4:5], stat[:, 3:4], 0.0, None, ALU.is_equal))
            stats.next(eng.tensor_scalar(stat[:, 5:6], stat[:, 1:2], float(S), None, ALU.is_equal))
            stats.next(eng.tensor_tensor(stat[:, 6:7], stat[:, 4:5], stat[:, 5:6], ALU.mult))
            stats.next(eng.tensor_copy(flag[:, :], stat[:, 6:7]))
            stats.end()
            eng.tensor_scalar(keybias[:, :], colsum[:, 1, :], -FAR / S, None, ALU.mult).then_inc(s_kbias, 1)
            eng.tensor_copy(stat[:, 7:8], stat[:, 6:7]).then_inc(s_flag, 1)

            ln = Chain(eng, s_ln, 4, wait)
            ln2 = Chain(eng, s_ln2, 4, wait)
            gmax = Chain(eng, s_mgen, 4 * H * NWIN + 1, wait)

            def moments(b):
                if isinstance(b, int):
                    wait(eng, s_rs, 2 * b)
                    eng.wait_ge(s_x[min(b, 2)], 16)
                c, xb = ln, x_pair(b)
                c.at(b)
                for q in range(QT):
                    c.also(eng.bn_stats(bn[:, q, :], xb[:, q, :]))

            def moments_end(b):
                c = ln.at(b)
                wait(eng, s_ln, 4 * b + 2)
                c.k = 2
                for q in range(QT):
                    c.also(eng.bn_aggr(mv[:, q, :], bn[:, q, :]))

            def normalise(path, b):
                wait(eng, s_rs, 2 * (b + 1))
                if path.general:
                    eng.tensor_tensor(rstd[:, :], rstd[:, :], valid[:, 1, :], ALU.mult).then_inc(s_rv, 1)
                    wait(eng, s_rv, b + 1)
                else:
                    wait(eng, s_xnT_ps, b)
                xb = x_pair(b)
                for q in range(QT):
                    eng.tensor_scalar(xn[:, q, :], xb[:, q, :], mv[:, q, 0:1], rstd[:, q:q + 1], ALU.subtract, ALU.mult)\
                       .then_inc(s_xn, 1)

            def rest_k(path, b, i):
                n = b * path.nw + i
                wait(eng, s_k_hi, n + 1)
                if i >= 1 or not path.general:
                    wait(eng, s_k_lo, n)
                eng.tensor_tensor(krest[:, :], ps_m[:, 0:WKEYS], kparts[:, 0, :], ALU.subtract).then_inc(s_k_r, 1)

            def rest_q(path, b):
                wait(eng, s_q_hi, b + 1)
                if not path.general:
                    wait(eng, s_q_lo, b)
                eng.tensor_tensor(qrest[:, :], ps_m[:, 0:S], qparts[:, 0, :], ALU.subtract).then_inc(s_q_r, 1)

            def maximum(b, k):
                if k == 0:
                    wait(eng, s_mp, 6 * (b - 1))
                wait(eng, s_sc, 2 * H * b + k + 1)
                eng.tensor_reduce(wmax[:, b % 2, k % 2, k // 2:k // 2 + 1], ps_s[k % 2][:, 0:WKEYS], AX.X, ALU.max)\
                   .then_inc(s_mx, 1)

            def general_maxima(b):
                c = gmax.at(b)
                for k in range(2 * H * NWIN):
                    i, h, q = k // (2 * H), k // 2 % H, k % 2
                    wait(eng, s_sc, 2 * H * NWIN * b + k + 1)
                    c.next(eng.tensor_tensor(masked, ps_s[k % 2][:, 0:WKEYS], attend[:, q, WIN * i:WIN * i + WKEYS], ALU.add))
                    c.next(eng.tensor_reduce(wmax[:, i, q, h:h + 1], masked, AX.X, ALU.max))
                c.next(eng.tensor_reduce(rowmax[:, :, :].rearrange("p q h -> p (q h)"),
                                         wmax[:, :, :, :].rearrange("p i q h -> p (q h) i"), AX.X, ALU.max))
                c.end()

            def norm_out(path, b, u, between=None):
                wait(eng, s_oq, 4 * b + u + 1)
                if u >= 1 or not path.general:
                    wait(eng, s_on, 4 * b + u)
                if u == 0 and not path.general:
                    wait(eng, s_oc_ps, b)
                turned = ps_m[:, 0:S].rearrange("p (q j c) -> p q j c", q=QT, c=VCOL)
                eng.reciprocal(rsum[:, :, :], turned[:, :, :, DK]).then_inc(s_rsum, 1)
                if between:
                    maximum(*between)
                wait(eng, s_rsum, 4 * b + u + 1)
                for q in range(QT):
                    ins = eng.tensor_tensor(O[:, q, 4 * u:4 * u + 4, :], turned[:, q, :, 0:DK],
                                            rsum[:, q, :].unsqueeze(2).broadcast_to([P, 4, DK]), ALU.mult)
                    if q == QT - 1:
                        ins.then_inc(s_on, 1)

            def add_out(b):
                wait(eng, s_y, b + 1)
                xb = x_pair(b)
                eng.tensor_tensor(xb, ps_m[:, 0:S].rearrange("p (q d) -> p q d", q=QT), xb, ALU.add).then_inc(s_x2, 1)

            def moments2(b):
                wait(eng, s_x2, b + 1)
                if isinstance(b, int):
                    wait(eng, s_rs2, 2 * b)
                c, xb = ln2.at(b), x_pair(b)
                for q in range(QT):
                    c.also(eng.bn_stats(bn2[:, q, :], xb[:, q, :]))

            def moments2_end(b):
                c = ln2.at(b)
                wait(eng, s_ln2, 4 * b + 2)
                c.k = 2
                for q in range(QT):
                    c.also(eng.bn_aggr(mv2[:, q, :], bn2[:, q, :]))

            def normalise2(b, p):
                wait(eng, s_rs2, 2 * (b + 1))
                if isinstance(b, int):
                    wait(eng, s_scat[p], 64 * (b // 2))
                xb = x_pair(b)
                for q in range(QT):
                    eng.tensor_scalar(rows[:, p, q, 0:D], xb[:, q, :], mv2[:, q, 0:1], rstd2[:, q:q + 1],
                                      ALU.subtract, ALU.mult).then_inc(s_xn2, 1)

            def top_two(b):
                if isinstance(b, int):
                    wait(eng, s_rt, 19 * b)
                wait(eng, s_lg_ps, b + 1)
                eng.tensor_tensor(logits[:, :, :], ps_m[:, 0:QT * E].rearrange("p (q e) -> p q e", q=QT), bg[:, :, :], ALU.add)\
                   .then_inc(s_lg, 1)
                wait(eng, s_lg, b + 1)
                for q in range(QT):
                    eng.max(top[:, q, :], logits[:, q, :]).then_inc(s_top, 1)
                for q in range(QT):
                    wait(eng, s_top, 2 * b + q + 1)
                    eng.max_index(topi[:, q, :], top[:, q, :], logits[:, q, :]).then_inc(s_topi, 1)

            def invert_den(b):
                wait(eng, s_rt, 19 * b + 9)
                eng.reciprocal(rden[:, :], den[:, :]).then_inc(s_rden, 1)

            def pick_places(b):
                wait(eng, s_seq, b + 1)
                for q in range(QT):
                    ins = eng.tensor_tensor(picked[:, q, :, :], ps_m[:, E * q:E * (q + 1)].unsqueeze(1).broadcast_to([P, 2, E]),
                                            hot[:, q, :, :], ALU.mult)
                    ins.then_inc(s_pickq, 1) if q == 0 else ins.then_inc(s_pick, 1)
                wait(eng, s_pickq, b + 1)
                wait(eng, s_pick, b + 1)
                eng.tensor_reduce(place[:, :, :].rearrange("p q c -> p (q c)"),
                                  picked[:, :, :, :].rearrange("p q c e -> p (q c) e"), AX.X, ALU.add).then_inc(s_place, 1)

            fast = eng.value_load(flag[0:1, 0:1], min_val=0, max_val=1)
            with eng.If(fast == 1):
                for b in range(2):
                    moments(b)
                    moments_end(b)
                    rest_k(padded, b, 0)
                    normalise(padded, b)
                    rest_q(padded, b)
                for k in range(2 * H):
                    maximum(0, k)
                for b in range(B):
                    left = list(range(2 * H)) if b + 1 < B else []
                    ahead = b + 2 < B
                    for h in range(H):
                        if h == 0 and ahead:
                            moments(b + 2)
                        if h == 2 and ahead:
                            rest_k(padded, b + 2, 0)
                        if h == 1 and ahead:
                            moments_end(b + 2)
                        if h == 4 and ahead:
                            normalise(padded, b + 2)
                        if h == 8 and b >= 1:
                            moments2_end(b - 1)
                        if h == 9 and ahead:
                            rest_q(padded, b + 2)
                        if h == 10 and b >= 1:
                            normalise2(b - 1, (b - 1) % 2)
                        for k in left[3 * h:3 * h + 1]:
                            maximum(b + 1, k)
                        rest = left[3 * h + 1:3 * h + 3]
                        between = (b + 1, rest[0]) if rest and (h == 9 or (h == 3 and b >= 1)) else None
                        if h == 2 and b >= 2:
                            pick_places(b - 2)
                        if h == 3 and b >= 1:
                            norm_out(padded, b - 1, 3, between)
                        if h == 7 and b >= 1:
                            add_out(b - 1)
                            moments2(b - 1)
                        if h == 9:
                            norm_out(padded, b, 0, between)
                        rest = rest[1:] if between else rest
                        if h == 11:
                            norm_out(padded, b, 1)
                        if h == 12 and b >= 1:
                            top_two(b - 1)
                        if h == 15:
                            norm_out(padded, b, 2)
                        for k in rest:
                            maximum(b + 1, k)
                    if b >= 1:
                        invert_den(b - 1)
                pick_places(B - 2)
                norm_out(padded, B - 1, 3)
                add_out(B - 1)
                moments2(B - 1)
                moments2_end(B - 1)
                normalise2(B - 1, (B - 1) % 2)
                top_two(B - 1)
                invert_den(B - 1)
                pick_places(B - 1)
            with eng.Else():
                gb = Chain(eng, s_gb, 4).at(0)
                gb.next(eng.tensor_reduce(valid[:, 0, :], attend[:, :, :], AX.X, ALU.max))
                gb.next(eng.tensor_scalar(valid[:, 1, :], valid[:, 0, :], 0.0, None, ALU.is_gt))
                gb.next(eng.tensor_scalar(valid[:, 2, :], valid[:, 1, :], FAR, None, ALU.mult))
                for q in range(QT):
                    ins = eng.tensor_scalar(attend[:, q, :], attend[:, q, :], -1.0, valid[:, 2, q:q + 1], ALU.add, ALU.mult)
                    if q == 0:
                        ins.then_inc(s_gbq, 1)
                gb.next(ins)
                eng.wait_ge(s_gbq, 1)
                for n in range(3):
                    eng.wait_ge(s_x[n], 16)
                with eng.Fori(0, B) as b:
                    moments(b)
                    moments_end(b)
                    for i in range(NWIN):
                        rest_k(general, b, i)
                    normalise(general, b)
                    rest_q(general, b)
                    general_maxima(b)
                    for u in range(4):
                        norm_out(general, b, u)
                    add_out(b)
                    moments2(b)
                    moments2_end(b)
                    normalise2(b, 0)
                    top_two(b)
                    invert_den(b)
                    pick_places(b)
                    end_of_batch(eng, b)

            def copy_slots(e):
                eng.wait_ge(s_dT_ps, e + 1)
                wait(eng, s_h_ps, HK * (e - 1))
                eng.tensor_copy(dispT[:, e % 2, :], ps_m[:, 0:CAP]).then_inc(s_dT, 1)

            copy_slots(0)
            for e in range(E):
                for k in range(HK):
                    n = HK * e + k
                    eng.wait_ge(s_silu, n + 1)
                    wait(eng, s_o_ps, e - 1)
                    eng.tensor_tensor(hT[e % 2][:, k, :], ps_t[n % 2][:, 512:512 + CAP], silu[:, n % 2, :], ALU.mult)\
                       .then_inc(s_h, 1)
                    if k == 2 and e + 1 < E:
                        copy_slots(e + 1)


_INS = ["x", "ctx_1024", "mask_1x1xSxS2_ik0", "g_xattn", "g_ffn", "L0_xattn_w_q", "L0_xattn_w_k", "L0_xattn_w_v",
        "L0_xattn_w_o", "L0_ffn_Wg", "L0_ffn_bg", "L0_ffn_W1", "L0_ffn_W2", "L0_ffn_W3"]
_OUT = ((B, S, D), "float32")


def kernel(**inputs):
    import numpy as _np
    import concourse.bacc as _bacc
    from concourse import mybir as _mybir
    from concourse.bass_utils import run_bass_kernel_spmd as _run

    nc = _bacc.Bacc("TRN2", target_bir_lowering=False, num_devices=1)
    arrays, args = {}, []
    for name in _INS:
        a = _np.ascontiguousarray(inputs[name])
        arrays[f"in_{name}_dram"] = a
        args.append(nc.dram_tensor(f"in_{name}_dram", a.shape, _mybir.dt.from_np(a.dtype), kind="ExternalInput").ap())
    shape, dtype = _OUT
    args.append(nc.dram_tensor("out_0_dram", shape, _mybir.dt.from_np(_np.dtype(dtype)), kind="ExternalOutput").ap())
    flamingo_kernel(nc, *args)
    r = _run(nc, [arrays], core_ids=[0])
    return r.results[0]["out_0_dram"]
```

```python
from contextlib import ExitStack

import concourse.bass as bass
from concourse import mybir

F32 = mybir.dt.float32
BF16 = mybir.dt.bfloat16
I32 = mybir.dt.int32
U32 = mybir.dt.uint32
ALU = mybir.AluOpType
ACT = mybir.ActivationFunctionType
AX = mybir.AxisListType

P = 128
B, S, D = 8, 256, 128
H, DK = 16, 8
SK = 1601
QT = S // P
NWIN = 4
TILE = 100
WIN = 4 * TILE
WKEYS = WIN + 1
NT = NWIN * 4
E, HID, CAP = 8, 512, 320
HK = HID // P
T = B * S
NTT = T // P
ROW = D + 4
PAIRS = H // 2
HH = H // 2
PROWS = 6 * DK
MASK_ROW = 2 * PROWS
MAX_ROW = MASK_ROW + 1
SROWS = MAX_ROW + 3
NSET = 3
KPAD = WKEYS + 1
VCOL = 32
SCALE = float(DK) ** -0.5
EPS = 1e-5
FAR = 1.0e30
SKIP = 1.0e6
WARM = 36
CT = [(0, 128), (128, 128), (256, 64)]


class Chain:

    def __init__(self, eng, sem, per, wait=None):
        self.eng, self.sem, self.per, self.wait = eng, sem, per, wait or (lambda eng, s, value: eng.wait_ge(s, value))

    def at(self, b):
        self.base, self.k = b * self.per, 0
        return self

    def next(self, instruction):
        self.k += 1
        instruction.then_inc(self.sem, 1)
        self.wait(self.eng, self.sem, self.base + self.k)

    def also(self, instruction):
        self.k += 1
        instruction.then_inc(self.sem, 1)

    def end(self):
        assert self.k == self.per, (self.k, self.per)


def flamingo_kernel(nc, x, ctx, mask, g_xattn, g_ffn, w_q, w_k, w_v, w_o, w_g, b_g, w1, w2, w3, out):
    slots = nc.dram_tensor("slots", [E * CAP, ROW], F32, kind="Internal").ap()
    kspread = nc.dram_tensor("kspread", [NSET, P, 6, WKEYS], BF16, kind="Internal").ap()
    qspread = nc.dram_tensor("qspread", [NSET, P, 6, S], BF16, kind="Internal").ap()
    out_rows = out.rearrange("b s d -> (b s) d")
    x_tiles = x.rearrange("b (q p) d -> p b q d", p=P)
    out_tiles = out.rearrange("b (q p) d -> p b q d", p=P)

    with ExitStack() as stack:
        def sb(name, shape, dt):
            return stack.enter_context(nc.sbuf_tensor(name, shape, dt))

        def sem(name):
            return stack.enter_context(nc.semaphore(name))

        ident = sb("ident", [P, P], F32)
        identb = sb("identb", [P, P], BF16)
        onesb = sb("onesb", [P, P], BF16)
        tri = sb("tri", [P, P], BF16)
        zrow = sb("zrow", [P, ROW], F32)
        iota8i = sb("iota8i", [P, E], I32)
        iota8 = sb("iota8", [P, E], F32)
        tok_i = sb("tok_i", [P, NTT], I32)
        tok = sb("tok", [P, NTT], F32)
        ones_row = sb("ones_row", [3, KPAD], BF16)
        zero_row = sb("zero_row", [1, KPAD], BF16)
        halfpow = sb("halfpow", [P, 2], F32)
        wT = sb("wT", [P, 4, D], F32)
        wg = sb("wg", [P, E], F32)
        bg = sb("bg", [P, QT, E], F32)
        gates = sb("gates", [P, 2], F32)
        tanhs = sb("tanhs", [P, 2], F32)
        attend = sb("attend", [P, QT, SK], BF16)
        colsum = sb("colsum", [1, 3, WKEYS], F32)
        stat = sb("stat", [1, 8], F32)
        keybias = sb("keybias", [1, WKEYS], BF16)
        flag = sb("flag", [1, 1], I32)
        X = sb("X", [P, NTT, D], F32)
        C = sb("C", [P, 2, 4, D], F32)
        ctxT = sb("ctxT", [P, WKEYS], F32)
        kparts = sb("kparts", [P, 3, WKEYS], BF16)
        krest = sb("krest", [P, WKEYS], F32)
        qparts = sb("qparts", [P, 3, S], BF16)
        qrest = sb("qrest", [P, S], F32)
        bn = sb("bn", [P, QT, 6], F32)
        mv = sb("mv", [P, QT, 2], F32)
        rstd = sb("rstd", [P, QT], F32)
        vareps = sb("vareps", [P, QT], F32)
        xn = sb("xn", [P, QT, D], F32)
        xnT = sb("xnT", [P, S], F32)
        valid = sb("valid", [P, 3, QT], F32)
        KSa = sb("KSa", [P, PAIRS * (SK + 3)], BF16)
        QS = sb("QS", [P, NSET, PAIRS, 2, S], BF16)
        VSf = sb("VSf", [P, NSET, 4, H * VCOL], F32)
        probs = sb("probs", [P, 8, 4 * S], F32)
        wmax = sb("wmax", [P, NWIN, QT, H], F32)
        rowmax = sb("rowmax", [P, QT, H], F32)
        mrest = sb("mrest", [P, 2, QT, HH], F32)
        mparts = sb("mparts", [P, 2, QT, 3, HH], BF16)
        mT = sb("mT", [3 * HH, 2, S], BF16)
        OT = sb("OT", [P, 2, S], F32)
        rsum = sb("rsum", [P, 2, QT, 4], F32)
        O = sb("O", [P, QT, H, DK], F32)
        OCT = sb("OCT", [P, S], F32)
        bn2 = sb("bn2", [P, QT, 6], F32)
        mv2 = sb("mv2", [P, QT, 2], F32)
        rstd2 = sb("rstd2", [P, QT], F32)
        vareps2 = sb("vareps2", [P, QT], F32)
        rows = sb("rows", [P, 2, QT, ROW], F32)
        xn2T = sb("xn2T", [P, S], F32)
        logits = sb("logits", [P, QT, E], F32)
        top = sb("top", [P, QT, 8], F32)
        topi = sb("topi", [P, QT, 8], U32)
        topf = sb("topf", [P, QT, 2], F32)
        gap = sb("gap", [P, QT], F32)
        e2 = sb("e2", [P, QT], F32)
        den = sb("den", [P, QT], F32)
        rden = sb("rden", [P, QT], F32)
        hot = sb("hot", [P, QT, 2, E], F32)
        label = sb("label", [P, QT, E], BF16)
        before = sb("before", [P, 3, E], BF16)
        picked = sb("picked", [P, QT, 2, E], F32)
        place = sb("place", [P, QT, 2], F32)
        over = sb("over", [P, QT, 2], F32)
        first = sb("first", [P, QT, 2], F32)
        slot_i = sb("slot_i", [P, 2, QT, 2], I32)
        W1S = sb("W1S", [P, E, HID], F32)
        W2S = sb("W2S", [P, E, HID], F32)
        W3S = sb("W3S", [P, E, HK, D], F32)
        dispT = sb("dispT", [P, 2, CAP], F32)
        spare = sb("spare", [P, 4, E, 3], F32)
        slot_w = sb("slot_w", [P, E, 3], F32)
        slot_t = sb("slot_t", [P, E, 3], F32)
        slot_to = sb("slot_to", [P, E, 3], I32)

        KSp = [KSa[:, p * PAIRS * KPAD:(p + 1) * PAIRS * KPAD].rearrange("p (s k) -> p s k", s=PAIRS)
               for p in range(NSET)]
        KSg = KSa[:, :].rearrange("p (s k) -> p s k", s=PAIRS)
        VSg = [w[:, :, :].rearrange("p e n -> p (e n)").rearrange("p (t n) -> p t n", n=H * VCOL) for w in (W1S, W2S)]
        w3flat = W3S[:, :, :, :].rearrange("p e k n -> p (e k n)").bitcast(BF16)
        biasT = w3flat[:, 0:NT * S].rearrange("p (t q) -> p t q", t=NT)
        pflat = probs[:, :, :].rearrange("p s n -> p (s n)")
        maski = pflat[:, 0:QT * SK].bitcast(I32).rearrange("p (q k) -> p q k", q=QT)
        wraw = pflat[:, QT * SK:QT * SK + 4 * D].rearrange("p (n d) -> p n d", n=4)
        masked = W3S[:, :, :, :].rearrange("p e k n -> p (e k n)")[:, NT * S // 2:NT * S // 2 + WKEYS]
        disp = pflat[:, 0:E * 3 * ROW].rearrange("p (e c n) -> p e c n", e=E, c=3)
        o0 = E * 3 * ROW
        hT = pflat[:, o0:o0 + HK * CAP].rearrange("p (k n) -> p k n", k=HK)
        o1 = o0 + HK * CAP
        silu = pflat[:, o1:o1 + 2 * CAP].rearrange("p (b n) -> p b n", b=2)
        o2 = o1 + 2 * CAP
        orow = pflat[:, o2:o2 + 2 * 3 * D].rearrange("p (b c n) -> p b c n", b=2, c=3)
        o3 = o2 + 6 * D
        hT = [hT, pflat[:, o3:o3 + HK * CAP].rearrange("p (k n) -> p k n", k=HK)]
        assert o3 + HK * CAP <= 8 * 4 * S

        ps_s = [stack.enter_context(nc.psum_tensor(f"ps_s{i}", [P, 512], F32)) for i in range(2)]
        ps_t = [stack.enter_context(nc.psum_tensor(f"ps_t{i}", [P, 1024], F32)) for i in range(2)]
        ps_o = stack.enter_context(nc.psum_tensor("ps_o", [P, 512], F32))
        ps_m = stack.enter_context(nc.psum_tensor("ps_m", [P, 512], F32))

        s_w = sem("weights_loaded")
        s_mask = sem("mask_loaded")
        s_x = [sem(f"x_loaded{i}") for i in range(3)]
        s_ctx = [sem("ctx_loaded0"), sem("ctx_loaded1")]
        s_expw = sem("expert_weights_loaded")
        s_zero = sem("slots_zeroed")
        s_pre = sem("pool_setup")
        s_vpre = sem("vector_setup")
        s_attend = sem("attend_made")
        s_wT_ps = sem("weights_turned")
        s_wT = sem("weights_copied")
        s_col = sem("column_sums")
        s_stat = sem("mask_statistics")
        s_flag = sem("path_decided")
        s_kbias = sem("key_bias_made")
        s_kb = sem("key_bias_rows")
        s_tanh = sem("tanhs_made")
        s_fill = sem("stacks_filled")
        s_rowpat = sem("row_patterns_made")
        s_const = sem("stack_constants_written")
        s_vones = sem("v_buffers_cleared")
        s_gates = sem("small_tensors_loaded")
        s_rv = sem("rstd_of_valid_rows")
        s_ctxT_ps = sem("ctxT_in_psum")
        s_ctxT = sem("ctxT_copied")
        s_k_ps = sem("k_in_psum")
        s_k_hi = sem("k_high")
        s_k_r = sem("k_rest")
        s_k_mid = sem("k_middle")
        s_k_lo = sem("k_low")
        s_v_ps = sem("v_in_psum")
        s_v = sem("v_copied")
        s_ln = sem("ln_chain")
        s_rs = sem("rstd_chain")
        s_xn = sem("xn_made")
        s_xnT_ps = sem("xnT_in_psum")
        s_xnT = sem("xnT_copied")
        s_q_ps = sem("q_in_psum")
        s_q_hi = sem("q_high")
        s_q_r = sem("q_rest")
        s_q_mid = sem("q_middle")
        s_q_lo = sem("q_low")
        s_kd = sem("k_parts_in_dram")
        s_qd = sem("q_parts_in_dram")
        s_ks = [sem(f"k_stack_written{i}") for i in range(NWIN)]
        s_qs = [sem(f"q_stack_written{i}") for i in range(NSET)]
        s_sc = sem("scores_for_max")
        s_mx = sem("maxima_taken")
        s_mgen = sem("general_max_chain")
        s_mp = sem("max_parts_chain")
        s_mT_ps = sem("mT_in_psum")
        s_mT = sem("mT_copied")
        s_mr = sem("max_rows_written")
        s_st = sem("scores_for_exp")
        s_ex = sem("exp_done")
        s_pv = sem("pv_done")
        s_ot = sem("out_copied")
        s_oq = sem("out_turned")
        s_rsum = sem("sums_inverted")
        s_on = sem("out_normed")
        s_oc_ps = sem("outT_in_psum")
        s_oc = sem("outT_copied")
        s_y = sem("projected")
        s_x2 = sem("x2_made")
        s_x2out = sem("x2_stored")
        s_ln2 = sem("ln2_chain")
        s_rs2 = sem("rstd2_chain")
        s_xn2 = sem("xn2_made")
        s_xn2T_ps = sem("xn2T_in_psum")
        s_xn2T = sem("xn2T_copied")
        s_lg_ps = sem("logits_in_psum")
        s_lg = sem("logits_made")
        s_top = sem("top_values")
        s_topi = sem("top_indices")
        s_gap = sem("gap_made")
        s_e2 = sem("gap_exp")
        s_den = sem("den_made")
        s_rden = sem("den_inverted")
        s_rt = sem("route_chain")
        s_seq = sem("seq_in_psum")
        s_pick = sem("place_picked")
        s_pickq = sem("first_tile_picked")
        s_place = sem("place_summed")
        s_scat = [sem("rows_scattered0"), sem("rows_scattered1")]
        s_disp = [sem(f"slots_loaded{e}") for e in range(E)]
        s_dT_ps = sem("dispT_in_psum")
        s_dT = sem("dispT_copied")
        s_h_ps = sem("h_in_psum")
        s_silu = sem("silu_done")
        s_h = sem("h_made")
        s_o_ps = sem("expert_out_in_psum")
        s_orow = sem("expert_rows")
        s_sw = sem("slot_chain")
        s_add = [sem("rows_added0"), sem("rows_added1")]
        s_gb = sem("general_bias_chain")
        s_gbq = sem("general_bias_first_tile")
        s_bT_ps = sem("biasT_in_psum")
        s_bT = sem("biasT_copied")
        s_vg = sem("general_v_cleared")
        s_settle = sem("nothing")

        class Path:

            def __init__(self, general):
                self.general = general
                self.windows = list(range(NWIN)) if general else [NWIN - 1]
                self.nw = len(self.windows)
                self.pre = int(general)

            def number(self, b, i):
                return b * self.nw + i + self.pre

            def batch(self, b):
                return b + self.pre

            def set_of(self, b):
                return 0 if self.general else b % NSET

            def ks(self, b, i):
                return KSg[:, :, WIN * i:WIN * i + WKEYS] if self.general else KSp[b % NSET][:, :, 0:WKEYS]

            def vs(self, b, i, t):
                if not self.general:
                    return VSf[:, b % NSET, t, :]
                n = 4 * i + t
                return VSg[n // 8][:, n % 8, :]

            def depth(self, i, t):
                return TILE + (self.windows[i] == NWIN - 1 and t == 3)

        padded, general = Path(False), Path(True)
        block = stack.enter_context(nc.Block())

        def settle(eng):
            eng.sem_inc(s_settle, 1)

        def wait(eng, s, value):
            if not isinstance(value, int):
                eng.wait_ge(s, value)
                settle(eng)
            elif value > 0:
                eng.wait_ge(s, value)

        def x_pair(b):
            return X[:, 2 * b:2 * b + 2, :] if isinstance(b, int) else X[:, bass.ds(2 * b, 2), :]

        def end_of_batch(eng, b):
            wait(eng, s_scat[0], 64 * (b + 1))
            wait(eng, s_x2out, 16 * (b + 1))

        @block.sync
        def _(eng):
            def load_ctx(path, b, i):
                cb = i % 2 if path.general else b % 2
                if not path.general:
                    wait(eng, s_ctxT_ps, b - 1)
                elif i >= 2:
                    wait(eng, s_ctxT_ps, path.number(b, i) - 1)
                base = WIN * path.windows[i]
                eng.dma_start(C[0:TILE, cb, :, :], ctx[b, base:base + WIN, :].rearrange("(t k) d -> k t d", k=TILE))\
                   .then_inc(s_ctx[cb], 16)
                eng.dma_start(C[TILE:TILE + 1, cb, 3, :], ctx[b, base + WIN:base + WKEYS, :]).then_inc(s_ctx[cb], 16)

            def load_x():
                eng.dma_start(X[:, 2:4, :], x_tiles[:, 1]).then_inc(s_x[1], 16)
                eng.dma_start(X[:, 4:, :].rearrange("p (b q) d -> p b q d", q=QT), x_tiles[:, 2:]).then_inc(s_x[2], 16)

            def spread_k(path, b, i):
                n = path.number(b, i)
                st = path.set_of(b)
                wait(eng, s_k_lo, n + 1)
                if not path.general:
                    wait(eng, s_ks[st], 32 * (b // NSET))
                elif i == 0:
                    wait(eng, s_ks[0], 32 * (b + 1))
                else:
                    wait(eng, s_ks[i - 1], 32 * (b + 1) + (32 if i == 1 else 0))
                for r0, parts in ((0, 3), (3, 2), (5, 1)):
                    eng.dma_start(kspread[st, :, r0:r0 + parts, :], kparts[:, 0:parts, :]).then_inc(s_kd, 16)

            def stack_k(path, b, i):
                st = path.set_of(b)
                wait(eng, s_kd, 48 * (path.number(b, i) + 1))
                if not path.general:
                    wait(eng, s_st, H * (b - NSET + 1))
                dst = path.ks(b, i)
                src = kspread[st].rearrange("(s h d) n k -> h (d n) s k", h=2, d=DK)
                for hp in range(2):
                    eng.dma_start(dst[PROWS * hp:PROWS * (hp + 1), :, :], src[hp])\
                       .then_inc(s_ks[i if path.general else st], 16)

            def spread_q(path, b):
                st = path.set_of(b)
                n = path.batch(b)
                wait(eng, s_q_lo, n + 1)
                if path.general:
                    wait(eng, s_qs[0], 32 * (b + 1))
                else:
                    wait(eng, s_qs[st], 32 * (b // NSET))
                for r0, parts, part in ((0, 3, 0), (3, 2, 1), (5, 1, 2)):
                    eng.dma_start(qspread[st, :, r0:r0 + parts, :],
                                  qparts[:, part:part + 1, :].broadcast_to([P, parts, S])).then_inc(s_qd, 16)

            def stack_q(path, b):
                st = path.set_of(b)
                wait(eng, s_qd, 48 * (path.batch(b) + 1))
                if not path.general:
                    wait(eng, s_st, H * (b - NSET + 1))
                src = qspread[st].rearrange("(s h d) n k -> h (d n) s k", h=2, d=DK)
                for hp in range(2):
                    eng.dma_start(QS[PROWS * hp:PROWS * (hp + 1), st, :, hp, :], src[hp]).then_inc(s_qs[st], 16)

            def max_rows(path, b, half):
                st, s0 = path.set_of(b), half * PAIRS // 2
                wait(eng, s_mT, 2 * b + half + 1)
                for c in range(3):
                    dst = QS[MAX_ROW + c:MAX_ROW + c + 1, st, s0:s0 + PAIRS // 2, :, :]
                    eng.dma_start(dst.rearrange("c s h q -> c (s h) q"), mT[HH * c:HH * (c + 1), half, :])\
                       .then_inc(s_mr, 16)

            def store_x2(b):
                wait(eng, s_x2, b + 1)
                eng.dma_start(out_tiles[:, b], x_pair(b)).then_inc(s_x2out, 16)

            def expert_weights(e):
                eng.dma_start(W1S[:, e, :], w1[e]).then_inc(s_expw, 16)
                eng.dma_start(W2S[:, e, :], w2[e]).then_inc(s_expw, 16)
                eng.dma_start(W3S[:, e, :, :], w3[e].rearrange("(k p) d -> p k d", p=P)).then_inc(s_expw, 16)

            def q_ones():
                eng.dma_start(QS[MASK_ROW:MAX_ROW].rearrange("c t s h q -> c (t s h) q"),
                              ones_row[0:1, 0:S].unsqueeze(1).broadcast_to([1, NSET * H, S])).then_inc(s_const, 16)

            eng.dma_start(wraw[:, 1, :], w_k).then_inc(s_w, 16)
            load_ctx(padded, 0, 0)
            eng.dma_start(X[:, 0:2, :], x_tiles[:, 0]).then_inc(s_x[0], 16)
            eng.dma_start(wraw[:, 0, :], w_q).then_inc(s_w, 16)
            eng.dma_start(wraw[:, 2, :], w_v).then_inc(s_w, 16)
            eng.dma_start(wraw[:, 3, :], w_o).then_inc(s_w, 16)
            eng.dma_start(maski, mask[0, 0].rearrange("(q p) k -> p q k", p=P)).then_inc(s_mask, 16)
            load_ctx(padded, 1, 0)
            load_x()
            quarter = (SK + 3) // 4
            quarters = KSa[:, :].rearrange("p (s k) -> p s k", k=quarter)
            eng.wait_ge(s_rowpat, 2)
            eng.dma_start(quarters[MAX_ROW:SROWS], ones_row[0:3, 0:quarter].unsqueeze(1)
                          .broadcast_to([3, 4 * PAIRS, quarter])).then_inc(s_const, 16)
            eng.wait_ge(s_fill, NSET)
            q_ones()
            spread_k(padded, 0, 0)
            spread_q(padded, 0)
            stack_k(padded, 0, 0)
            stack_q(padded, 0)
            eng.wait_ge(s_flag, 1)
            fast = eng.value_load(flag[0:1, 0:1], min_val=0, max_val=1)
            with eng.If(fast == 1):
                every = KSa[:, 0:NSET * PAIRS * KPAD].rearrange("p (s k) -> p s k", k=KPAD)
                eng.wait_ge(s_kbias, 1)
                eng.dma_start(every[MASK_ROW:MAX_ROW, :, 0:WKEYS],
                              keybias[:, :].unsqueeze(1).broadcast_to([1, NSET * PAIRS, WKEYS])).then_inc(s_const, 16)
                spread_k(padded, 1, 0)
                spread_q(padded, 1)
                stack_k(padded, 1, 0)
                stack_q(padded, 1)
                load_ctx(padded, 2, 0)
                max_rows(padded, 0, 0)
                for b in range(B):
                    if b + 3 < B:
                        load_ctx(padded, b + 3, 0)
                    max_rows(padded, b, 1)
                    expert_weights(b)
                    if b + 2 < B:
                        spread_k(padded, b + 2, 0)
                        stack_k(padded, b + 2, 0)
                        spread_q(padded, b + 2)
                    if b + 1 < B:
                        max_rows(padded, b + 1, 0)
                    if b + 2 < B:
                        stack_q(padded, b + 2)
                    if b >= 1:
                        store_x2(b - 1)
                store_x2(B - 1)
            with eng.Else():
                eng.dma_start(quarters[MASK_ROW:MAX_ROW], zero_row[:, 0:quarter].unsqueeze(1)
                              .broadcast_to([1, 4 * PAIRS, quarter])).then_inc(s_const, 16)
                eng.wait_ge(s_ctxT_ps, 1)
                for n in range(2):
                    eng.wait_ge(s_ctx[n], 32)
                with eng.Fori(0, B) as b:
                    load_ctx(general, b, 0)
                    load_ctx(general, b, 1)
                    for i in range(NWIN):
                        spread_k(general, b, i)
                        stack_k(general, b, i)
                        if i + 2 < NWIN:
                            load_ctx(general, b, i + 2)
                    spread_q(general, b)
                    stack_q(general, b)
                    for half in range(2):
                        max_rows(general, b, half)
                    store_x2(b)
                    end_of_batch(eng, b)
                for e in range(E):
                    expert_weights(e)
            with eng.If(fast == 1):
                eng.wait_ge(s_scat[0], 32 * B)
                eng.wait_ge(s_scat[1], 32 * B)
            with eng.Else():
                eng.wait_ge(s_scat[0], 64 * B)
            for e in range(E):
                eng.dma_start(disp[:, e, 0:2, :], slots[CAP * e:CAP * e + 256, :].rearrange("(c p) n -> p c n", p=P))\
                   .then_inc(s_disp[e], 16)
                eng.dma_start(disp[0:64, e, 2, :], slots[CAP * e + 256:CAP * (e + 1), :]).then_inc(s_disp[e], 16)
            eng.wait_ge(s_add[0], 24 * E)
            eng.wait_ge(s_add[1], 24 * E)
            eng.wait_ge(s_zero, 16)
            eng.wait_ge(s_x2out, 16 * B)

        @block.gpsimd
        def _(eng):
            setup = Chain(eng, s_pre, 11).at(0)
            setup.next(eng.memset(ident[:, :], 0.0))
            setup.next(eng.affine_select(out=ident[:, :], in_=ident[:, :], compare_op=ALU.not_equal, fill=1.0,
                                         base=0, pattern=[[-1, P]], channel_multiplier=1))
            setup.next(eng.memset(onesb[:, :], 1.0))
            setup.next(eng.tensor_copy(identb[:, :], ident[:, :]))
            setup.next(eng.affine_select(out=tri[:, :], in_=onesb[:, :], compare_op=ALU.is_ge, fill=0.0,
                                         base=0, pattern=[[1, P]], channel_multiplier=-1))
            setup.next(eng.iota(iota8i[:, :], pattern=[[1, E]], base=0, channel_multiplier=0))
            setup.next(eng.tensor_copy(iota8[:, :], iota8i[:, :]))
            setup.next(eng.iota(tok_i[:, :], pattern=[[P, NTT]], base=1, channel_multiplier=1))
            setup.next(eng.tensor_copy(tok[:, :], tok_i[:, :]))
            setup.next(eng.memset(halfpow[:, :], -0.5))
            setup.next(eng.memset(before[:, :, :], 0.0))
            setup.end()
            def clear_v(st):
                eng.memset(VSf[:, st, :, :], 0.0).then_inc(s_vones, 1)
                eng.wait_ge(s_vones, 2 * st + 1)
                eng.memset(VSf[:, st, :, :].rearrange("p t (h c) -> p (t h) c", c=VCOL)[:, :, DK:DK + 1], 1.0)\
                   .then_inc(s_vones, 1)

            rs_chain = Chain(eng, s_rs, 2, wait)
            mp_chain = Chain(eng, s_mp, 6, wait)
            rs2_chain = Chain(eng, s_rs2, 2, wait)
            rt_chain = Chain(eng, s_rt, 18, wait)

            def rstd_of(path, b):
                n = path.batch(b)
                wait(eng, s_ln, 4 * (n + 1))
                wait(eng, s_xn, 2 * n)
                c = rs_chain.at(n)
                c.next(eng.tensor_scalar(vareps[:, :], mv[:, :, 1], EPS, None, ALU.add))
                c.next(eng.tensor_tensor(rstd[:, :], vareps[:, :], halfpow[:, :], ALU.pow))

            def split_k(path, b, i):
                n = path.number(b, i)
                wait(eng, s_k_r, n + 1)
                wait(eng, s_kd, 48 * n)
                eng.tensor_copy(kparts[:, 1, :], krest[:, :]).then_inc(s_k_mid, 1)
                wait(eng, s_k_mid, n + 1)
                eng.tensor_tensor(kparts[:, 2, :], krest[:, :], kparts[:, 1, :], ALU.subtract).then_inc(s_k_lo, 1)

            def split_q(path, b):
                n = path.batch(b)
                wait(eng, s_q_r, n + 1)
                wait(eng, s_qd, 48 * n)
                eng.tensor_copy(qparts[:, 1, :], qrest[:, :]).then_inc(s_q_mid, 1)
                wait(eng, s_q_mid, n + 1)
                eng.tensor_tensor(qparts[:, 2, :], qrest[:, :], qparts[:, 1, :], ALU.subtract).then_inc(s_q_lo, 1)

            def max_parts(path, b, half):
                if path.general:
                    wait(eng, s_mgen, (2 * 2 * H * NWIN + 1) * (b + 1))
                else:
                    eng.wait_ge(s_mx, 2 * H * b + 2 * HH * (half + 1))
                    wait(eng, s_mT_ps, 2 * b + half - 1)
                c = mp_chain.at(2 * b + half)
                src = (rowmax[:, :, :] if path.general else wmax[:, b % 2, :, :])[:, :, HH * half:HH * (half + 1)]
                c.next(eng.tensor_scalar(mrest[:, 0], src, -1.0, None, ALU.mult))
                c.next(eng.tensor_copy(mparts[:, half, :, 0, :], mrest[:, 0]))
                c.next(eng.tensor_tensor(mrest[:, 1], mrest[:, 0], mparts[:, half, :, 0, :], ALU.subtract))
                c.next(eng.tensor_copy(mparts[:, half, :, 1, :], mrest[:, 1]))
                c.next(eng.tensor_tensor(mrest[:, 0], mrest[:, 1], mparts[:, half, :, 1, :], ALU.subtract))
                c.next(eng.tensor_copy(mparts[:, half, :, 2, :], mrest[:, 0]))
                c.end()

            def rstd2_of(b):
                wait(eng, s_ln2, 4 * (b + 1))
                c = rs2_chain.at(b)
                c.next(eng.tensor_scalar(vareps2[:, :], mv2[:, :, 1], EPS, None, ALU.add))
                c.next(eng.tensor_tensor(rstd2[:, :], vareps2[:, :], halfpow[:, :], ALU.pow))

            def route_labels(b):
                wait(eng, s_topi, 2 * (b + 1))
                if isinstance(b, int):
                    wait(eng, s_e2, b)
                eng.tensor_tensor(gap[:, :], top[:, :, 1], top[:, :, 0], ALU.subtract).then_inc(s_gap, 1)
                c = rt_chain.at(b)
                c.next(eng.tensor_copy(topf[:, :, :], topi[:, :, 0:2]))
                for q in range(QT):
                    for k in range(2):
                        (c.next if q * k else c.also)(eng.tensor_scalar(hot[:, q, k, :], iota8[:, :], topf[:, q, k:k + 1], None, ALU.is_equal))
                c.next(eng.tensor_tensor(label[:, :, :], hot[:, :, 0, :], hot[:, :, 1, :], ALU.add))
                c.next(eng.tensor_tensor(before[:, 1, :], before[:, 0, :], label[:, 0, :], ALU.add))
                c.next(eng.tensor_tensor(before[:, 2, :], before[:, 1, :], label[:, 1, :], ALU.add))
                c.next(eng.tensor_scalar(first[:, :, :], topf[:, :, :], float(CAP), -1.0, ALU.mult, ALU.add))
                return c

            def route_weights(b, p, c):
                row = rows[:, p, :, :]
                wait(eng, s_rden, b + 1)
                if isinstance(b, int):
                    wait(eng, s_scat[p], 64 * (b // 2))
                c.also(eng.tensor_copy(row[:, :, D + 3], topf[:, :, 0]))
                c.next(eng.tensor_scalar(row[:, :, D + 1], rden[:, :], tanhs[:, 1:2], None, ALU.mult))
                c.also(eng.tensor_tensor(row[:, :, D + 2], row[:, :, D + 1], e2[:, :], ALU.mult))
                c.next(eng.tensor_copy(row[:, :, D], tok[:, 2 * b:2 * b + 2] if isinstance(b, int)
                                       else tok[:, bass.ds(2 * b, 2)]))

            def scatter(b, p, c):
                row = rows[:, p, :, :]
                eng.wait_ge(s_zero, 16)
                wait(eng, s_place, b + 1)
                c.also(eng.tensor_scalar(over[:, :, :], place[:, :, :], float(CAP), SKIP, ALU.is_gt, ALU.mult))
                c.next(eng.tensor_tensor(first[:, :, :], first[:, :, :], place[:, :, :], ALU.add))
                c.next(eng.tensor_tensor(first[:, :, :], over[:, :, :], first[:, :, :], ALU.add))
                c.also(eng.tensor_copy(slot_i[:, p, :, :], first[:, :, :]))
                c.next(eng.tensor_copy(before[:, 0, :], before[:, 2, :]))
                c.end()
                for q in range(QT):
                    for k in range(2):
                        eng.indirect_dma_start(slots[:, :], bass.IndirectOffsetOnAxis(ap=slot_i[:, p, q, k:k + 1], axis=0),
                                               row[:, q, :], None, bounds_check=E * CAP - 1, oob_is_err=False)\
                           .then_inc(s_scat[p], 16)

            clear_v(0)
            rstd_of(padded, 0)
            split_k(padded, 0, 0)
            split_q(padded, 0)
            for st in range(1, NSET):
                clear_v(st)
            eng.wait_ge(s_tanh, 1)
            eng.wait_ge(s_flag, 1)
            fast = eng.value_load(flag[0:1, 0:1], min_val=0, max_val=1)
            with eng.If(fast == 1):
                rstd_of(padded, 1)
                split_k(padded, 1, 0)
                split_q(padded, 1)
                max_parts(padded, 0, 0)
                rstd_of(padded, 2)
                for b in range(B):
                    max_parts(padded, b, 1)
                    if b >= 2:
                        c = route_labels(b - 2)
                    if b + 2 < B:
                        split_k(padded, b + 2, 0)
                    if b >= 2:
                        route_weights(b - 2, b % 2, c)
                        scatter(b - 2, b % 2, c)
                    if b + 1 < B:
                        max_parts(padded, b + 1, 0)
                    if b + 2 < B:
                        split_q(padded, b + 2)
                    if b >= 1:
                        rstd2_of(b - 1)
                    if b + 3 < B:
                        rstd_of(padded, b + 3)
                c = route_labels(B - 2)
                route_weights(B - 2, B % 2, c)
                scatter(B - 2, B % 2, c)
                rstd2_of(B - 1)
                c = route_labels(B - 1)
                route_weights(B - 1, (B - 1) % 2, c)
                scatter(B - 1, (B - 1) % 2, c)
            with eng.Else():
                eng.memset(VSg[0], 0.0).then_inc(s_vg, 1)
                eng.memset(VSg[1], 0.0).then_inc(s_vg, 1)
                eng.wait_ge(s_vg, 2)
                for g in range(2):
                    eng.memset(VSg[g].rearrange("p t (h c) -> p (t h) c", c=VCOL)[:, :, DK:DK + 1], 1.0).then_inc(s_vg, 1)
                with eng.Fori(0, B) as b:
                    rstd_of(general, b)
                    for i in range(NWIN):
                        split_k(general, b, i)
                    split_q(general, b)
                    for half in range(2):
                        max_parts(general, b, half)
                    rstd2_of(b)
                    c = route_labels(b)
                    route_weights(b, 0, c)
                    scatter(b, 0, c)
                    end_of_batch(eng, b)

            for e in range(E):
                eng.wait_ge(s_disp[e], 32)
            c = Chain(eng, s_sw, 16).at(0)
            for n, cs in ((P, slice(0, 2)), (64, slice(2, 3))):
                number, first_w, second_w, first_e = (disp[0:n, :, cs, D + k] for k in range(4))
                away, gain, other, same = (spare[0:n, k, :, cs] for k in range(4))
                expert = iota8[0:n, :].unsqueeze(2).broadcast_to([n, E, cs.stop - cs.start])
                c.also(eng.tensor_tensor(other, first_e, expert, ALU.subtract))
                c.also(eng.tensor_tensor(gain, first_w, second_w, ALU.subtract))
                c.next(eng.tensor_scalar(away, number, 0.0, SKIP, ALU.is_equal, ALU.mult))
                c.also(eng.tensor_scalar(same, other, 0.0, None, ALU.is_equal))
                c.next(eng.tensor_tensor(slot_t[0:n, :, cs], away, number, ALU.add))
                c.also(eng.tensor_scalar(slot_to[0:n, :, cs], slot_t[0:n, :, cs], -1.0, None, ALU.add))
                c.next(eng.tensor_tensor(other, gain, same, ALU.mult))
                c.next(eng.tensor_tensor(slot_w[0:n, :, cs], other, second_w, ALU.add))
            c.end()
            eng.wait_ge(s_x2out, 16 * B)
            for e in range(E):
                if e >= 1:
                    eng.wait_ge(s_add[(e - 1) % 2], 48 * ((e + 1) // 2))
                for k, (_, n) in enumerate(CT):
                    eng.wait_ge(s_orow, 3 * e + k + 1)
                    eng.indirect_dma_start(out_rows, bass.IndirectOffsetOnAxis(ap=slot_to[0:n, e, k:k + 1], axis=0),
                                           orow[0:n, e % 2, k, :], None, bounds_check=T - 1, oob_is_err=False,
                                           compute_op=ALU.add).then_inc(s_add[e % 2], 16)

        @block.scalar
        def _(eng):
            eng.dma_start(gates[:, 0:1], g_xattn.rearrange("(a n) -> a n", a=1).broadcast_to([P, 1])).then_inc(s_gates, 16)
            eng.dma_start(gates[:, 1:2], g_ffn.rearrange("(a n) -> a n", a=1).broadcast_to([P, 1])).then_inc(s_gates, 16)
            eng.dma_start(wg[:, :], w_g).then_inc(s_gates, 16)
            for q in range(QT):
                eng.dma_start(bg[:, q, :], b_g.rearrange("(a n) -> a n", a=1).broadcast_to([P, E])).then_inc(s_gates, 16)
            eng.wait_ge(s_gates, 80)
            eng.activation(tanhs[:, :], gates[:, :], ACT.Tanh).then_inc(s_tanh, 1)

            def copy_ctxT(path, b, i, bank=ps_m):
                n = path.number(b, i)
                eng.wait_ge(s_ctxT_ps, n + 1)
                wait(eng, s_v_ps, n)
                eng.activation(ctxT[:, :], bank[:, 0:WKEYS], ACT.Copy).then_inc(s_ctxT, 1)

            def high_k(path, b, i, bank=ps_m):
                n = path.number(b, i)
                eng.wait_ge(s_k_ps, n + 1)
                wait(eng, s_kd, 48 * n)
                eng.activation(kparts[:, 0, :], bank[:, 0:WKEYS], ACT.Copy).then_inc(s_k_hi, 1)

            def copy_xnT(path, b, bank=ps_m):
                eng.wait_ge(s_xnT_ps, path.batch(b) + 1)
                eng.activation(xnT[:, :], bank[:, 0:S], ACT.Copy).then_inc(s_xnT, 1)

            def copy_v(path, b, i, bank=ps_m):
                eng.wait_ge(s_v_ps, path.number(b, i) + 1)
                if path.general:
                    eng.wait_ge(s_vg, 4)
                    g = 4 * i
                    dst = VSg[g // 8][:, g % 8:g % 8 + 4, :]
                else:
                    if b < NSET:
                        eng.wait_ge(s_vones, 2 * (b + 1))
                    wait(eng, s_pv, 4 * (b - NSET + 1))
                    dst = VSf[:, b % NSET, :, :]
                dst = dst.rearrange("p t (h c) -> p (t h) c", c=VCOL)[0:TILE + 1, :, 0:DK]
                src = bank[0:TILE + 1, 0:4 * D].rearrange("p (n c) -> p n c", c=DK)
                eng.activation(dst, src, ACT.Copy).then_inc(s_v, 1)

            def high_q(path, b, bank=ps_m):
                n = path.batch(b)
                eng.wait_ge(s_q_ps, n + 1)
                wait(eng, s_qd, 48 * n)
                eng.activation(qparts[:, 0, :], bank[:, 0:S], ACT.Copy).then_inc(s_q_hi, 1)

            def copy_mT(path, b, half):
                eng.wait_ge(s_mT_ps, 2 * b + half + 1)
                if not path.general:
                    wait(eng, s_mr, 48 * (2 * b + half - 1))
                eng.activation(mT[:, half, :], ps_m[0:3 * HH, 0:S // 2].bitcast(BF16), ACT.Copy).then_inc(s_mT, 1)

            def exp(path, b, r, j):
                n = 16 * path.nw * b + 4 * r + j
                eng.wait_ge(s_st, n + 1)
                if r >= 2 or not path.general:
                    wait(eng, s_pv, 4 * path.nw * b + r - 1)
                eng.activation(probs[0:TILE + 1, (4 * r + j) % 8, :], ps_t[(4 * r + j) % 2][0:TILE + 1, :], ACT.Exp,
                               scale=SCALE).then_inc(s_ex, 1)

            def copy_o(path, b, u):
                eng.wait_ge(s_pv, path.nw * (4 * b + u + 1))
                if u >= 2 or not path.general:
                    wait(eng, s_oq, 2 * b + u // 2)
                eng.activation(OT[:, u % 2, :], ps_o[:, 0:S], ACT.Copy).then_inc(s_ot, 1)

            def copy_oc(b):
                eng.wait_ge(s_oc_ps, b + 1)
                eng.activation(OCT[:, :], ps_m[:, 0:S], ACT.Copy).then_inc(s_oc, 1)

            def copy_xn2T(b):
                eng.wait_ge(s_xn2T_ps, b + 1)
                eng.activation(xn2T[:, :], ps_m[:, 0:S], ACT.Copy).then_inc(s_xn2T, 1)

            def exp_gap(b):
                eng.wait_ge(s_gap, b + 1)
                if isinstance(b, int):
                    wait(eng, s_rt, 18 * b)
                eng.activation(e2[:, :], gap[:, :], ACT.Exp).then_inc(s_e2, 1)

            copy_ctxT(padded, 0, 0, ps_t[0])
            high_k(padded, 0, 0, ps_t[1])
            copy_xnT(padded, 0, ps_t[0][:, 512:])
            high_q(padded, 0, ps_t[1][:, 512:])
            copy_v(padded, 0, 0, ps_o)
            eng.wait_ge(s_flag, 1)
            fast = eng.value_load(flag[0:1, 0:1], min_val=0, max_val=1)
            with eng.If(fast == 1):
                copy_ctxT(padded, 1, 0)
                high_k(padded, 1, 0)
                copy_xnT(padded, 1)
                high_q(padded, 1)
                copy_v(padded, 1, 0)
                copy_mT(padded, 0, 0)
                copy_ctxT(padded, 2, 0)
                eng.wait_ge(s_vpre, 1)
                eng.dma_start(slots.rearrange("(p r) n -> p r n", p=P),
                              zrow[:, :].unsqueeze(1).broadcast_to([P, E * CAP // P, ROW])).then_inc(s_zero, 16)
                for b in range(B):
                    ahead, last = b + 2 < B, b == B - 1
                    for h in range(H):
                        if h == 0 and b >= 1:
                            copy_o(padded, b - 1, 2)
                        if h == 1 and ahead:
                            high_k(padded, b + 2, 0)
                        if h == 3:
                            copy_mT(padded, b, 1)
                        if h == 3 and b >= 2:
                            exp_gap(b - 2)
                        if h == 4 and ahead:
                            copy_xnT(padded, b + 2)
                        if h == 4 and b >= 1:
                            copy_o(padded, b - 1, 3)
                        if h == 7 and b >= 1:
                            copy_oc(b - 1)
                        if h == 8 and ahead:
                            high_q(padded, b + 2)
                        if h == 8:
                            copy_o(padded, b, 0)
                        if h == 11 and ahead:
                            copy_v(padded, b + 2, 0)
                        if h == 12 and b + 1 < B:
                            copy_mT(padded, b + 1, 0)
                        if h == 12:
                            copy_o(padded, b, 1)
                        if h == (11 if last else 13) and b >= 1:
                            copy_xn2T(b - 1)
                        if h == 15 and last:
                            exp_gap(b - 1)
                        if h == 15 and b + 3 < B:
                            copy_ctxT(padded, b + 3, 0)
                        exp(padded, b, h // 4, h % 4)
                copy_o(padded, B - 1, 2)
                copy_o(padded, B - 1, 3)
                copy_oc(B - 1)
                copy_xn2T(B - 1)
                exp_gap(B - 1)
            with eng.Else():
                eng.wait_ge(s_vpre, 1)
                eng.dma_start(slots.rearrange("(p r) n -> p r n", p=P),
                              zrow[:, :].unsqueeze(1).broadcast_to([P, E * CAP // P, ROW])).then_inc(s_zero, 16)
                for t in range(0, NT, 4):
                    eng.wait_ge(s_bT_ps, t // 4 + 1)
                    eng.activation(biasT[0:TILE + 1, t:t + 4, :].rearrange("p t q -> p (t q)"),
                                   ps_m[0:TILE + 1, :].bitcast(BF16), ACT.Copy).then_inc(s_bT, 1)
                with eng.Fori(0, B) as b:
                    for i in range(NWIN):
                        copy_ctxT(general, b, i)
                        high_k(general, b, i)
                        copy_v(general, b, i)
                    copy_xnT(general, b)
                    high_q(general, b)
                    for half in range(2):
                        copy_mT(general, b, half)
                    for u in range(4):
                        for i in range(NWIN):
                            for j in range(4):
                                exp(general, b, NWIN * u + i, j)
                        copy_o(general, b, u)
                    copy_oc(b)
                    copy_xn2T(b)
                    exp_gap(b)
                    end_of_batch(eng, b)

            def silu_of(e, k):
                n = HK * e + k
                eng.wait_ge(s_h_ps, n + 1)
                wait(eng, s_h, n - 1)
                eng.activation(silu[:, n % 2, :], ps_t[n % 2][:, 0:CAP], ACT.Silu).then_inc(s_silu, 1)

            def weighted_rows(e):
                eng.wait_ge(s_o_ps, e + 1)
                eng.wait_ge(s_sw, 16)
                wait(eng, s_add[e % 2], 48 * (e // 2))
                for k, (_, n) in enumerate(CT):
                    eng.activation(orow[0:n, e % 2, k, :], ps_s[e % 2][0:n, D * k:D * (k + 1)], ACT.Copy,
                                   scale=slot_w[0:n, e, k:k + 1]).then_inc(s_orow, 1)

            for e in range(E):
                for k in range(HK):
                    silu_of(e, k)
                    if k == 1 and e >= 1:
                        weighted_rows(e - 1)
            weighted_rows(E - 1)

        @block.tensor
        def _(eng):
            eng.wait_ge(s_pre, 5)
            eng.wait_ge(s_w, 64)
            for n in range(4):
                ins = eng.transpose(ps_m[:, D * n:D * (n + 1)], wraw[:, n, :], ident[:, :])
            ins.then_inc(s_wT_ps, 1)
            def turn_ctx(path, b, i, free, bank=ps_m):
                wait(eng, *free)
                if path.general:
                    eng.wait_ge(s_ctx[i % 2], 32 * (2 * b + i // 2 + 2))
                    cb = i % 2
                else:
                    eng.wait_ge(s_ctx[b % 2], 32 * (b // 2 + 1))
                    cb = b % 2
                for t in range(4):
                    n = TILE + (t == 3)
                    ins = eng.transpose(bank[:, TILE * t:TILE * t + n], C[0:n, cb, t, :], ident[0:n, 0:n])
                ins.then_inc(s_ctxT_ps, 1)

            def project_k(path, b, i, free=(s_ctxT, 0), bank=ps_m):
                wait(eng, *free)
                eng.wait_ge(s_ctxT, path.number(b, i) + 1)
                eng.matmul(bank[:, 0:WKEYS], wT[:, 1, :], ctxT[:, :], start=True, stop=True).then_inc(s_k_ps, 1)

            def turn_xn(path, b, free, bank=ps_m):
                wait(eng, *free)
                eng.wait_ge(s_xn, 2 * (path.batch(b) + 1))
                for q in range(QT):
                    ins = eng.transpose(bank[:, P * q:P * (q + 1)], xn[:, q, :], ident[:, :])
                ins.then_inc(s_xnT_ps, 1)

            def project_v(path, b, i, free, bank=ps_m):
                wait(eng, *free)
                eng.wait_ge(s_ctxT, path.number(b, i) + 1)
                for t in range(4):
                    ins = eng.matmul(bank[0:TILE + 1, D * t:D * (t + 1)], ctxT[:, TILE * t:TILE * t + TILE + 1],
                                     wT[:, 2, :], start=True, stop=True)
                ins.then_inc(s_v_ps, 1)

            def project_q(path, b, free, bank=ps_m):
                wait(eng, *free)
                eng.wait_ge(s_xnT, path.batch(b) + 1)
                eng.matmul(bank[:, 0:S], wT[:, 0, :], xnT[:, :], start=True, stop=True).then_inc(s_q_ps, 1)

            def score_for_max(path, b, k):
                i, h, q = k // (2 * H), k // 2 % H, k % 2
                n = 2 * H * path.nw * b + k
                if k % (2 * H) == 0:
                    if path.general:
                        eng.wait_ge(s_ks[i], 32 * (b + 1) + (32 if i == 0 else 0))
                    else:
                        eng.wait_ge(s_ks[b % NSET], 32 * (b // NSET + 1))
                if k == 0:
                    if path.general:
                        eng.wait_ge(s_qs[0], 32 * (b + 2))
                    else:
                        eng.wait_ge(s_qs[b % NSET], 32 * (b // NSET + 1))
                    eng.wait_ge(s_const, 48)
                if not path.general:
                    wait(eng, s_mx, n - 1)
                elif k >= 2:
                    eng.wait_ge(s_mgen, 257 * b + 2 * (k - 2) + 1)
                eng.matmul(ps_s[k % 2][:, 0:WKEYS], QS[0:MAX_ROW, path.set_of(b), h // 2, h % 2, P * q:P * (q + 1)],
                           path.ks(b, i)[0:MAX_ROW, h // 2, :], start=True, stop=True).then_inc(s_sc, 1)

            def turn_max(b, half, free):
                wait(eng, *free)
                wait(eng, s_mp, 6 * (2 * b + half + 1))
                dst = ps_m[0:3 * HH, 0:S // 2].bitcast(BF16)
                for q in range(QT):
                    ins = eng.transpose(dst[:, P * q:P * (q + 1)], mparts[:, half, q, :, :].rearrange("p c h -> p (c h)"),
                                        identb[:, :])
                ins.then_inc(s_mT_ps, 1)

            def score_for_exp(path, b, r, j):
                u, i = r // path.nw, r % path.nw
                h, k = 4 * u + j, 4 * r + j
                n = 16 * path.nw * b + k
                if path.general:
                    if k == 0:
                        eng.wait_ge(s_mr, 96 * (b + 1))
                elif h % HH == 0:
                    eng.wait_ge(s_mr, 96 * b + 48 * (h // HH + 1))
                if k >= 2 or not path.general:
                    wait(eng, s_ex, n - 1)
                dst, st = ps_t[k % 2], path.set_of(b)
                for t in range(4):
                    ins = eng.matmul(dst[0:TILE + 1, S * t:S * (t + 1)],
                                     path.ks(b, i)[0:SROWS, h // 2, TILE * t:TILE * t + TILE + 1],
                                     QS[0:SROWS, st, h // 2, h % 2, :], start=True, stop=not path.general)
                    if path.general:
                        ins = eng.matmul(dst[0:TILE + 1, S * t:S * (t + 1)], identb[0:TILE + 1, 0:TILE + 1],
                                         biasT[0:TILE + 1, 4 * i + t, :], start=False, stop=True)
                ins.then_inc(s_st, 1)

            def weigh_v(path, b, r, tiles=range(4)):
                u, i = r // path.nw, r % path.nw
                if 0 in tiles:
                    eng.wait_ge(s_ex, path.nw * 16 * b + 4 * r + 4)
                    if u == 0 and i == 0:
                        eng.wait_ge(s_v, path.nw * (b + 1) + path.pre)
                    if i == 0 and (u >= 1 or not path.general):
                        wait(eng, s_ot, 4 * b + u)
                for t in tiles:
                    d = path.depth(i, t)
                    for j in range(4):
                        h = 4 * u + j
                        ins = eng.matmul(ps_o[VCOL * j:VCOL * (j + 1), 0:S],
                                         path.vs(b, i, t)[0:d, VCOL * h:VCOL * (h + 1)],
                                         probs[0:d, (4 * r + j) % 8, S * t:S * (t + 1)],
                                         start=(i == 0 and t == 0), stop=(i == path.nw - 1 and t == 3))
                if 3 in tiles:
                    ins.then_inc(s_pv, 1)

            def turn_out(b, v, free):
                wait(eng, *free)
                eng.wait_ge(s_ot, 4 * b + 2 * v + 2)
                for n in range(2 * QT):
                    ins = eng.transpose(ps_m[:, P * n:P * (n + 1)], OT[:, n // QT, P * (n % QT):P * (n % QT + 1)], ident[:, :])
                ins.then_inc(s_oq, 1)

            def turn_normed(b, free):
                wait(eng, *free)
                eng.wait_ge(s_on, 2 * (b + 1))
                for q in range(QT):
                    ins = eng.transpose(ps_m[:, P * q:P * (q + 1)], O[:, q, :, :].rearrange("p h d -> p (h d)"), ident[:, :])
                ins.then_inc(s_oc_ps, 1)

            def project_out(b, free):
                wait(eng, *free)
                eng.wait_ge(s_oc, b + 1)
                for q in range(QT):
                    ins = eng.matmul(ps_m[:, D * q:D * (q + 1)], OCT[:, P * q:P * (q + 1)], wT[:, 3, :], start=True, stop=True)
                ins.then_inc(s_y, 1)

            def turn_xn2(b, p, free):
                wait(eng, *free)
                eng.wait_ge(s_xn2, 2 * (b + 1))
                for q in range(QT):
                    ins = eng.transpose(ps_m[:, P * q:P * (q + 1)], rows[:, p, q, 0:D], ident[:, :])
                ins.then_inc(s_xn2T_ps, 1)

            def make_logits(b, free):
                wait(eng, *free)
                eng.wait_ge(s_xn2T, b + 1)
                for q in range(QT):
                    ins = eng.matmul(ps_m[:, E * q:E * (q + 1)], xn2T[:, P * q:P * (q + 1)], wg[:, :], start=True, stop=True)
                ins.then_inc(s_lg_ps, 1)

            def number_tokens(b, free):
                wait(eng, *free)
                eng.wait_ge(s_rt, 18 * b + 8)
                both = QT * E
                eng.matmul(ps_m[:, 0:both], tri[:, :], label[:, :, :].rearrange("p q e -> p (q e)"), start=True, stop=False)
                eng.matmul(ps_m[:, 0:both], onesb[:, :], before[:, 0:QT, :].rearrange("p q e -> p (q e)"),
                           start=False, stop=True).then_inc(s_seq, 1)

            turn_ctx(padded, 0, 0, (s_wT, 0), ps_t[0])
            eng.wait_ge(s_wT, 1)
            project_k(padded, 0, 0, bank=ps_t[1])
            turn_xn(padded, 0, (s_wT, 0), ps_t[0][:, 512:])
            project_q(padded, 0, (s_wT, 0), ps_t[1][:, 512:])
            project_v(padded, 0, 0, (s_wT, 0), ps_o)
            eng.wait_ge(s_attend, 1)
            for q in range(QT):
                eng.matmul(ps_s[0][0:1, 0:WKEYS], onesb[:, 0:1], attend[:, q, SK - WKEYS:SK],
                           start=(q == 0), stop=(q == QT - 1)).then_inc(s_col, 1)
            for n in range(QT * (NWIN - 1)):
                q, w = n % QT, n // QT
                eng.matmul(ps_s[1][0:1, 0:WIN], onesb[:, 0:1], attend[:, q, WIN * w:WIN * (w + 1)],
                           start=(n == 0), stop=(n == QT * (NWIN - 1) - 1)).then_inc(s_col, 1)

            def keep_warm(count):
                eng.wait_ge(s_ex, H * B)
                for n in range(count):
                    eng.matmul(ps_t[0][:, 0:512], identb[:, :], onesb[:, 0:1].broadcast_to([P, 512]), start=True, stop=True)

            eng.wait_ge(s_wT, 2)
            eng.wait_ge(s_gates, 80)
            eng.wait_ge(s_flag, 1)
            fast = eng.value_load(flag[0:1, 0:1], min_val=0, max_val=1)
            with eng.If(fast == 1):
                for k in range(2 * H):
                    if k == 2:
                        turn_ctx(padded, 1, 0, (s_wT, 2))
                    if k == 4:
                        project_k(padded, 1, 0)
                    if k == 7:
                        turn_xn(padded, 1, (s_k_r, 2))
                    if k == 9:
                        project_q(padded, 1, (s_xnT, 2))
                    if k == 12:
                        project_v(padded, 1, 0, (s_q_r, 2))
                    if k == 22:
                        turn_max(0, 0, (s_v, 2))
                    if k == 26:
                        turn_ctx(padded, 2, 0, (s_mT, 1))
                    score_for_max(padded, 0, k)
                eng.wait_ge(s_k_r, 1)
                eng.wait_ge(s_v, 1)
                for b in range(B):
                    ahead, last = b + 2 < B, b == B - 1
                    for h in range(H):
                        score_for_exp(padded, b, h // 4, h % 4)
                        if b + 1 < B:
                            score_for_max(padded, b + 1, 2 * h)
                        if h == 0 and ahead:
                            project_k(padded, b + 2, 0, (s_lg, max(b - 1, 0)))
                        if h == 2:
                            turn_max(b, 1, (s_k_r, b + 3) if ahead else (s_lg, b - 1))
                        if h == 3 and ahead:
                            turn_xn(padded, b + 2, (s_mT, 2 * b + 2))
                        if h == 4 and b >= 2:
                            number_tokens(b - 2, (s_xnT, b + 3) if ahead else (s_mT, 2 * b + 2))
                        if h == 5 and b >= 1:
                            turn_out(b - 1, 1, (s_pick, b - 1) if b >= 2 else (s_xnT, b + 3))
                        if h == 6 and b >= 1:
                            turn_normed(b - 1, (s_on, 2 * b))
                        if h == 7 and ahead:
                            project_q(padded, b + 2, (s_oc, b))
                        if h == (8 if last else 9) and b >= 1:
                            project_out(b - 1, (s_q_r, b + 3) if ahead else (s_oc, b))
                        if h == 10 and ahead:
                            project_v(padded, b + 2, 0, (s_x2, b) if b else (s_q_r, b + 3))
                        if h == 11 and b + 1 < B:
                            turn_max(b + 1, 0, (s_v, b + 3) if ahead else (s_x2, b))
                        if h == (10 if last else 12) and b >= 1:
                            turn_xn2(b - 1, (b - 1) % 2, (s_mT, 2 * b + 3) if b + 1 < B else (s_x2, b))
                        if h == 13:
                            turn_out(b, 0, (s_lg, b) if last else (s_xn2T, b) if b else (s_mT, 3))
                        if h == 14 and b + 3 < B:
                            turn_ctx(padded, b + 3, 0, (s_on, 2 * b + 1))
                        if h == (12 if last else 15) and b >= 1:
                            make_logits(b - 1, (s_xn2T, b) if last else (s_ctxT, b + 4) if b + 3 < B else (s_on, 2 * b + 1))
                        if h == 15 and last:
                            number_tokens(b - 1, (s_on, 2 * b + 1))
                        group = (b, h // 4 - 1) if h >= 4 else (b - 1, 3)
                        if group[0] >= 0:
                            weigh_v(padded, *group, tiles=[h % 4])
                        if b + 1 < B:
                            score_for_max(padded, b + 1, 2 * h + 1)
                weigh_v(padded, B - 1, 3)
                turn_out(B - 1, 1, (s_pick, B - 1))
                turn_normed(B - 1, (s_on, 2 * B))
                project_out(B - 1, (s_oc, B))
                turn_xn2(B - 1, (B - 1) % 2, (s_x2, B))
                make_logits(B - 1, (s_xn2T, B))
                number_tokens(B - 1, (s_lg, B))
                keep_warm(WARM)
            with eng.Else():
                eng.wait_ge(s_gb, 4)
                eng.wait_ge(s_wT, 2)
                for t in range(NT):
                    if t % 4 == 0 and t:
                        eng.wait_ge(s_bT, t // 4)
                    for q in range(QT):
                        ins = eng.transpose(ps_m[0:TILE + 1, :].bitcast(BF16)[:, S * (t % 4) + P * q:S * (t % 4) + P * (q + 1)],
                                            attend[:, q, TILE * t:TILE * t + TILE + 1], identb[:, :])
                    if t % 4 == 3:
                        ins.then_inc(s_bT_ps, 1)
                eng.wait_ge(s_bT, 4)
                with eng.Fori(0, B) as b:
                    for i in range(NWIN):
                        turn_ctx(general, b, i, (s_v, NWIN * b + i + 1) if i else (s_bT, 4))
                        project_k(general, b, i)
                        project_v(general, b, i, (s_k_r, NWIN * b + i + 2))
                    turn_xn(general, b, (s_v, NWIN * (b + 1) + 1))
                    project_q(general, b, (s_xnT, b + 2))
                    for k in range(2 * H * NWIN):
                        score_for_max(general, b, k)
                    for half in range(2):
                        turn_max(b, half, (s_mT, 2 * b + 1) if half else (s_q_r, b + 2))
                    for u in range(4):
                        for i in range(NWIN):
                            for j in range(4):
                                score_for_exp(general, b, NWIN * u + i, j)
                            weigh_v(general, b, NWIN * u + i)
                        if u % 2:
                            turn_out(b, u // 2, (s_on, 2 * b + 1) if u > 1 else (s_mT, 2 * b + 2))
                    turn_normed(b, (s_on, 2 * b + 2))
                    project_out(b, (s_oc, b + 1))
                    turn_xn2(b, 0, (s_x2, b + 1))
                    make_logits(b, (s_xn2T, b + 1))
                    number_tokens(b, (s_lg, b + 1))
                    end_of_batch(eng, b)

            def turn_slots(e):
                if e == 0:
                    eng.wait_ge(s_pick, B)
                else:
                    eng.wait_ge(s_dT, e)
                eng.wait_ge(s_disp[e], 32)
                for k, (c0, n) in enumerate(CT):
                    ins = eng.transpose(ps_m[:, c0:c0 + n], disp[0:n, e, k, 0:D], ident[0:n, 0:n])
                ins.then_inc(s_dT_ps, 1)

            def hidden(e, k):
                n = HK * e + k
                if k == 0:
                    eng.wait_ge(s_dT, e + 1)
                    wait(eng, s_expw, 48 * E if e == 0 else 0)
                wait(eng, s_h, n - 1)
                for g, w in enumerate((W1S, W2S)):
                    ins = eng.matmul(ps_t[n % 2][:, 512 * g:512 * g + CAP], w[:, e, P * k:P * (k + 1)],
                                     dispT[:, e % 2, :], start=True, stop=True)
                ins.then_inc(s_h_ps, 1)

            def expert_out(e, chunks):
                if 0 in chunks:
                    eng.wait_ge(s_h, HK * (e + 1))
                    wait(eng, s_orow, 3 * (e - 1))
                for c in chunks:
                    c0, n = CT[c]
                    for k in range(HK):
                        ins = eng.matmul(ps_s[e % 2][0:n, D * c:D * (c + 1)], hT[e % 2][:, k, c0:c0 + n], W3S[:, e, k, :],
                                         start=(k == 0), stop=(k == HK - 1))
                if 2 in chunks:
                    ins.then_inc(s_o_ps, 1)

            turn_slots(0)
            for e in range(E):
                for k in range(HK):
                    hidden(e, k)
                    if k == 0 and e >= 1:
                        expert_out(e - 1, (0, 1))
                    if k == 1 and e >= 1:
                        expert_out(e - 1, (2,))
                    if k == 2 and e + 1 < E:
                        turn_slots(e + 1)
            expert_out(E - 1, (0, 1, 2))

        @block.vector
        def _(eng):
            eng.memset(zrow[:, :], 0.0).then_inc(s_vpre, 1)
            eng.memset(ones_row[:, :], 1.0).then_inc(s_rowpat, 1)
            eng.memset(zero_row[:, :], 0.0).then_inc(s_rowpat, 1)
            ln = Chain(eng, s_ln, 4, wait)
            ln2 = Chain(eng, s_ln2, 4, wait)
            gmax = Chain(eng, s_mgen, 4 * H * NWIN + 1, wait)

            def moments(path, b):
                n = path.batch(b)
                wait(eng, s_rs, 2 * n)
                if not path.general:
                    eng.wait_ge(s_x[min(b, 2)], 16)
                c, xb = ln.at(n), x_pair(b)
                for q in range(QT):
                    c.also(eng.bn_stats(bn[:, q, :], xb[:, q, :]))

            def moments_end(path, b):
                n = path.batch(b)
                c = ln.at(n)
                wait(eng, s_ln, 4 * n + 2)
                c.k = 2
                for q in range(QT):
                    c.also(eng.bn_aggr(mv[:, q, :], bn[:, q, :]))

            def normalise(path, b):
                n = path.batch(b)
                wait(eng, s_rs, 2 * (n + 1))
                if path.general:
                    eng.tensor_tensor(rstd[:, :], rstd[:, :], valid[:, 1, :], ALU.mult).then_inc(s_rv, 1)
                    wait(eng, s_rv, b + 1)
                wait(eng, s_xnT_ps, n)
                xb = x_pair(b)
                for q in range(QT):
                    eng.tensor_scalar(xn[:, q, :], xb[:, q, :], mv[:, q, 0:1], rstd[:, q:q + 1], ALU.subtract, ALU.mult)\
                       .then_inc(s_xn, 1)

            def rest_k(path, b, i, bank=ps_m):
                n = path.number(b, i)
                wait(eng, s_k_hi, n + 1)
                wait(eng, s_k_lo, n)
                eng.tensor_tensor(krest[:, :], bank[:, 0:WKEYS], kparts[:, 0, :], ALU.subtract).then_inc(s_k_r, 1)

            def rest_q(path, b, bank=ps_m):
                n = path.batch(b)
                wait(eng, s_q_hi, n + 1)
                wait(eng, s_q_lo, n)
                eng.tensor_tensor(qrest[:, :], bank[:, 0:S], qparts[:, 0, :], ALU.subtract).then_inc(s_q_r, 1)

            def maximum(b, k):
                if k == 0:
                    wait(eng, s_mp, 6 * (b - 1))
                wait(eng, s_sc, 2 * H * b + k + 1)
                eng.tensor_reduce(wmax[:, b % 2, k % 2, k // 2:k // 2 + 1], ps_s[k % 2][:, 0:WKEYS], AX.X, ALU.max)\
                   .then_inc(s_mx, 1)

            def general_maxima(b):
                c = gmax.at(b)
                for k in range(2 * H * NWIN):
                    i, h, q = k // (2 * H), k // 2 % H, k % 2
                    wait(eng, s_sc, 2 * H * NWIN * b + k + 1)
                    c.next(eng.tensor_tensor(masked, ps_s[k % 2][:, 0:WKEYS], attend[:, q, WIN * i:WIN * i + WKEYS], ALU.add))
                    c.next(eng.tensor_reduce(wmax[:, i, q, h:h + 1], masked, AX.X, ALU.max))
                c.next(eng.tensor_reduce(rowmax[:, :, :].rearrange("p q h -> p (q h)"),
                                         wmax[:, :, :, :].rearrange("p i q h -> p (q h) i"), AX.X, ALU.max))
                c.end()

            def norm_out(path, b, v):
                wait(eng, s_oq, 2 * b + v + 1)
                if v >= 1 or not path.general:
                    wait(eng, s_on, 2 * b + v)
                if v == 0 and not path.general:
                    wait(eng, s_oc_ps, b)
                turned = ps_m[:, :].rearrange("p (g q j c) -> p g q j c", g=2, q=QT, c=VCOL)
                eng.reciprocal(rsum[:, :, :, :], turned[:, :, :, :, DK]).then_inc(s_rsum, 1)
                wait(eng, s_rsum, 2 * b + v + 1)
                for g in range(2):
                    h0 = 8 * v + 4 * g
                    ins = eng.tensor_tensor(O[:, :, h0:h0 + 4, :], turned[:, g, :, :, 0:DK],
                                            rsum[:, g, :, :].unsqueeze(3).broadcast_to([P, QT, 4, DK]), ALU.mult)
                ins.then_inc(s_on, 1)

            def add_out(b):
                wait(eng, s_y, b + 1)
                xb = x_pair(b)
                eng.tensor_tensor(xb, ps_m[:, 0:S].rearrange("p (q d) -> p q d", q=QT), xb, ALU.add).then_inc(s_x2, 1)

            def moments2(b):
                wait(eng, s_x2, b + 1)
                if isinstance(b, int):
                    wait(eng, s_rs2, 2 * b)
                c, xb = ln2.at(b), x_pair(b)
                for q in range(QT):
                    c.also(eng.bn_stats(bn2[:, q, :], xb[:, q, :]))

            def moments2_end(b):
                c = ln2.at(b)
                wait(eng, s_ln2, 4 * b + 2)
                c.k = 2
                for q in range(QT):
                    c.also(eng.bn_aggr(mv2[:, q, :], bn2[:, q, :]))

            def normalise2(b, p):
                wait(eng, s_rs2, 2 * (b + 1))
                if isinstance(b, int):
                    wait(eng, s_scat[p], 64 * (b // 2))
                xb = x_pair(b)
                for q in range(QT):
                    eng.tensor_scalar(rows[:, p, q, 0:D], xb[:, q, :], mv2[:, q, 0:1], rstd2[:, q:q + 1],
                                      ALU.subtract, ALU.mult).then_inc(s_xn2, 1)

            def top_two(b):
                if isinstance(b, int):
                    wait(eng, s_rt, 18 * b)
                wait(eng, s_lg_ps, b + 1)
                eng.tensor_tensor(logits[:, :, :], ps_m[:, 0:QT * E].rearrange("p (q e) -> p q e", q=QT), bg[:, :, :], ALU.add)\
                   .then_inc(s_lg, 1)
                wait(eng, s_lg, b + 1)
                for q in range(QT):
                    eng.max(top[:, q, :], logits[:, q, :]).then_inc(s_top, 1)
                for q in range(QT):
                    wait(eng, s_top, 2 * b + q + 1)
                    eng.max_index(topi[:, q, :], top[:, q, :], logits[:, q, :]).then_inc(s_topi, 1)

            def invert_den(b):
                wait(eng, s_e2, b + 1)
                eng.tensor_scalar(den[:, :], e2[:, :], 1.0, None, ALU.add).then_inc(s_den, 1)
                wait(eng, s_den, b + 1)
                eng.reciprocal(rden[:, :], den[:, :]).then_inc(s_rden, 1)

            def pick_places(b):
                wait(eng, s_seq, b + 1)
                for q in range(QT):
                    ins = eng.tensor_tensor(picked[:, q, :, :], ps_m[:, E * q:E * (q + 1)].unsqueeze(1).broadcast_to([P, 2, E]),
                                            hot[:, q, :, :], ALU.mult)
                    ins.then_inc(s_pickq, 1) if q == 0 else ins.then_inc(s_pick, 1)
                wait(eng, s_pickq, b + 1)
                wait(eng, s_pick, b + 1)
                eng.tensor_reduce(place[:, :, :].rearrange("p q c -> p (q c)"),
                                  picked[:, :, :, :].rearrange("p q c e -> p (q c) e"), AX.X, ALU.add).then_inc(s_place, 1)

            def clear_q(st):
                eng.memset(QS[:, st].rearrange("p s h q -> p (s h q)").bitcast(U32), 0).then_inc(s_fill, 1)

            clear_q(0)
            clear_q(1)
            moments(padded, 0)
            clear_q(2)
            eng.wait_ge(s_wT_ps, 1)
            eng.tensor_copy(wT[:, 0:3, :], ps_m[:, 0:3 * D].rearrange("p (n d) -> p n d", n=3)).then_inc(s_wT, 1)
            moments_end(padded, 0)
            normalise(padded, 0)
            rest_k(padded, 0, 0, ps_t[1])
            eng.wait_ge(s_mask, 16)
            eng.tensor_scalar(attend[:, :, :], maski, 0.0, None, ALU.not_equal).then_inc(s_attend, 1)
            rest_q(padded, 0, ps_t[1][:, 512:])
            eng.wait_ge(s_tanh, 1)
            eng.tensor_scalar(wT[:, 3, :], ps_m[:, 3 * D:4 * D], tanhs[:, 0:1], None, ALU.mult).then_inc(s_wT, 1)
            stats = Chain(eng, s_stat, 11).at(0)
            eng.wait_ge(s_col, 2)
            stats.next(eng.tensor_copy(colsum[:, 0, :], ps_s[0][0:1, 0:WKEYS]))
            stats.also(eng.tensor_reduce(stat[:, 1:2], ps_s[0][0:1, 0:WKEYS], AX.X, ALU.max))
            stats.next(eng.tensor_scalar(colsum[:, 1, :], colsum[:, 0, :], -1.0, float(S), ALU.mult, ALU.add))
            eng.tensor_scalar(keybias[:, :], colsum[:, 1, :], -FAR / S, None, ALU.mult).then_inc(s_kbias, 1)
            stats.next(eng.tensor_tensor(colsum[:, 2, :], colsum[:, 0, :], colsum[:, 1, :], ALU.min))
            stats.also(eng.tensor_reduce(stat[:, 0:1], colsum[:, 2, :], AX.X, ALU.max))
            eng.wait_ge(s_col, QT * NWIN)
            stats.next(eng.tensor_reduce(stat[:, 2:3], ps_s[1][0:1, 0:WIN], AX.X, ALU.max))
            stats.also(eng.tensor_scalar(stat[:, 5:6], stat[:, 1:2], float(S), None, ALU.is_equal))
            stats.next(eng.tensor_tensor(stat[:, 3:4], stat[:, 0:1], stat[:, 2:3], ALU.add))
            stats.next(eng.tensor_scalar(stat[:, 4:5], stat[:, 3:4], 0.0, None, ALU.is_equal))
            stats.next(eng.tensor_tensor(stat[:, 6:7], stat[:, 4:5], stat[:, 5:6], ALU.mult))
            stats.next(eng.tensor_copy(flag[:, :], stat[:, 6:7]))
            stats.end()
            eng.tensor_copy(stat[:, 7:8], stat[:, 6:7]).then_inc(s_flag, 1)

            fast = eng.value_load(flag[0:1, 0:1], min_val=0, max_val=1)
            with eng.If(fast == 1):
                for k in range(2 * H):
                    if k == 0:
                        moments(padded, 1)
                    if k == 2:
                        moments_end(padded, 1)
                    if k == 5:
                        normalise(padded, 1)
                    if k == 6:
                        rest_k(padded, 1, 0)
                    if k == 11:
                        rest_q(padded, 1)
                    if k == 28:
                        moments(padded, 2)
                    if k == 30:
                        moments_end(padded, 2)
                    maximum(0, k)
                for b in range(B):
                    ahead, last = b + 2 < B, b == B - 1
                    for h in range(H):
                        if h == 1 and ahead:
                            rest_k(padded, b + 2, 0)
                        if h == 2 and ahead:
                            normalise(padded, b + 2)
                        if h == 4 and b >= 2:
                            invert_den(b - 2)
                        if h == 8 and ahead:
                            rest_q(padded, b + 2)
                        if h == (9 if last else 10) and b >= 1:
                            moments2_end(b - 1)
                        if h == 7 and b + 3 < B:
                            moments(padded, b + 3)
                        if h == 8 and b + 3 < B:
                            moments_end(padded, b + 3)
                        if b + 1 < B:
                            maximum(b + 1, 2 * h)
                        then = (b + 1, 2 * h + 1) if b + 1 < B else None
                        norms = {5: (b - 1, 1), 13: (b, 0)}.get(h, (-1, 0))
                        if h == 4 and b >= 2:
                            pick_places(b - 2)
                        if h == (8 if last else 9) and b >= 1:
                            add_out(b - 1)
                            moments2(b - 1)
                        if h == (9 if last else 11) and b >= 1:
                            normalise2(b - 1, (b - 1) % 2)
                        if h == (12 if last else 15) and b >= 1:
                            top_two(b - 1)
                        if h == 15 and last:
                            pick_places(b - 1)
                            invert_den(b - 1)
                        if norms[0] >= 0:
                            norm_out(padded, *norms)
                        if then:
                            maximum(*then)
                norm_out(padded, B - 1, 1)
                add_out(B - 1)
                moments2(B - 1)
                moments2_end(B - 1)
                normalise2(B - 1, (B - 1) % 2)
                top_two(B - 1)
                invert_den(B - 1)
                pick_places(B - 1)
            with eng.Else():
                gb = Chain(eng, s_gb, 4).at(0)
                gb.next(eng.tensor_reduce(valid[:, 0, :], attend[:, :, :], AX.X, ALU.max))
                gb.next(eng.tensor_scalar(valid[:, 1, :], valid[:, 0, :], 0.0, None, ALU.is_gt))
                gb.next(eng.tensor_scalar(valid[:, 2, :], valid[:, 1, :], FAR, None, ALU.mult))
                for q in range(QT):
                    ins = eng.tensor_scalar(attend[:, q, :], attend[:, q, :], -1.0, valid[:, 2, q:q + 1], ALU.add, ALU.mult)
                    if q == 0:
                        ins.then_inc(s_gbq, 1)
                gb.next(ins)
                eng.wait_ge(s_gbq, 1)
                for n in range(3):
                    eng.wait_ge(s_x[n], 16)
                with eng.Fori(0, B) as b:
                    moments(general, b)
                    moments_end(general, b)
                    for i in range(NWIN):
                        rest_k(general, b, i)
                    normalise(general, b)
                    rest_q(general, b)
                    general_maxima(b)
                    for v in range(2):
                        norm_out(general, b, v)
                    add_out(b)
                    moments2(b)
                    moments2_end(b)
                    normalise2(b, 0)
                    top_two(b)
                    invert_den(b)
                    pick_places(b)
                    end_of_batch(eng, b)

            def copy_slots(e):
                eng.wait_ge(s_dT_ps, e + 1)
                wait(eng, s_h_ps, HK * (e - 1))
                eng.tensor_copy(dispT[:, e % 2, :], ps_m[:, 0:CAP]).then_inc(s_dT, 1)

            copy_slots(0)
            for e in range(E):
                for k in range(HK):
                    n = HK * e + k
                    eng.wait_ge(s_silu, n + 1)
                    wait(eng, s_o_ps, e - 1)
                    eng.tensor_tensor(hT[e % 2][:, k, :], ps_t[n % 2][:, 512:512 + CAP], silu[:, n % 2, :], ALU.mult)\
                       .then_inc(s_h, 1)
                    if k == 2 and e + 1 < E:
                        copy_slots(e + 1)


_INS = ["x", "ctx_1024", "mask_1x1xSxS2_ik0", "g_xattn", "g_ffn", "L0_xattn_w_q", "L0_xattn_w_k", "L0_xattn_w_v",
        "L0_xattn_w_o", "L0_ffn_Wg", "L0_ffn_bg", "L0_ffn_W1", "L0_ffn_W2", "L0_ffn_W3"]
_OUT = ((B, S, D), "float32")


def kernel(**inputs):
    import numpy as _np
    import concourse.bacc as _bacc
    from concourse import mybir as _mybir
    from concourse.bass_utils import run_bass_kernel_spmd as _run

    nc = _bacc.Bacc("TRN2", target_bir_lowering=False, num_devices=1)
    arrays, args = {}, []
    for name in _INS:
        a = _np.ascontiguousarray(inputs[name])
        arrays[f"in_{name}_dram"] = a
        args.append(nc.dram_tensor(f"in_{name}_dram", a.shape, _mybir.dt.from_np(a.dtype), kind="ExternalInput").ap())
    shape, dtype = _OUT
    args.append(nc.dram_tensor("out_0_dram", shape, _mybir.dt.from_np(_np.dtype(dtype)), kind="ExternalOutput").ap())
    flamingo_kernel(nc, *args)
    r = _run(nc, [arrays], core_ids=[0])
    return r.results[0]["out_0_dram"]
```
